# Optimizing a Trainium2 kernel written in Bass

```python
import numpy as np
import jax
import jax.numpy as jnp

def _softmax(x, axis=-1):
    return jax.nn.softmax(x, axis=axis)

def _gelu(x):
    return jax.nn.gelu(x, approximate=True)

def _silu(x):
    return jax.nn.silu(x)

def _sigmoid(x):
    return jax.nn.sigmoid(x)

def _layernorm(x, axis=-1, eps=1e-05):
    m = jnp.mean(x, axis=axis, keepdims=True)
    v = jnp.var(x, axis=axis, keepdims=True)
    return (x - m) / jnp.sqrt(v + eps)

def _scatter_add(tgt, idx, src, axis=0):
    return tgt.at[idx].add(src)

def _segment_sum(src, seg, n):
    return jax.ops.segment_sum(src, seg, n)
kernel_name = 'mk_early_fusion_d2_tok_img1024_r4_4190af'

def setup_inputs(seed: int=0):
    np.random.seed(seed)
    _w = jnp.asarray

    def _rec_inputs():
        import jax
        import jax.numpy as jnp
        _rk = jax.random.key(seed)
        x = -0.00016672 + 0.999947 * jax.random.normal(jax.random.fold_in(_rk, 1), (16, 3, 96, 96), jnp.float32)
        txt = -0.000497171 + 0.57724 * jax.random.normal(jax.random.fold_in(_rk, 2), (16, 77, 256), jnp.float32)
        return (x, txt)
    x, txt = _rec_inputs()

    def _L0_tok_setup():
        import jax, jax.numpy as jnp
        import numpy as np
        IMG = 96
        PATCH = 16
        CH = 3
        EMBED = 256
        PATCH_DIM = CH * PATCH * PATCH

        def _patchify(x):
            B, C, H, Wd = x.shape
            hp, wp = (H // PATCH, Wd // PATCH)
            p = x.reshape(B, C, hp, PATCH, wp, PATCH)
            p = p.transpose(0, 2, 4, 1, 3, 5)
            return p.reshape(B, hp * wp, C * PATCH * PATCH)
        key = jax.random.key(seed)
        kx, kw, kb, kc = jax.random.split(key, 4)
        x = jax.random.normal(kx, (64, CH, IMG, IMG), dtype=jnp.float32)
        bound = 1.0 / np.sqrt(PATCH_DIM)
        W = jax.random.uniform(kw, (PATCH_DIM, EMBED), minval=-bound, maxval=bound, dtype=jnp.float32)
        b = jax.random.uniform(kb, (EMBED,), minval=-bound, maxval=bound, dtype=jnp.float32)
        cls_token = jnp.zeros((1, 1, EMBED), dtype=jnp.float32)
        return {'x': x, 'W': W, 'b': b, 'cls_token': cls_token}
    _L0_tok_all = _L0_tok_setup()
    _L0_tok_in = {k: v for k, v in _L0_tok_all.items() if k in ('W', 'b', 'cls_token')}
    del _L0_tok_all

    def _L0_attn_setup():
        import jax, jax.numpy as jnp
        import numpy as np
        key = jax.random.key(seed)
        ks = jax.random.split(key, 5)
        B, T, C = (2, 512, 256)
        x = jax.random.normal(ks[0], (B, T, C), dtype=jnp.float32)
        Wqkv = jax.random.normal(ks[1], (C, 3 * C), dtype=jnp.float32) * C ** (-0.5)
        bqkv = jax.random.normal(ks[2], (3 * C,), dtype=jnp.float32) * 0.02
        Wproj = jax.random.normal(ks[3], (C, C), dtype=jnp.float32) * C ** (-0.5)
        bproj = jax.random.normal(ks[4], (C,), dtype=jnp.float32) * 0.02
        return {'x': x, 'Wqkv': Wqkv, 'bqkv': bqkv, 'Wproj': Wproj, 'bproj': bproj}
    _L0_attn_all = _L0_attn_setup()
    _L0_attn_in = {k: v for k, v in _L0_attn_all.items() if k in ('Wqkv', 'bqkv', 'Wproj', 'bproj')}
    del _L0_attn_all

    def _L0_ffn_setup():
        import jax, jax.numpy as jnp
        import numpy as np
        from jax import lax
        D = 256
        H = 1024
        E = 8
        TOPK = 2
        key = jax.random.key(seed)
        ks = jax.random.split(key, 7)
        s = 0.02
        return {'x': jax.random.normal(ks[0], (2, 512, D), dtype=jnp.float32), 'W1': jax.random.normal(ks[1], (E, D, H), dtype=jnp.float32) * s, 'b1': jnp.zeros((E, H), dtype=jnp.float32), 'W2': jax.random.normal(ks[2], (E, H, D), dtype=jnp.float32) * s, 'b2': jnp.zeros((E, D), dtype=jnp.float32), 'Wr': jax.random.normal(ks[3], (D, E), dtype=jnp.float32) * s, 'br': jnp.zeros((E,), dtype=jnp.float32)}
    _L0_ffn_all = _L0_ffn_setup()
    _L0_ffn_in = {k: v for k, v in _L0_ffn_all.items() if k in ('W1', 'b1', 'W2', 'b2', 'Wr', 'br')}
    del _L0_ffn_all

    def _L1_attn_setup():
        import jax, jax.numpy as jnp
        import numpy as np
        HEADS = 16
        key = jax.random.key(seed)
        k1, k2, k3 = jax.random.split(key, 3)
        b, n, c = (4, 1024, 256)
        x = jax.random.normal(k1, (b, n, c), dtype=jnp.float32)
        qkv_w = jax.random.normal(k2, (c, c), dtype=jnp.float32) * c ** (-0.5)
        temp = jnp.ones((HEADS, 1), dtype=jnp.float32)
        out_w = jax.random.normal(k3, (c, c), dtype=jnp.float32) * c ** (-0.5)
        out_b = jnp.zeros((c,), dtype=jnp.float32)
        return {'x': x, 'qkv_w': qkv_w, 'temp': temp, 'out_w': out_w, 'out_b': out_b}
    _L1_attn_all = _L1_attn_setup()
    _L1_attn_in = {k: v for k, v in _L1_attn_all.items() if k in ('qkv_w', 'temp', 'out_w', 'out_b')}
    del _L1_attn_all

    def _L1_ffn_setup():
        import jax, jax.numpy as jnp
        import numpy as np
        B, L, C1, C2, K, K_IN = (4, 256, 256, 256, 32, 32)
        BN_EPS = 1e-05

        def _gated_bottleneck(x2d, conv_w, conv_b, gamma, beta, lin_w, lin_b):
            n = x2d.shape[0]
            g = conv_w.shape[0]
            xc = jnp.einsum('ngf,gf->ng', x2d.reshape(n, g, 4), conv_w) + conv_b
            mean = jnp.mean(xc, axis=0)
            var = jnp.mean((xc - mean) ** 2, axis=0)
            xn = (xc - mean) * jax.lax.rsqrt(var + BN_EPS) * gamma + beta
            xa = jax.nn.gelu(xn, approximate=False)
            return xa @ lin_w.T + lin_b
        key = jax.random.key(seed)
        ks = jax.random.split(key, 8)
        g = C1 // 4
        w_std = (2.0 / C2) ** 0.5
        lin_std = (1.0 / g) ** 0.5
        return {'x': jax.random.normal(ks[0], (B, L, C1), jnp.float32), 'weight': jax.random.normal(ks[1], (C1, C2), jnp.float32) * w_std, 'bias': jnp.zeros((C2,), jnp.float32), 'so_conv_w': jax.random.normal(ks[2], (g, 4), jnp.float32) * 0.5, 'so_conv_b': jnp.zeros((g,), jnp.float32), 'so_gamma': jnp.ones((g,), jnp.float32), 'so_beta': jnp.zeros((g,), jnp.float32), 'so_lin_w': jax.random.normal(ks[3], (C2, g), jnp.float32) * lin_std, 'so_lin_b': jnp.zeros((C2,), jnp.float32), 'si_conv_w': jax.random.normal(ks[4], (g, 4), jnp.float32) * 0.5, 'si_conv_b': jnp.zeros((g,), jnp.float32), 'si_gamma': jnp.ones((g,), jnp.float32), 'si_beta': jnp.zeros((g,), jnp.float32), 'si_lin_w': jax.random.normal(ks[5], (C1, g), jnp.float32) * lin_std, 'si_lin_b': jnp.zeros((C1,), jnp.float32)}
    _L1_ffn_all = _L1_ffn_setup()
    _L1_ffn_in = {k: v for k, v in _L1_ffn_all.items() if k in ('weight', 'bias', 'so_conv_w', 'so_conv_b', 'so_gamma', 'so_beta', 'so_lin_w', 'so_lin_b', 'si_conv_w', 'si_conv_b', 'si_gamma', 'si_beta', 'si_lin_w', 'si_lin_b')}
    del _L1_ffn_all
    return {'x': x, 'txt': txt, 'L0_tok_W': _L0_tok_in['W'], 'L0_tok_b': _L0_tok_in['b'], 'L0_tok_cls_token': _L0_tok_in['cls_token'], 'L0_attn_Wqkv': _L0_attn_in['Wqkv'], 'L0_attn_bqkv': _L0_attn_in['bqkv'], 'L0_attn_Wproj': _L0_attn_in['Wproj'], 'L0_attn_bproj': _L0_attn_in['bproj'], 'L0_ffn_W1': _L0_ffn_in['W1'], 'L0_ffn_b1': _L0_ffn_in['b1'], 'L0_ffn_W2': _L0_ffn_in['W2'], 'L0_ffn_b2': _L0_ffn_in['b2'], 'L0_ffn_Wr': _L0_ffn_in['Wr'], 'L0_ffn_br': _L0_ffn_in['br'], 'L1_attn_qkv_w': _L1_attn_in['qkv_w'], 'L1_attn_temp': _L1_attn_in['temp'], 'L1_attn_out_w': _L1_attn_in['out_w'], 'L1_attn_out_b': _L1_attn_in['out_b'], 'L1_ffn_weight': _L1_ffn_in['weight'], 'L1_ffn_bias': _L1_ffn_in['bias'], 'L1_ffn_so_conv_w': _L1_ffn_in['so_conv_w'], 'L1_ffn_so_conv_b': _L1_ffn_in['so_conv_b'], 'L1_ffn_so_gamma': _L1_ffn_in['so_gamma'], 'L1_ffn_so_beta': _L1_ffn_in['so_beta'], 'L1_ffn_so_lin_w': _L1_ffn_in['so_lin_w'], 'L1_ffn_so_lin_b': _L1_ffn_in['so_lin_b'], 'L1_ffn_si_conv_w': _L1_ffn_in['si_conv_w'], 'L1_ffn_si_conv_b': _L1_ffn_in['si_conv_b'], 'L1_ffn_si_gamma': _L1_ffn_in['si_gamma'], 'L1_ffn_si_beta': _L1_ffn_in['si_beta'], 'L1_ffn_si_lin_w': _L1_ffn_in['si_lin_w'], 'L1_ffn_si_lin_b': _L1_ffn_in['si_lin_b']}

def reference(x, txt, L0_tok_W, L0_tok_b, L0_tok_cls_token, L0_attn_Wqkv, L0_attn_bqkv, L0_attn_Wproj, L0_attn_bproj, L0_ffn_W1, L0_ffn_b1, L0_ffn_W2, L0_ffn_b2, L0_ffn_Wr, L0_ffn_br, L1_attn_qkv_w, L1_attn_temp, L1_attn_out_w, L1_attn_out_b, L1_ffn_weight, L1_ffn_bias, L1_ffn_so_conv_w, L1_ffn_so_conv_b, L1_ffn_so_gamma, L1_ffn_so_beta, L1_ffn_so_lin_w, L1_ffn_so_lin_b, L1_ffn_si_conv_w, L1_ffn_si_conv_b, L1_ffn_si_gamma, L1_ffn_si_beta, L1_ffn_si_lin_w, L1_ffn_si_lin_b):
    import jax
    import jax.numpy as jnp

    def _L0_tok_ref(x, W, b, cls_token):
        import jax, jax.numpy as jnp
        import numpy as np
        IMG = 96
        PATCH = 16
        CH = 3
        EMBED = 256
        PATCH_DIM = CH * PATCH * PATCH

        def _patchify(x):
            B, C, H, Wd = x.shape
            hp, wp = (H // PATCH, Wd // PATCH)
            p = x.reshape(B, C, hp, PATCH, wp, PATCH)
            p = p.transpose(0, 2, 4, 1, 3, 5)
            return p.reshape(B, hp * wp, C * PATCH * PATCH)
        B = x.shape[0]
        patches = _patchify(x)
        proj = jnp.einsum('bnd,de->bne', patches, W) + b
        cls = jnp.broadcast_to(cls_token, (B, 1, cls_token.shape[-1]))
        return jnp.concatenate((cls, proj), axis=1)

    def _L0_attn_ref(x, Wqkv, bqkv, Wproj, bproj):
        import jax, jax.numpy as jnp
        import numpy as np
        B, T, C = x.shape
        n_head = 16
        hd = C // n_head
        x_proj = x @ Wqkv + bqkv
        q = x_proj[:, :, :C].reshape(B, n_head, T, hd)
        k = x_proj[:, :, C:2 * C].reshape(B, n_head, T, hd)
        v = x_proj[:, :, 2 * C:].reshape(B, n_head, T, hd)
        att = jnp.einsum('bhtd,bhsd->bhts', q, k) * (1.0 / jnp.sqrt(jnp.float32(hd)))
        causal = jnp.tril(jnp.ones((T, T), dtype=bool))
        att = jnp.where(causal, att, jnp.float32(-jnp.inf))
        att = jax.nn.softmax(att, axis=-1)
        y = att @ v
        y = jnp.transpose(y, (0, 2, 1, 3)).reshape(B, T, C)
        return y @ Wproj + bproj

    def _L0_ffn_ref(x, W1, b1, W2, b2, Wr, br):
        import jax, jax.numpy as jnp
        import numpy as np
        from jax import lax
        D = 256
        H = 1024
        E = 8
        TOPK = 2
        B, S, _ = x.shape
        xf = x.reshape(-1, D)
        logits = xf @ Wr + br
        topv, _ = lax.top_k(logits, TOPK)
        thresh = topv[:, TOPK - 1:TOPK]
        masked = jnp.where(logits >= thresh, logits, -jnp.inf)
        weights = jax.nn.softmax(masked, axis=-1)
        h = jax.nn.gelu(jnp.einsum('td,edh->eth', xf, W1) + b1[:, None, :], approximate=False)
        expert_out = jnp.einsum('eth,ehd->etd', h, W2) + b2[:, None, :]
        out = jnp.einsum('etd,te->td', expert_out, weights)
        return out.reshape(B, S, D)

    def _L1_attn_ref(x, qkv_w, temp, out_w, out_b):
        import jax, jax.numpy as jnp
        import numpy as np
        HEADS = 16
        b, n, c = x.shape
        h = HEADS
        d = c // h
        w = jnp.einsum('bnc,oc->bno', x, qkv_w).reshape(b, n, h, d).transpose(0, 2, 1, 3)
        norm = jnp.sqrt(jnp.sum(w * w, axis=-2, keepdims=True))
        w_normed = w / jnp.maximum(norm, 1e-12)
        s = jnp.sum(w_normed * w_normed, axis=-1) * temp[None, :, :]
        pi = jax.nn.softmax(s, axis=1)
        pi_norm = pi / (jnp.sum(pi, axis=-1, keepdims=True) + 1e-08)
        dots = jnp.einsum('bhn,bhnd->bhd', pi_norm, w * w)
        attn = 1.0 / (1.0 + dots)
        out = -w * pi[..., None] * attn[:, :, None, :]
        out = out.transpose(0, 2, 1, 3).reshape(b, n, c)
        return jnp.einsum('bnc,oc->bno', out, out_w) + out_b

    def _L1_ffn_ref(x, weight, bias, so_conv_w, so_conv_b, so_gamma, so_beta, so_lin_w, so_lin_b, si_conv_w, si_conv_b, si_gamma, si_beta, si_lin_w, si_lin_b):
        import jax, jax.numpy as jnp
        import numpy as np
        B, L, C1, C2, K, K_IN = (4, 256, 256, 256, 32, 32)
        BN_EPS = 1e-05

        def _gated_bottleneck(x2d, conv_w, conv_b, gamma, beta, lin_w, lin_b):
            n = x2d.shape[0]
            g = conv_w.shape[0]
            xc = jnp.einsum('ngf,gf->ng', x2d.reshape(n, g, 4), conv_w) + conv_b
            mean = jnp.mean(xc, axis=0)
            var = jnp.mean((xc - mean) ** 2, axis=0)
            xn = (xc - mean) * jax.lax.rsqrt(var + BN_EPS) * gamma + beta
            xa = jax.nn.gelu(xn, approximate=False)
            return xa @ lin_w.T + lin_b
        b, l, c1 = x.shape
        c2 = weight.shape[1]
        x2d = x.reshape(b * l, c1)
        bi = jnp.arange(b)[:, None, None]
        li = jnp.arange(l)[None, :, None]
        score_out = jax.nn.softmax(_gated_bottleneck(x2d, so_conv_w, so_conv_b, so_gamma, so_beta, so_lin_w, so_lin_b).reshape(b, l, c2), axis=-1)
        s_v_out, s_i_out = jax.lax.top_k(score_out, K)
        full = jnp.einsum('blc,co->blo', x, weight)
        out_k = jnp.take_along_axis(full, s_i_out, axis=-1) * s_v_out
        out_branch = jnp.zeros((b, l, c2), x.dtype).at[bi, li, s_i_out].add(out_k)
        score_in = jax.nn.softmax(_gated_bottleneck(x2d, si_conv_w, si_conv_b, si_gamma, si_beta, si_lin_w, si_lin_b).reshape(b, l, c1), axis=-1)
        s_v_in, s_i_in = jax.lax.top_k(score_in, K_IN)
        x_gated = jnp.take_along_axis(x, s_i_in, axis=-1) * s_v_in
        x_sparse = jnp.zeros((b, l, c1), x.dtype).at[bi, li, s_i_in].add(x_gated)
        in_branch = jnp.einsum('blc,co->blo', x_sparse, weight)
        return out_branch + in_branch + bias
    h = _L0_tok_ref(x, L0_tok_W, L0_tok_b, L0_tok_cls_token)
    h = jnp.concatenate([h, txt], axis=1)
    h = h + _L0_attn_ref(_layernorm(h, axis=-1), L0_attn_Wqkv, L0_attn_bqkv, L0_attn_Wproj, L0_attn_bproj)
    h = h + _L0_ffn_ref(_layernorm(h, axis=-1), L0_ffn_W1, L0_ffn_b1, L0_ffn_W2, L0_ffn_b2, L0_ffn_Wr, L0_ffn_br)
    h = h + _L1_attn_ref(_layernorm(h, axis=-1), L1_attn_qkv_w, L1_attn_temp, L1_attn_out_w, L1_attn_out_b)
    h = h + _L1_ffn_ref(_layernorm(h, axis=-1), L1_ffn_weight, L1_ffn_bias, L1_ffn_so_conv_w, L1_ffn_so_conv_b, L1_ffn_so_gamma, L1_ffn_so_beta, L1_ffn_so_lin_w, L1_ffn_so_lin_b, L1_ffn_si_conv_w, L1_ffn_si_conv_b, L1_ffn_si_gamma, L1_ffn_si_beta, L1_ffn_si_lin_w, L1_ffn_si_lin_b)
    return h

_drawn_inputs = setup_inputs


def setup_inputs(seed=0):
    import zlib

    import numpy as np

    out = dict(_drawn_inputs(seed))
    spreads = {'L0_tok_cls_token': (0.0, 0.1),
     'L0_ffn_b1': (0.0, 0.1),
     'L0_ffn_b2': (0.0, 0.1),
     'L0_ffn_br': (0.0, 0.1),
     'L1_attn_temp': (1.0, 0.6),
     'L1_attn_out_b': (0.0, 0.1),
     'L1_ffn_bias': (0.0, 0.1),
     'L1_ffn_so_conv_b': (0.0, 0.8),
     'L1_ffn_so_gamma': (1.0, 0.6),
     'L1_ffn_so_beta': (0.0, 0.8),
     'L1_ffn_so_lin_b': (0.0, 0.8),
     'L1_ffn_si_conv_b': (0.0, 0.8),
     'L1_ffn_si_gamma': (1.0, 0.6),
     'L1_ffn_si_beta': (0.0, 0.8),
     'L1_ffn_si_lin_b': (0.0, 0.8)}
    factors = {'L0_attn_bqkv': 2.79,
     'L1_ffn_weight': 4.693,
     'L1_ffn_so_conv_w': 7.954,
     'L1_ffn_so_lin_w': 7.423,
     'L1_ffn_si_conv_w': 7.872,
     'L1_ffn_si_lin_w': 7.489}
    for name, (base, spread) in spreads.items():
        noise = np.random.default_rng([zlib.crc32(name.encode()), seed]).standard_normal(out[name].shape)
        drawn = base * np.exp(spread * noise) if base else spread * noise
        out[name] = jnp.asarray(drawn.astype(out[name].dtype))
    for name, factor in factors.items():
        out[name] = (out[name] * factor).astype(out[name].dtype)
    return out
```

```python
from contextlib import ExitStack

import concourse.bass as bass
from concourse import mybir

F32 = mybir.dt.float32
BF16 = mybir.dt.bfloat16
ALU = mybir.AluOpType
ACT = mybir.ActivationFunctionType
AX = mybir.AxisListType

B = 16
T = 114
NP = 36
C = 256
KT = C // 128
PK = 768 // 128
GB = 4
G = B // GB
GT = GB * T
NH, HD = 16, 16
HQ = 4
NQ = NH // HQ
E = 8
HID = 1024
HT = HID // 128
EPS = 1e-5
TOPK = 32
NEG = -1.0e30


def early_fusion(nc: bass.Bass, patches, h_base, tok_w, wkv, wq, bkv, bq, wproj, bproj, mask4, ident,
                 w1, b1, w2, b2, wr, br, tssa_w, temp, head_of, head_to, out_w, out_b,
                 conv_col, conv_mask, conv_b, gamma, beta, lin_w, lin_b, ffn_w, ffn_bias, out):
    with ExitStack() as ctx:
        def sb(name, shape, dt=F32):
            return ctx.enter_context(nc.sbuf_tensor(name, shape, dt))

        def sem(name):
            return ctx.enter_context(nc.semaphore(name))

        bank = [ctx.enter_context(nc.psum_tensor(f"bank{i}", [128, 512], F32)) for i in range(8)]

        H = sb("h", [T, B, C])
        ID = sb("identity", [128, 128])
        EP = sb("eps", [128, 1])
        ONE = sb("ones_row", [1, 128])
        XN = sb("x_normed", [T, GB, C])
        XT = sb("x_normed_T", [128, KT, GT])
        ST = sb("ln_stats", [T, B, 6])
        MV = sb("ln_mean_var", [T, B, 2])
        SD = sb("ln_std", [T, B])
        RS = sb("ln_rstd", [T, B])

        h_loaded = sem("h_loaded")
        consts_loaded = sem("consts_loaded")
        const_set = sem("const_set")
        waited = sem("waited")

        def finish_norm(stage):
            stats_made, std_made, aggregated = (sem(f"{stage}_{n}") for n in ("stats", "std", "aggr"))

            def on_vector(dve):
                for b in range(B):
                    ins = dve.bn_aggr(MV[:, b, :], ST[:, b, :])
                ins.then_inc(aggregated, 1)
                dve.wait_ge(std_made, 1)
                dve.reciprocal(RS[:, :], SD[:, :]).then_inc(stats_made, 1)
                dve.wait_ge(stats_made, 1)

            def on_scalar(act):
                act.wait_ge(aggregated, 1)
                act.activation(SD[:, :], MV[:, :, 1], ACT.Sqrt, bias=EP[0:T, :]).then_inc(std_made, 1)
            return on_vector, on_scalar

        with ExitStack() as p1:
            PT = p1.enter_context(nc.sbuf_tensor("patches_T", [128, GB // 2, PK, 128], F32))
            TW = p1.enter_context(nc.sbuf_tensor("tok_w", [128, PK, C], F32))
            patches_loaded, tok_w_loaded = sem("patches_loaded"), sem("tok_w_loaded")
            tok_in_psum, tok_added = sem("tok_in_psum"), sem("tok_added")
            with nc.Block() as block:
                @block.sync
                def _(sp):
                    sp.dma_start(TW[:], tok_w).then_inc(tok_w_loaded, 16)
                    sp.dma_start(H[:], h_base).then_inc(h_loaded, 16)
                    sp.dma_start(ID[:], ident).then_inc(consts_loaded, 16)
                    sp.dma_start(PT[:], patches[0]).then_inc(patches_loaded, 16)
                    with sp.Fori(1, G) as g:
                        sp.wait_ge(tok_in_psum, g * 2)
                        sp.dma_start(PT[:], patches[bass.ds(g, 1)].rearrange("a p q k m -> (a p) q k m")).then_inc(patches_loaded, 16)

                @block.tensor
                def _(pe):
                    pe.wait_ge(tok_w_loaded, 16)
                    with pe.Fori(0, G) as g:
                        pe.wait_ge(patches_loaded, g * 16 + 16)
                        for q in range(2):
                            pe.wait_ge(tok_added, g * GB + 2 * q + 1)
                            for k in range(PK):
                                mm = pe.matmul(bank[q][:, 0:C], PT[:, q, k, :], TW[:, k, :], start=k == 0, stop=k == PK - 1)
                            mm.then_inc(tok_in_psum, 1)

                @block.vector
                def _(dve):
                    dve.memset(EP[:], EPS)
                    dve.memset(ONE[:], 1.0).then_inc(tok_added, 3)
                    dve.wait_ge(h_loaded, 16)
                    with dve.Fori(0, G) as g:
                        for q in range(2):
                            dve.wait_ge(tok_in_psum, g * 2 + q + 1)
                            for j in range(2):
                                b = g * GB + 2 * q + j
                                rows = H[0:NP + 1, bass.ds(b, 1), :].rearrange("p a c -> p (a c)")
                                dve.tensor_tensor(rows, bank[q][64 * j:64 * j + NP + 1, 0:C], rows, ALU.add).then_inc(tok_added, 1)
                        dve.wait_ge(tok_added, g * GB + GB + 3)
                        for j in range(GB):
                            b = g * GB + j
                            dve.bn_stats(ST[:, bass.ds(b, 1), :].rearrange("p a c -> p (a c)"),
                                         H[:, bass.ds(b, 1), :].rearrange("p a c -> p (a c)")).then_inc(const_set, 1)
                    dve.wait_ge(const_set, B)

        def after(eng, signal, value):
            eng.wait_ge(signal, value)
            eng.sem_inc(waited, 1)

        def normalise(dve, g, xn_ready):
            for j in range(GB):
                b = g * GB + j
                dve.tensor_scalar(XN[:, j, :], H[:, bass.ds(b, 1), :].rearrange("p a c -> p (a c)"),
                                  MV[:, bass.ds(b, 1), 0], RS[:, bass.ds(b, 1)],
                                  ALU.subtract, ALU.mult).then_inc(xn_ready, 1)

        def row(t, b):
            return t[:, bass.ds(b, 1), :].rearrange("p a c -> p (a c)")

        with ExitStack() as p2:
            def psb(name, shape, dt=F32):
                return p2.enter_context(nc.sbuf_tensor(name, shape, dt))
            WKV = psb("wkv", [128, KT, NH * 32])
            WQ = psb("wq", [128, KT, NH * 32])
            BKV = psb("bkv", [128, NH])
            BQ = psb("bq", [128, NH])
            WP = psb("wproj", [128, KT, C])
            BP = psb("bproj", [T, C])
            MF = psb("mask4_f", [T, GT])
            MK = psb("mask4", [T, GT], BF16)
            IB = psb("identity_bf", [128, 128], BF16)
            KV = psb("kv_T", [128, T * NH])
            Q = psb("q_T", [128, T * NH])
            VS = psb("v_rows", [T, NH, GB, 32])
            PR = psb("probs", [T, 2, GB, GT])
            PTR = psb("probs_T", [T, 2, GB, GT])
            MX = psb("row_max", [T, GB, HQ])
            YT = psb("y_T", [128, 2, GT])
            RD = psb("row_sum_recip", [T, HQ, GB])
            YN = psb("y_normed", [T, GB, C])
            YNT = psb("y_normed_T", [128, KT, GT])
            attn_w_loaded = sem("attn_w_loaded")
            v_frame_set, mask_made = sem("v_frame_set"), sem("mask_made")
            xn_ready, xnT_in_psum, xnT_ready = sem("a_xn"), sem("a_xnT_psum"), sem("a_xnT")
            qkv_in_psum, qkv_ready = sem("qkv_psum"), sem("qkv")
            vT_in_psum, v_ready = sem("vT_psum"), sem("v_ready")
            s_in_psum, s_shifted, max_made, p_ready = sem("s_psum"), sem("s_shifted"), sem("max_made"), sem("p_ready")
            pT_in_psum, pT_ready = sem("pT_psum"), sem("pT")
            y_in_psum, yT_ready, yrow_in_psum, y_normed, rd_made = (sem(n) for n in ("y_psum", "yT", "yrow_psum", "y_normed", "rd_made"))
            ynT_in_psum, ynT_ready, proj_in_psum, h_added, bias_added = (sem(n) for n in ("ynT_psum", "ynT", "proj_psum", "h_added", "bproj_added"))
            st_made = sem("a_stats_made")
            on_vector, on_scalar = finish_norm("ln1")
            n_loads = 7
            with nc.Block() as block:
                @block.sync
                def _(sp):
                    for dst, src in ((WKV, wkv), (WQ, wq), (BKV, bkv), (BQ, bq), (WP, wproj), (BP, bproj), (MF, mask4)):
                        sp.dma_start(dst[:], src).then_inc(attn_w_loaded, 16)

                @block.gpsimd
                def _(pool):
                    pool.wait_ge(attn_w_loaded, 16 * n_loads)
                    with pool.Fori(0, G) as g:
                        pool.wait_ge(xn_ready, g * GB + GB)
                        hs = H[:, bass.ds(g * GB, GB), :]
                        pool.tensor_tensor(hs, hs, BP[:].rearrange("p (a c) -> p a c", a=1).to_broadcast([T, GB, C]), ALU.add).then_inc(bias_added, 1)

                @block.scalar
                def _(act):
                    on_scalar(act)
                    act.wait_ge(v_frame_set, 1)

                    def exp_scores(g, q, b):
                        act.wait_ge(s_shifted, g * 16 + 4 * q + b + 1)
                        act.activation(PR[:, q % 2, b, :], PR[:, q % 2, b, :], ACT.Exp, scale=HD ** -0.5).then_inc(p_ready, 1)

                    def move_probs(g, q, b):
                        n = 4 * q + b
                        act.wait_ge(pT_in_psum, g * 16 + n + 1)
                        act.activation(PTR[:, q % 2, b, :], bank[4 + n % 2][0:T, 0:GT], ACT.Copy).then_inc(pT_ready, 1)

                    def move_y(g, q):
                        act.wait_ge(y_in_psum, g * 4 + q + 1)
                        act.activation(YT[:, q % 2, :], bank[6][:, 0:GT], ACT.Copy).then_inc(yT_ready, 1)

                    with act.Fori(0, G) as g:
                        for k in range(KT):
                            act.wait_ge(xnT_in_psum, g * KT + k + 1)
                            act.activation(XT[:, k, :], bank[4 + k][:, 0:GT], ACT.Copy).then_inc(xnT_ready, 1)
                        for q in range(NQ):
                            act.wait_ge(vT_in_psum, g * NQ + q + 1)
                            act.activation(VS[:, HQ * q:HQ * q + HQ, :, 0:HD],
                                           bank[4 + q % 2][0:T, :].rearrange("p (h b d) -> p h b d", h=HQ, b=GB)[:, :, :, HD:2 * HD],
                                           ACT.Copy).then_inc(v_ready, 1)
                        for b in range(GB):
                            exp_scores(g, 0, b)
                        for q in range(NQ):
                            for b in range(GB):
                                move_probs(g, q, b)
                                if q + 1 < NQ:
                                    exp_scores(g, q + 1, b)
                            move_y(g, q)
                        for k in range(KT):
                            act.wait_ge(ynT_in_psum, g * KT + k + 1)
                            act.activation(YNT[:, k, :], bank[4 + k][:, 0:GT], ACT.Copy).then_inc(ynT_ready, 1)

                @block.vector
                def _(dve):
                    on_vector(dve)
                    dve.memset(VS[:, :, :, HD:32], 0.0).then_inc(rd_made, 1)
                    dve.wait_ge(rd_made, 1)
                    dve.memset(VS[:, :, :, HD:HD + 1], 1.0).then_inc(v_frame_set, 1)
                    dve.sem_inc(yT_ready, 1)
                    dve.sem_inc(y_normed, 1)
                    dve.sem_inc(h_added, GB)
                    dve.wait_ge(attn_w_loaded, 16 * n_loads)
                    dve.wait_ge(consts_loaded, 16)
                    dve.tensor_copy(IB[:], ID[:])
                    dve.tensor_copy(MK[:], MF[:]).then_inc(mask_made, 1)

                    def shift_scores(g, q, b):
                        n = g * 16 + 4 * q + b + 1
                        dve.wait_ge(s_in_psum, n)
                        s = bank[b][0:T, 0:GT].rearrange("p (h s) -> p h s", h=HQ)
                        dve.tensor_reduce(MX[:, b, :], s, AX.X, ALU.max).then_inc(max_made, 1)
                        if q >= 2:
                            dve.wait_ge(pT_in_psum, g * 16 + 4 * (q - 2) + b + 1)
                        dve.wait_ge(max_made, n)
                        dve.tensor_tensor(PR[:, q % 2, b, :].rearrange("p (h s) -> p h s", h=HQ), s,
                                          MX[:, b, :].rearrange("p (h a) -> p h a", a=1).to_broadcast([T, HQ, T]),
                                          ALU.subtract).then_inc(s_shifted, 1)

                    def norm_y(g, q):
                        dve.wait_ge(yrow_in_psum, g * NQ + q + 1)
                        y = bank[7][0:T, :].rearrange("p (h b d) -> p h b d", h=HQ, b=GB)
                        dve.reciprocal(RD[:], y[:, :, :, HD]).then_inc(rd_made, 1)
                        dve.wait_ge(rd_made, g * NQ + q + 2)
                        dve.tensor_tensor(YN[:].rearrange("p b (h d) -> p h b d", d=HD)[:, HQ * q:HQ * q + HQ],
                                          y[:, :, :, 0:HD],
                                          RD[:].rearrange("p h (b a) -> p h b a", a=1).to_broadcast([T, HQ, GB, HD]),
                                          ALU.mult).then_inc(y_normed, 1)

                    with dve.Fori(0, G) as g:
                        normalise(dve, g, xn_ready)
                        for n in range(8):
                            dve.wait_ge(qkv_in_psum, g * 8 + n + 1)
                            dst, bias = (KV, BKV) if n < 4 else (Q, BQ)
                            c0 = 4 * (n % 4)
                            dve.tensor_tensor(dst[:].rearrange("p (t c) -> p c t", c=NH)[:, c0:c0 + 4, :],
                                              bank[n % 4][:, 0:GT].rearrange("p (c t) -> p c t", c=4),
                                              bias[:, c0:c0 + 4].rearrange("p (c a) -> p c a", a=1).to_broadcast([128, 4, T]),
                                              ALU.add).then_inc(qkv_ready, 1)
                        for q in range(NQ):
                            if q == NQ - 1:
                                norm_y(g, 0)
                            for b in range(GB):
                                shift_scores(g, q, b)
                        for q in range(1, NQ):
                            norm_y(g, q)
                        dve.wait_ge(bias_added, g + 1)
                        for j in range(GB):
                            b = g * GB + j
                            dve.wait_ge(proj_in_psum, g * GB + j + 1)
                            dve.tensor_tensor(row(H, b), bank[j][0:T, 0:C], row(H, b), ALU.add).then_inc(h_added, 1)
                            dve.wait_ge(h_added, g * GB + j + 1 + GB)
                            dve.bn_stats(row(ST, b), row(H, b)).then_inc(st_made, 1)
                    dve.wait_ge(st_made, B)

                @block.tensor
                def _(pe):
                    pe.wait_ge(consts_loaded, 16)
                    pe.wait_ge(attn_w_loaded, 16 * n_loads)
                    pe.wait_ge(mask_made, 1)

                    def scores(g, q):
                        for b in range(GB):
                            if q:
                                pe.wait_ge(s_shifted, g * 16 + 4 * (q - 1) + b + 1)
                            pe.matmul(bank[b][0:T, 0:GT], IB[0:T, 0:T], MK[:, :], start=True, stop=False, skip_group_check=True)
                        for h in range(HQ):
                            r = (HQ * q + h) * T
                            for b in range(GB):
                                mm = pe.matmul(bank[b][0:T, h * T:h * T + T], Q[32 * b:32 * b + HD, r:r + T],
                                               KV[32 * b:32 * b + HD, r:r + T], start=False, stop=True, skip_group_check=True)
                                if h == HQ - 1:
                                    mm.then_inc(s_in_psum, 1)

                    def transpose_probs(g, q):
                        for b in range(GB):
                            n = 4 * q + b
                            if n >= 2:
                                pe.wait_ge(pT_ready, g * 16 + n - 1)
                            pe.wait_ge(p_ready, g * 16 + n + 1)
                            for h in range(HQ):
                                mm = pe.transpose(bank[4 + n % 2][0:T, h * T:h * T + T], PR[:, q % 2, b, h * T:h * T + T], ID[0:T, 0:T])
                            mm.then_inc(pT_in_psum, 1)

                    def apply_probs(g, q):
                        pe.wait_ge(pT_ready, g * 16 + 4 * q + 4)
                        pe.wait_ge(yT_ready, g * NQ + q + 1)
                        for h in range(HQ):
                            for b in range(GB):
                                mm = pe.matmul(bank[6][32 * b:32 * b + 32, h * T:h * T + T], VS[:, HQ * q + h, b, :],
                                               PTR[:, q % 2, b, h * T:h * T + T], start=True, stop=True)
                        mm.then_inc(y_in_psum, 1)

                    def y_rows(g, q):
                        pe.wait_ge(yT_ready, g * NQ + q + 2)
                        pe.wait_ge(y_normed, g * NQ + q + 1)
                        for h in range(HQ):
                            mm = pe.transpose(bank[7][0:T, h * 128:h * 128 + 128], YT[:, q % 2, h * T:h * T + T], ID[:, :])
                        mm.then_inc(yrow_in_psum, 1)

                    with pe.Fori(0, G) as g:
                        pe.wait_ge(xn_ready, g * GB + GB)
                        for k in range(KT):
                            for b in range(GB):
                                mm = pe.transpose(bank[4 + k][:, b * T:b * T + T], XN[:, b, k * 128:k * 128 + 128], ID[0:T, 0:T])
                            mm.then_inc(xnT_in_psum, 1)
                        pe.wait_ge(xnT_ready, g * KT + KT)
                        pe.wait_ge(h_added, g * GB + GB)
                        for n in range(8):
                            if n >= 4:
                                pe.wait_ge(qkv_ready, g * 8 + n - 3)
                            w = WKV if n < 4 else WQ
                            for c in range(4):
                                col = (4 * (n % 4) + c) * 32
                                for k in range(KT):
                                    for b in range(GB):
                                        mm = pe.matmul(bank[n % 4][32 * b:32 * b + 32, c * T:c * T + T], w[:, k, col:col + 32],
                                                       XT[:, k, b * T:b * T + T], start=k == 0, stop=k == KT - 1)
                            mm.then_inc(qkv_in_psum, 1)
                        for q in range(NQ):
                            pe.wait_ge(qkv_ready, g * 8 + 4)
                            if q >= 2:
                                pe.wait_ge(v_ready, g * NQ + q - 1)
                            for h in range(HQ):
                                r = (HQ * q + h) * T
                                mm = pe.transpose(bank[4 + q % 2][0:T, h * 128:h * 128 + 128], KV[:, r:r + T], ID[:, :])
                            mm.then_inc(vT_in_psum, 1)
                        pe.wait_ge(qkv_ready, g * 8 + 8)
                        scores(g, 0)
                        pe.wait_ge(v_ready, g * NQ + NQ)
                        for q in range(NQ):
                            if q + 1 < NQ:
                                scores(g, q + 1)
                            transpose_probs(g, q)
                            if q:
                                y_rows(g, q - 1)
                            apply_probs(g, q)
                        y_rows(g, NQ - 1)
                        pe.wait_ge(y_normed, g * NQ + NQ + 1)
                        pe.wait_ge(pT_ready, g * 16 + 16)
                        for k in range(KT):
                            for b in range(GB):
                                mm = pe.transpose(bank[4 + k][:, b * T:b * T + T], YN[:, b, k * 128:k * 128 + 128], ID[0:T, 0:T])
                            mm.then_inc(ynT_in_psum, 1)
                        pe.wait_ge(ynT_ready, g * KT + KT)
                        pe.wait_ge(s_shifted, g * 16 + 16)
                        for b in range(GB):
                            for k in range(KT):
                                mm = pe.matmul(bank[b][0:T, 0:C], YNT[:, k, b * T:b * T + T], WP[:, k, :], start=k == 0, stop=k == KT - 1)
                            mm.then_inc(proj_in_psum, 1)

        with ExitStack() as p3:
            def psb(name, shape, dt=F32):
                return p3.enter_context(nc.sbuf_tensor(name, shape, dt))
            X2T = psb("moe_x_T", [128, KT, B * T])
            WG = psb("expert_weight", [T, E, B])
            W1 = psb("w1", [128, 2, KT, HID])
            W2 = psb("w2", [128, 2, HT, C])
            B1 = psb("b1", [128, 2, HT])
            WR = psb("wr", [128, KT, E])
            BR = psb("br", [E, 1])
            B2 = psb("b2", [E, C])
            LT = psb("logits_T", [E, GT])
            LG = psb("logits", [T, GB, E])
            M8 = psb("logits_sorted", [T, GB, E])
            KEEP = psb("kept", [T, GB, E])
            EX = psb("gate_exp", [T, GB, E])
            SM = psb("gate_sum", [T, GB])
            GT8 = psb("gates", [T, GB, E])
            GTT = psb("gates_T", [E, GT])
            HB = psb("hidden", [128, 4, GT])
            ld, wld = sem("router_loaded"), [sem(f"experts_loaded{i}") for i in range(2)]
            xn_ready, xnT_in_psum, xnT_ready = sem("m_xn"), sem("m_xnT_psum"), sem("m_xnT")
            lT_in_psum, lT_ready, l_in_psum = sem("lT_psum"), sem("lT"), sem("l_psum")
            gate, gate_exp, gT_in_psum, gT_ready = sem("gate"), sem("gate_exp_made"), sem("gT_psum"), sem("gT")
            bias_in_psum, bias_added = sem("b2_psum"), sem("b2_added")
            hid_in_psum, hid_ready, y_in_psum, y_added = (sem(n) for n in ("hid_psum", "hid", "moe_y_psum", "moe_added"))
            st_made = sem("m_stats_made")
            on_vector, on_scalar = finish_norm("ln2")

            def load_expert(sp, e, s):
                for dst, src in ((W1[:, s], w1), (W2[:, s], w2), (B1[:, s], b1)):
                    src = src[e] if isinstance(e, int) else src[bass.ds(e, 1)]
                    if not isinstance(e, int):
                        src = src.rearrange("a p k n -> (a p) k n") if len(src.shape) == 4 else src.rearrange("a p k -> (a p) k")
                    sp.dma_start(dst, src).then_inc(wld[s], 16)

            with nc.Block() as block:
                @block.sync
                def _(sp):
                    for dst, src in ((WR, wr), (BR, br), (B2, b2)):
                        sp.dma_start(dst[:], src).then_inc(ld, 16)
                    load_expert(sp, 0, 0)
                    load_expert(sp, 1, 1)

                @block.scalar
                def _(act):
                    on_scalar(act)
                    act.wait_ge(ld, 48)
                    with act.Fori(0, G) as g:
                        for k in range(KT):
                            act.wait_ge(xnT_in_psum, g * KT + k + 1)
                            act.activation(X2T[:, k, bass.ds(g * GT, GT)], bank[4 + k][:, 0:GT], ACT.Copy).then_inc(xnT_ready, 1)
                        act.wait_ge(lT_in_psum, g + 1)
                        act.activation(LT[:], bank[0][0:E, 0:GT], ACT.Identity, bias=BR[:]).then_inc(lT_ready, 1)
                        act.wait_ge(gate, g * 7 + 3)
                        act.activation(EX[:], EX[:], ACT.Exp).then_inc(gate_exp, 1)
                        act.wait_ge(gT_in_psum, g + 1)
                        act.activation(GTT[:], bank[2][0:E, 0:GT], ACT.Copy).then_inc(gT_ready, 1)

                @block.vector
                def _(dve):
                    on_vector(dve)
                    dve.sem_inc(bias_added, GB)
                    with dve.Fori(0, G) as g:
                        normalise(dve, g, xn_ready)
                        dve.wait_ge(l_in_psum, g + 1)
                        dve.tensor_copy(LG[:], bank[1][0:T, 0:GB * E].rearrange("p (b e) -> p b e", e=E)).then_inc(gate, 1)
                        after(dve, gate, g * 7 + 1)
                        for b in range(GB):
                            ins = dve.max(M8[:, b, :], LG[:, b, :])
                        ins.then_inc(gate, 1)
                        dve.wait_ge(gate, g * 7 + 2)
                        dve.tensor_tensor(KEEP[:], LG[:], M8[:, :, 1:2].to_broadcast([T, GB, E]), ALU.is_ge)
                        dve.tensor_tensor(EX[:], LG[:], M8[:, :, 0:1].to_broadcast([T, GB, E]), ALU.subtract).then_inc(gate, 1)
                        dve.wait_ge(gate_exp, g + 1)
                        dve.tensor_tensor(EX[:], EX[:], KEEP[:], ALU.mult).then_inc(gate, 1)
                        dve.wait_ge(gate, g * 7 + 4)
                        dve.tensor_reduce(SM[:], EX[:], AX.X, ALU.add).then_inc(gate, 1)
                        dve.wait_ge(gate, g * 7 + 5)
                        dve.reciprocal(SM[:], SM[:]).then_inc(gate, 1)
                        dve.wait_ge(gate, g * 7 + 6)
                        dve.tensor_tensor(WG[:, :, bass.ds(g * GB, GB)].rearrange("p e b -> p b e"), EX[:],
                                          SM[:].rearrange("p (b a) -> p b a", a=1).to_broadcast([T, GB, E]), ALU.mult)
                        dve.tensor_tensor(GT8[:], EX[:],
                                          SM[:].rearrange("p (b a) -> p b a", a=1).to_broadcast([T, GB, E]), ALU.mult).then_inc(gate, 1)
                        for j in range(GB):
                            b = g * GB + j
                            dve.wait_ge(bias_in_psum, g * GB + j + 1)
                            dve.tensor_tensor(row(H, b), bank[3 + 4 * (j % 2)][0:T, 0:C], row(H, b), ALU.add).then_inc(bias_added, 1)
                    dve.wait_ge(gate, 7 * G)
                    dve.wait_ge(bias_added, B + GB)

                @block.tensor
                def _(pe):
                    pe.wait_ge(ld, 48)
                    with pe.Fori(0, G) as g:
                        pe.wait_ge(xn_ready, g * GB + GB)
                        for k in range(KT):
                            for b in range(GB):
                                mm = pe.transpose(bank[4 + k][:, b * T:b * T + T], XN[:, b, k * 128:k * 128 + 128], ID[0:T, 0:T])
                            mm.then_inc(xnT_in_psum, 1)
                        pe.wait_ge(xnT_ready, g * KT + KT)
                        for k in range(KT):
                            mm = pe.matmul(bank[0][0:E, 0:GT], WR[:, k, :], X2T[:, k, bass.ds(g * GT, GT)], start=k == 0, stop=k == KT - 1)
                        mm.then_inc(lT_in_psum, 1)
                        after(pe, lT_ready, g + 1)
                        for b in range(GB):
                            mm = pe.transpose(bank[1][0:T, b * E:b * E + E], LT[:, b * T:b * T + T], ID[0:E, 0:E])
                        mm.then_inc(l_in_psum, 1)
                        pe.wait_ge(gate, g * 7 + 7)
                        for b in range(GB):
                            mm = pe.transpose(bank[2][0:E, b * T:b * T + T], GT8[:, b, :], ID[0:T, 0:T])
                        mm.then_inc(gT_in_psum, 1)
                        pe.wait_ge(gT_ready, g + 1)
                        for b in range(GB):
                            pe.wait_ge(bias_added, g * GB + b + GB - 1)
                            pe.matmul(bank[3 + 4 * (b % 2)][0:T, 0:C], GTT[:, b * T:b * T + T], B2[:, :], start=True, stop=True).then_inc(bias_in_psum, 1)

            with nc.Block() as block:
                @block.sync
                def _(sp):
                    with sp.Fori(1, E // 2) as p:
                        for s in range(2):
                            sp.wait_ge(y_in_psum, p * (2 * G * GB) + (s - 1) * G * GB)
                            load_expert(sp, p * 2 + s, s)

                @block.scalar
                def _(act):
                    act.sem_inc(hid_ready, 2)
                    with act.Fori(0, E // 2) as p:
                        for s in range(2):
                            with act.Fori(0, G) as g:
                                act.wait_ge(wld[s], p * 48 + 48)
                                u = p * (2 * G) + g + s * G
                                for i in range(HT):
                                    act.wait_ge(hid_in_psum, u * HT + i + 1)
                                    act.activation(HB[:, i % 4, :], bank[4 + i % 2][:, 0:GT], ACT.Gelu, bias=B1[:, s, i:i + 1]).then_inc(hid_ready, 1)

                @block.vector
                def _(dve):
                    dve.sem_inc(y_added, GB)
                    with dve.Fori(0, E // 2) as p:
                        for s in range(2):
                            with dve.Fori(0, G) as g:
                                u = p * (2 * G) + g + s * G
                                for j in range(GB):
                                    b = g * GB + j
                                    dve.wait_ge(y_in_psum, u * GB + j + 1)
                                    wge = WG[:, bass.ds(p * 2 + s, 1), bass.ds(b, 1)].rearrange("p a c -> p (a c)")
                                    dve.scalar_tensor_tensor(out=row(H, b), in0=bank[j][0:T, 0:C], scalar=wge,
                                                             in1=row(H, b), op0=ALU.mult, op1=ALU.add).then_inc(y_added, 1)
                    dve.wait_ge(y_added, E * B + GB)
                    for b in range(B):
                        dve.bn_stats(ST[:, b, :], H[:, b, :]).then_inc(st_made, 1)
                    dve.wait_ge(st_made, B)

                @block.tensor
                def _(pe):
                    with pe.Fori(0, E // 2) as p:
                        for s in range(2):
                            with pe.Fori(0, G) as g:
                                pe.wait_ge(wld[s], p * 48 + 48)
                                u = p * (2 * G) + g + s * G

                                def hidden(i):
                                    pe.wait_ge(hid_ready, u * HT + i + 1)
                                    for k in range(KT):
                                        mm = pe.matmul(bank[4 + i % 2][:, 0:GT], W1[:, s, k, i * 128:i * 128 + 128],
                                                       X2T[:, k, bass.ds(g * GT, GT)], start=k == 0, stop=k == KT - 1)
                                    mm.then_inc(hid_in_psum, 1)

                                hidden(0)
                                for i in range(HT):
                                    if i + 1 < HT:
                                        hidden(i + 1)
                                    pe.wait_ge(hid_ready, u * HT + i + 3)
                                    if i == 0:
                                        pe.wait_ge(y_added, u * GB + GB)
                                    for b in range(GB):
                                        mm = pe.matmul(bank[b][0:T, 0:C], HB[:, i % 4, b * T:b * T + T], W2[:, s, i, :],
                                                       start=i == 0, stop=i == HT - 1)
                                        if i == HT - 1:
                                            mm.then_inc(y_in_psum, 1)

        with ExitStack() as p4:
            def psb(name, shape, dt=F32):
                return p4.enter_context(nc.sbuf_tensor(name, shape, dt))
            AW = psb("tssa_w", [128, KT, C])
            OW = psb("out_w", [128, KT, C])
            OB = psb("out_b", [T, C])
            TM = psb("temp", [T, NH])
            HO = psb("head_of", [128, KT, NH])
            HTO = psb("head_to", [NH, KT, 128])
            WT = psb("w_T", [128, KT, GT])
            WSQ = psb("w_sq_T", [128, KT, GT])
            NS = psb("norm_sq", [128, KT, GB])
            RI = psb("head_of_scaled", [128, KT, GB, NH])
            SC = psb("tssa_score", [T, GB, NH])
            SX = psb("tssa_max", [T, GB])
            PI = psb("pi", [T, GB, NH])
            PIT = psb("pi_T", [NH, GT])
            AA = psb("pi_w_sq", [128, KT, GT])
            DOT = psb("dots", [128, KT, GB])
            SP_ = psb("pi_sum", [128, KT, GB])
            OT = psb("tssa_out_T", [128, KT, GT])
            ld = sem("tssa_loaded")
            xn_ready, xnT_in_psum, xnT_ready = sem("t_xn"), sem("t_xnT_psum"), sem("t_xnT")
            w_in_psum, w_ready, chain, act_chain = sem("w_psum"), sem("w_ready"), sem("tssa_chain"), sem("tssa_act")
            s_in_psum, piT_in_psum, piT_ready, pie_in_psum = sem("ts_psum"), sem("piT_psum"), sem("piT"), sem("pie_psum")
            o_in_psum, h_added, bias_added, st_made = sem("to_psum"), sem("t_h_added"), sem("t_bias"), sem("t_stats_made")
            on_vector, on_scalar = finish_norm("ln3")
            NC_ = 18
            with nc.Block() as block:
                @block.sync
                def _(sp):
                    for dst, src in ((AW, tssa_w), (OW, out_w), (OB, out_b), (TM, temp), (HO, head_of), (HTO, head_to)):
                        sp.dma_start(dst[:], src).then_inc(ld, 16)

                @block.gpsimd
                def _(pool):
                    pool.wait_ge(ld, 96)
                    with pool.Fori(0, G) as g:
                        pool.wait_ge(xn_ready, g * GB + GB)
                        hs = H[:, bass.ds(g * GB, GB), :]
                        pool.tensor_tensor(hs, hs, OB[:].rearrange("p (a c) -> p a c", a=1).to_broadcast([T, GB, C]), ALU.add).then_inc(bias_added, 1)

                @block.scalar
                def _(act):
                    on_scalar(act)
                    with act.Fori(0, G) as g:
                        for k in range(KT):
                            act.wait_ge(xnT_in_psum, g * KT + k + 1)
                            act.activation(XT[:, k, :], bank[4 + k][:, 0:GT], ACT.Copy).then_inc(xnT_ready, 1)
                        for k in range(KT):
                            act.wait_ge(w_in_psum, g * KT + k + 1)
                            act.activation(WSQ[:, k, :], bank[k][:, 0:GT], ACT.Square)
                            act.activation(WT[:, k, :], bank[k][:, 0:GT], ACT.Copy).then_inc(w_ready, 1)
                        act.wait_ge(chain, g * NC_ + 6)
                        act.activation(PI[:], SC[:], ACT.Exp).then_inc(act_chain, 1)
                        act.wait_ge(piT_in_psum, g + 1)
                        act.activation(PIT[:], bank[3][0:NH, 0:GT], ACT.Copy).then_inc(piT_ready, 1)

                @block.vector
                def _(dve):
                    on_vector(dve)
                    dve.sem_inc(h_added, GB)
                    dve.wait_ge(ld, 96)
                    with dve.Fori(0, G) as g:
                        n = [0]

                        def link(ins):
                            n[0] += 1
                            ins.then_inc(chain, 1)
                            dve.wait_ge(chain, g * NC_ + n[0])

                        normalise(dve, g, xn_ready)
                        dve.wait_ge(w_ready, g * KT + KT)
                        link(dve.tensor_reduce(NS[:], WSQ[:].rearrange("p k (b t) -> p k b t", b=GB), AX.X, ALU.add))
                        link(dve.tensor_scalar(NS[:], NS[:], 1e-24, None, ALU.max))
                        link(dve.reciprocal(NS[:], NS[:]))
                        for k in range(KT):
                            ins = dve.tensor_tensor(RI[:, k], HO[:, k:k + 1, :].to_broadcast([128, GB, NH]),
                                                    NS[:, k].rearrange("p (b a) -> p b a", a=1).to_broadcast([128, GB, NH]), ALU.mult)
                        link(ins)
                        dve.wait_ge(s_in_psum, g + 1)
                        link(dve.tensor_tensor(SC[:], bank[2][0:T, 0:GB * NH].rearrange("p (b h) -> p b h", b=GB),
                                               TM[:].rearrange("p (a h) -> p a h", a=1).to_broadcast([T, GB, NH]), ALU.mult))
                        dve.tensor_reduce(SX[:], SC[:], AX.X, ALU.max).then_inc(st_made, 1)
                        dve.wait_ge(st_made, g * 5 + 1)
                        link(dve.tensor_tensor(SC[:], SC[:], SX[:].rearrange("p (b a) -> p b a", a=1).to_broadcast([T, GB, NH]), ALU.subtract))
                        dve.wait_ge(act_chain, g + 1)
                        link(dve.tensor_reduce(SX[:], PI[:], AX.X, ALU.add))
                        link(dve.reciprocal(SX[:], SX[:]))
                        link(dve.tensor_tensor(PI[:], PI[:], SX[:].rearrange("p (b a) -> p b a", a=1).to_broadcast([T, GB, NH]), ALU.mult))
                        dve.wait_ge(pie_in_psum, g + 1)
                        for k in range(KT):
                            ins = dve.tensor_tensor(AA[:, k, :], bank[4 + k][:, 0:GT], WSQ[:, k, :], ALU.mult)
                        link(ins)
                        for k in range(KT):
                            dve.tensor_reduce(SP_[:, k, :], bank[4 + k][:, 0:GT].rearrange("p (b t) -> p b t", b=GB), AX.X, ALU.add)
                            ins = dve.tensor_reduce(DOT[:, k, :], AA[:, k, :].rearrange("p (b t) -> p b t", b=GB), AX.X, ALU.add)
                        link(ins)
                        link(dve.tensor_scalar(SP_[:], SP_[:], 1e-8, None, ALU.add))
                        link(dve.reciprocal(SP_[:], SP_[:]))
                        link(dve.tensor_tensor(DOT[:], DOT[:], SP_[:], ALU.mult))
                        link(dve.tensor_scalar(DOT[:], DOT[:], 1.0, None, ALU.add))
                        link(dve.reciprocal(DOT[:], DOT[:]))
                        for k in range(KT):
                            ins = dve.tensor_tensor(AA[:, k, :], bank[4 + k][:, 0:GT], WT[:, k, :], ALU.mult)
                        link(ins)
                        for k in range(KT):
                            ins = dve.scalar_tensor_tensor(out=OT[:, k, :].rearrange("p (b t) -> p b t", b=GB),
                                                           in0=AA[:, k, :].rearrange("p (b t) -> p b t", b=GB), scalar=-1.0,
                                                           in1=DOT[:, k].rearrange("p (b a) -> p b a", a=1).to_broadcast([128, GB, T]),
                                                           op0=ALU.mult, op1=ALU.mult)
                        link(ins)
                        dve.wait_ge(bias_added, g + 1)
                        for j in range(GB):
                            b = g * GB + j
                            dve.wait_ge(o_in_psum, g * GB + j + 1)
                            dve.tensor_tensor(row(H, b), bank[j][0:T, 0:C], row(H, b), ALU.add).then_inc(h_added, 1)
                            dve.wait_ge(h_added, g * GB + j + 1 + GB)
                            dve.bn_stats(row(ST, b), row(H, b)).then_inc(st_made, 1)
                        assert n[0] == NC_, n
                    dve.wait_ge(st_made, 5 * G)

                @block.tensor
                def _(pe):
                    pe.wait_ge(ld, 96)
                    with pe.Fori(0, G) as g:
                        pe.wait_ge(xn_ready, g * GB + GB)
                        for k in range(KT):
                            for b in range(GB):
                                mm = pe.transpose(bank[4 + k][:, b * T:b * T + T], XN[:, b, k * 128:k * 128 + 128], ID[0:T, 0:T])
                            mm.then_inc(xnT_in_psum, 1)
                        pe.wait_ge(xnT_ready, g * KT + KT)
                        pe.wait_ge(h_added, g * GB + GB)
                        for o in range(KT):
                            for k in range(KT):
                                mm = pe.matmul(bank[o][:, 0:GT], AW[:, k, o * 128:o * 128 + 128], XT[:, k, :], start=k == 0, stop=k == KT - 1)
                            mm.then_inc(w_in_psum, 1)
                        pe.wait_ge(chain, g * NC_ + 4)
                        for b in range(GB):
                            for k in range(KT):
                                mm = pe.matmul(bank[2][0:T, b * NH:b * NH + NH], WSQ[:, k, b * T:b * T + T], RI[:, k, b, :], start=k == 0, stop=k == KT - 1)
                        mm.then_inc(s_in_psum, 1)
                        pe.wait_ge(chain, g * NC_ + 9)
                        for b in range(GB):
                            mm = pe.transpose(bank[3][0:NH, b * T:b * T + T], PI[:, b, :], ID[0:T, 0:T])
                        mm.then_inc(piT_in_psum, 1)
                        pe.wait_ge(piT_ready, g + 1)
                        for k in range(KT):
                            mm = pe.matmul(bank[4 + k][:, 0:GT], HTO[:, k, :], PIT[:], start=True, stop=True)
                        mm.then_inc(pie_in_psum, 1)
                        pe.wait_ge(chain, g * NC_ + 18)
                        for b in range(GB):
                            for k in range(KT):
                                mm = pe.matmul(bank[b][0:T, 0:C], OT[:, k, b * T:b * T + T], OW[:, k, :], start=k == 0, stop=k == KT - 1)
                            mm.then_inc(o_in_psum, 1)

        with ExitStack() as p5:
            def psb(name, shape, dt=F32):
                return p5.enter_context(nc.sbuf_tensor(name, shape, dt))
            CC = psb("conv_col", [128, KT, 2])
            CM = psb("conv_mask", [128, KT, 64])
            CWT = psb("conv_w", [128, KT, 128])
            CB = psb("conv_b", [128, 1])
            GA = psb("gamma", [128, 1])
            BE = psb("beta", [128, 1])
            LW = psb("lin_w", [128, C])
            LB = psb("lin_b", [1, 2 * C])
            FW = psb("ffn_w", [128, KT, C])
            FB = psb("ffn_bias", [T, C])
            XC = psb("gate_pre", [128, B * T])
            XA = psb("gate_act", [128, B * T])
            FU = psb("full", [T, B, C])
            X4 = psb("x_kept", [T, B, C])
            CST = psb("bn_stats", [128, G, 6])
            CMV = psb("bn_mean_var", [128, 2])
            CS = psb("bn_scale_bias", [128, 4])
            ld = sem("ffn_loaded")
            xn_ready, xnT_in_psum, xnT_ready = sem("f_xn"), sem("f_xnT_psum"), sem("f_xnT")
            cw_made, xc_in_psum, xc_ready, full_in_psum, full_ready = (sem(n) for n in ("cw_made", "xc_psum", "xc", "full_psum", "full_ready"))
            x_kept = sem("x_kept")
            cst_made, bn_made, bn_sd, xa_ready = sem("cst_made"), sem("bn_made"), sem("bn_sd"), sem("xa_ready")
            on_vector, on_scalar = finish_norm("ln4")
            with nc.Block() as block:
                @block.sync
                def _(sp):
                    for dst, src in ((CC, conv_col), (CM, conv_mask), (CB, conv_b), (GA, gamma), (BE, beta), (LW, lin_w), (LB, lin_b), (FW, ffn_w), (FB, ffn_bias)):
                        sp.dma_start(dst[:], src).then_inc(ld, 16)

                @block.gpsimd
                def _(pool):
                    pool.wait_ge(ld, 144)
                    for k in range(KT):
                        for br_ in range(2):
                            pool.tensor_scalar(CWT[:, k, 64 * br_:64 * br_ + 64], CM[:, k, :], CC[:, k, br_:br_ + 1], None, ALU.mult).then_inc(cw_made, 1)
                    with pool.Fori(0, G) as g:
                        after(pool, xn_ready, g * GB + GB)
                        pool.tensor_copy(X4[:, bass.ds(g * GB, GB), :], XN[:]).then_inc(x_kept, 1)
                        hs = H[:, bass.ds(g * GB, GB), :]
                        pool.tensor_tensor(hs, hs, FB[:].rearrange("p (a c) -> p a c", a=1).to_broadcast([T, GB, C]), ALU.add).then_inc(x_kept, 1)
                    pool.wait_ge(x_kept, 2 * G)

                @block.scalar
                def _(act):
                    on_scalar(act)
                    act.wait_ge(ld, 144)
                    act.sem_inc(full_ready, 2)
                    with act.Fori(0, G) as g:
                        for k in range(KT):
                            act.wait_ge(xnT_in_psum, g * KT + k + 1)
                            act.activation(XT[:, k, :], bank[4 + k][:, 0:GT], ACT.Copy).then_inc(xnT_ready, 1)
                        act.wait_ge(xc_in_psum, g + 1)
                        act.activation(XC[:, bass.ds(g * GT, GT)], bank[0][:, 0:GT], ACT.Identity, bias=CB[:]).then_inc(xc_ready, 1)
                        for j in range(GB):
                            act.wait_ge(full_in_psum, g * GB + j + 1)
                            act.activation(row(FU, g * GB + j), bank[2 + j % 2][0:T, 0:C], ACT.Copy).then_inc(full_ready, 1)
                    act.wait_ge(bn_made, 1)
                    act.activation(CS[:, 0:1], CMV[:, 1:2], ACT.Sqrt, bias=EP[:]).then_inc(bn_sd, 1)
                    act.wait_ge(bn_made, 5)
                    act.activation(XA[:], XC[:], ACT.Gelu, bias=CS[:, 3:4], scale=CS[:, 2:3]).then_inc(xa_ready, 1)

                @block.vector
                def _(dve):
                    on_vector(dve)
                    with dve.Fori(0, G) as g:
                        normalise(dve, g, xn_ready)
                        dve.wait_ge(xc_ready, g + 1)
                        dve.bn_stats(CST[:, bass.ds(g, 1), :].rearrange("p a c -> p (a c)"), XC[:, bass.ds(g * GT, GT)]).then_inc(cst_made, 1)
                        dve.wait_ge(xnT_ready, g * KT + KT)
                        dve.wait_ge(x_kept, g * 2 + 2)
                    dve.wait_ge(cst_made, G)
                    dve.bn_aggr(CMV[:], CST[:]).then_inc(bn_made, 1)
                    dve.wait_ge(bn_sd, 1)
                    dve.reciprocal(CS[:, 1:2], CS[:, 0:1]).then_inc(bn_made, 1)
                    dve.wait_ge(bn_made, 2)
                    dve.tensor_tensor(CS[:, 2:3], CS[:, 1:2], GA[:], ALU.mult).then_inc(bn_made, 1)
                    dve.wait_ge(bn_made, 3)
                    dve.tensor_tensor(CS[:, 3:4], CS[:, 2:3], CMV[:, 0:1], ALU.mult).then_inc(bn_made, 1)
                    dve.wait_ge(bn_made, 4)
                    dve.tensor_tensor(CS[:, 3:4], BE[:], CS[:, 3:4], ALU.subtract).then_inc(bn_made, 1)

                @block.tensor
                def _(pe):
                    pe.wait_ge(ld, 144)
                    pe.wait_ge(cw_made, 4)
                    with pe.Fori(0, G) as g:
                        pe.wait_ge(xn_ready, g * GB + GB)
                        for k in range(KT):
                            for b in range(GB):
                                mm = pe.transpose(bank[4 + k][:, b * T:b * T + T], XN[:, b, k * 128:k * 128 + 128], ID[0:T, 0:T])
                            mm.then_inc(xnT_in_psum, 1)
                        pe.wait_ge(xnT_ready, g * KT + KT)
                        for k in range(KT):
                            mm = pe.matmul(bank[0][:, 0:GT], CWT[:, k, :], XT[:, k, :], start=k == 0, stop=k == KT - 1)
                        mm.then_inc(xc_in_psum, 1)
                        for b in range(GB):
                            pe.wait_ge(full_ready, g * GB + b + 1)
                            for k in range(KT):
                                mm = pe.matmul(bank[2 + b % 2][0:T, 0:C], XT[:, k, b * T:b * T + T], FW[:, k, :], start=k == 0, stop=k == KT - 1)
                            mm.then_inc(full_in_psum, 1)

            NB = 2
            XAB = psb("gate_act_step", [128, NB, T])
            M8 = psb("top8", [T, NB, 2, 8])
            NM = psb("neg_max", [T, NB, 2])
            EE = psb("score_exp", [T, NB, 2, C])
            E8 = psb("top8_exp", [T, NB, 2, 8])
            REM = psb("score_rest", [T, NB, 2, C])
            SS = psb("score_sum", [T, NB, 2])
            XS = psb("x_sparse", [T, NB, C])
            OS = psb("out_sparse", [T, NB, C])
            XST = psb("x_sparse_T", [128, NB, KT, T])
            OO = psb("out_tile", [T, NB, C])
            xab, l_in_psum, m8, ee, top, xs_ready, xsT_in_psum, xsT, in_psum, oo, stored = (
                sem(n) for n in ("xab", "ffn_l_psum", "m8", "ee", "topk", "xs", "xsT_psum", "xsT", "in_psum", "oo", "stored"))
            NT = 10 * NB
            with nc.Block() as block:
                @block.gpsimd
                def _(pool):
                    with pool.Fori(0, B // NB) as i:
                        after(pool, l_in_psum, i * NB + 1)
                        pool.tensor_copy(XAB[:], XA[:, bass.ds(i * NB * T, NB * T)].rearrange("p (a t) -> p a t", a=NB)).then_inc(xab, 1)

                @block.scalar
                def _(act):
                    with act.Fori(0, B // NB) as i:
                        for j in range(NB):
                            act.wait_ge(m8, i * 2 * NB + 2 * j + 2)
                            for r in range(2):
                                act.activation(EE[:, j, r, :], bank[6 * r + j][0:T, 0:C], ACT.Exp, bias=NM[:, j, r:r + 1],
                                               accum_out=SS[:, j, r:r + 1])
                                ins = act.activation(E8[:, j, r, :], M8[:, j, r, :], ACT.Exp, bias=NM[:, j, r:r + 1])
                            ins.then_inc(ee, 1)
                        for j in range(NB):
                            act.wait_ge(xsT_in_psum, i * NB + j + 1)
                            act.activation(XST[:, j], bank[2 + j][:, 0:KT * T].rearrange("p (k t) -> p k t", k=KT), ACT.Copy).then_inc(xsT, 1)

                @block.vector
                def _(dve):
                    dve.sem_inc(l_in_psum, 1)
                    dve.sem_inc(ee, NB)
                    with dve.Fori(0, B // NB) as i:
                        n = [0]

                        def mark(ins):
                            n[0] += 1
                            ins.then_inc(top, 1)

                        def done():
                            after(dve, top, i * NT + n[0])

                        for j in range(NB):
                            after(dve, l_in_psum, i * NB + j + 2)
                            for r in range(2):
                                ins = dve.max(M8[:, j, r, :], bank[6 * r + j][0:T, 0:C])
                            ins.then_inc(m8, 1)
                            dve.wait_ge(m8, i * 2 * NB + 2 * j + 1)
                            dve.tensor_scalar(NM[:, j, :], M8[:, j, :, 0], -1.0, None, ALU.mult).then_inc(m8, 1)
                        for rnd in range(TOPK // 8):
                            for j in range(NB):
                                if rnd == 0:
                                    after(dve, ee, i * NB + j + 1 + NB)
                                else:
                                    for r in range(2):
                                        ins = dve.max(E8[:, j, r, :], REM[:, j, r, :])
                                    mark(ins)
                            if rnd:
                                done()
                            for j in range(NB):
                                for r in range(2):
                                    src = EE if rnd == 0 else REM
                                    ins = dve.match_replace(REM[:, j, r, :], E8[:, j, r, :], src[:, j, r, :], 0.0)
                                mark(ins)
                            done()
                        for j in range(NB):
                            dve.reciprocal(SS[:, j, :], SS[:, j, :])
                            mark(dve.tensor_tensor(REM[:, j], EE[:, j], REM[:, j], ALU.subtract))
                        done()
                        for j in range(NB):
                            b = i * NB + j
                            dve.scalar_tensor_tensor(out=XS[:, j, :], in0=REM[:, j, 1, :], scalar=SS[:, j, 1:2], in1=row(X4, b),
                                                     op0=ALU.mult, op1=ALU.mult).then_inc(xs_ready, 1)
                            mark(dve.scalar_tensor_tensor(out=OS[:, j, :], in0=REM[:, j, 0, :], scalar=SS[:, j, 0:1], in1=row(FU, b),
                                                          op0=ALU.mult, op1=ALU.mult))
                        done()
                        for j in range(NB):
                            mark(dve.tensor_tensor(OS[:, j, :], OS[:, j, :], row(H, i * NB + j), ALU.add))
                        done()
                        dve.wait_ge(stored, i * 16 + 16)
                        for j in range(NB):
                            dve.wait_ge(in_psum, i * NB + j + 1)
                            dve.tensor_tensor(OO[:, j, :], bank[4 + j][0:T, 0:C], OS[:, j, :], ALU.add).then_inc(oo, 1)
                        assert n[0] == NT, n

                @block.sync
                def _(sp):
                    sp.sem_inc(stored, 16)
                    with sp.Fori(0, B // NB) as i:
                        sp.wait_ge(oo, i * NB + NB)
                        sp.dma_start(out[bass.ds(i * NB, NB)].rearrange("b t c -> t b c"), OO[:]).then_inc(stored, 16)
                    sp.wait_ge(stored, 16 * (B // NB) + 16)

                @block.tensor
                def _(pe):
                    with pe.Fori(0, B // NB) as i:
                        pe.wait_ge(xab, i + 1)
                        for j in range(NB):
                            pe.wait_ge(ee, i * NB + j + 1)
                            for r in range(2):
                                pe.matmul(bank[6 * r + j][0:T, 0:C], ONE[:, 0:T], LB[:, r * C:r * C + C], start=True, stop=False)
                            for r in range(2):
                                mm = pe.matmul(bank[6 * r + j][0:T, 0:C], XAB[64 * r:64 * r + 64, j, :], LW[64 * r:64 * r + 64, :], start=False, stop=True)
                            mm.then_inc(l_in_psum, 1)
                        for j in range(NB):
                            pe.wait_ge(xs_ready, i * NB + j + 1)
                            for k in range(KT):
                                mm = pe.transpose(bank[2 + j][:, k * T:k * T + T], XS[:, j, k * 128:k * 128 + 128], ID[0:T, 0:T])
                            mm.then_inc(xsT_in_psum, 1)
                        for j in range(NB):
                            pe.wait_ge(xsT, i * NB + j + 1)
                            for k in range(KT):
                                mm = pe.matmul(bank[4 + j][0:T, 0:C], XST[:, j, k, :], FW[:, k, :], start=k == 0, stop=k == KT - 1)
                            mm.then_inc(in_psum, 1)


def _layout(i):
    import numpy as np
    f = np.float32
    a = {k: np.asarray(v) for k, v in i.items()}
    o = {}
    p = a["x"].reshape(B, 3, 6, 16, 6, 16).transpose(1, 3, 5, 0, 2, 4).reshape(768, B, NP)
    pt = np.zeros((768, B // 2, 2, 64), f)
    pt[:, :, :, 1:1 + NP] = p.reshape(768, B // 2, 2, NP)
    o["patches"] = pt.reshape(PK, 128, G, GB // 2, 128).transpose(2, 1, 3, 0, 4)
    hb = np.zeros((B, T, C), f)
    hb[:, 0] = a["L0_tok_cls_token"][0]
    hb[:, 1:1 + NP] = a["L0_tok_b"]
    hb[:, 1 + NP:] = a["txt"]
    o["h_base"] = hb.transpose(1, 0, 2)
    kt = lambda w: w.reshape(-1, 128, w.shape[-1]).transpose(1, 0, 2)
    o["tok_w"] = kt(a["L0_tok_W"])
    w = a["L0_attn_Wqkv"].reshape(C, 3, NH, HD)
    bb = a["L0_attn_bqkv"].reshape(3, NH, HD)
    z = np.zeros_like(w[:, 0])
    o["wkv"] = kt(np.concatenate([w[:, 1], w[:, 2]], -1).reshape(C, -1))
    o["wq"] = kt(np.concatenate([w[:, 0], z], -1).reshape(C, -1))
    o["bkv"] = np.tile(np.concatenate([bb[1], bb[2]], -1).T, (GB, 1))
    o["bq"] = np.tile(np.concatenate([bb[0], np.zeros_like(bb[0])], -1).T, (GB, 1))
    o["wproj"] = kt(a["L0_attn_Wproj"])
    rep = lambda v: np.tile(v.reshape(1, -1), (T, 1))
    o["bproj"] = rep(a["L0_attn_bproj"])
    m = np.where(np.arange(T)[None, :] <= np.arange(T)[:, None], 0.0, NEG)
    o["mask4"] = np.tile(m, (1, HQ)).astype(f)
    o["ident"] = np.eye(128, dtype=f)
    o["w1"] = a["L0_ffn_W1"].reshape(E, KT, 128, HID).transpose(0, 2, 1, 3)
    o["b1"] = a["L0_ffn_b1"].reshape(E, HT, 128).transpose(0, 2, 1)
    o["w2"] = a["L0_ffn_W2"].reshape(E, HT, 128, C).transpose(0, 2, 1, 3)
    o["b2"] = a["L0_ffn_b2"]
    o["wr"] = kt(a["L0_ffn_Wr"])
    o["br"] = a["L0_ffn_br"].reshape(E, 1)
    o["tssa_w"] = kt(a["L1_attn_qkv_w"].T)
    o["temp"] = rep(a["L1_attn_temp"])
    ho = np.repeat(np.eye(NH, dtype=f), HD, axis=0)
    o["head_of"] = kt(ho)
    o["head_to"] = ho.T.reshape(NH, KT, 128)
    o["out_w"] = kt(a["L1_attn_out_w"].T)
    o["out_b"] = rep(a["L1_attn_out_b"])
    cc = np.stack([a["L1_ffn_so_conv_w"].reshape(-1), a["L1_ffn_si_conv_w"].reshape(-1)], -1)
    o["conv_col"] = kt(cc)
    o["conv_mask"] = kt(np.repeat(np.eye(64, dtype=f), 4, axis=0))
    both = lambda n: np.concatenate([a[f"L1_ffn_so_{n}"], a[f"L1_ffn_si_{n}"]]).reshape(-1, 1)
    o["conv_b"], o["gamma"], o["beta"] = both("conv_b"), both("gamma"), both("beta")
    o["lin_w"] = np.concatenate([a["L1_ffn_so_lin_w"].T, a["L1_ffn_si_lin_w"].T])
    o["lin_b"] = both("lin_b").reshape(1, -1)
    o["ffn_w"] = kt(a["L1_ffn_weight"])
    o["ffn_bias"] = rep(a["L1_ffn_bias"])
    return {k: np.ascontiguousarray(v) for k, v in o.items()}


def kernel(**inputs):
    import concourse.bacc as _bacc
    from concourse import mybir as _mybir
    from concourse.bass_utils import run_bass_kernel_spmd as _run

    nc = _bacc.Bacc("TRN2", target_bir_lowering=False, num_devices=1)
    arrays = _layout(inputs)
    args = {k: nc.dram_tensor(f"in_{k}", v.shape, _mybir.dt.from_np(v.dtype), kind="ExternalInput").ap() for k, v in arrays.items()}
    args["out"] = nc.dram_tensor("out", (B, T, C), F32, kind="ExternalOutput").ap()
    early_fusion(nc, **args)
    arrays = {f"in_{k}": v for k, v in arrays.items()}
    return _run(nc, [arrays], core_ids=[0]).results[0]["out"]
```

```python
from contextlib import ExitStack

import concourse.bass as bass
from concourse import mybir

F32 = mybir.dt.float32
BF16 = mybir.dt.bfloat16
ALU = mybir.AluOpType
ACT = mybir.ActivationFunctionType
AX = mybir.AxisListType

B = 16
T = 114
NP = 36
C = 256
KT = C // 128
PK = 768 // 128
GB = 4
G = B // GB
GT = GB * T
NH, HD = 16, 16
HQ = 4
NQ = NH // HQ
E = 8
HID = 1024
HT = HID // 128
EPS = 1e-5
TOPK = 32
NEG = -1.0e30
I32 = mybir.dt.int32
NBLK = -(-B * T // 128)
RUN = 5
assert NBLK % RUN == 0
ROW = C + E
RAT = [0]
for _w in (128, NBLK + 1, 1, 1, 1, E * B, E * B, T):
    RAT.append(RAT[-1] + _w)
RCOLS = RAT[-1]


def early_fusion(nc: bass.Bass, patches, h_base, tok_w, wkv, wq, bkv, bq, wproj, bproj, mask4, ident,
                 w1, b1, w2, b2, wr, br, route_consts, tssa_w, temp, head_of, head_to, out_w, out_b,
                 conv_col, conv_mask, conv_b, gamma, beta, lin_w, lin_b, ffn_w, ffn_bias, out):
    with ExitStack() as ctx:
        def sb(name, shape, dt=F32):
            return ctx.enter_context(nc.sbuf_tensor(name, shape, dt))

        def sem(name):
            return ctx.enter_context(nc.semaphore(name))

        bank = [ctx.enter_context(nc.psum_tensor(f"bank{i}", [128, 512], F32)) for i in range(8)]

        x_rows = nc.dram_tensor("x_rows", (B * T + 128, ROW), F32, kind="Internal").ap()
        h_rows = nc.dram_tensor("h_rows", (B * T + 128, C), F32, kind="Internal").ap()

        H = sb("h", [T, B, C])
        ID = sb("identity", [128, 128])
        EP = sb("eps", [128, 1])
        ONE = sb("ones_row", [1, 128])
        XN = sb("x_normed", [T, GB, C])
        XT = sb("x_normed_T", [128, KT, GT])
        ST = sb("ln_stats", [T, B, 6])
        MV = sb("ln_mean_var", [T, B, 2])
        SD = sb("ln_std", [T, B])
        RS = sb("ln_rstd", [T, B])

        h_loaded = sem("h_loaded")
        consts_loaded = sem("consts_loaded")
        const_set = sem("const_set")
        waited = sem("waited")

        def finish_norm(stage):
            stats_made, std_made, aggregated = (sem(f"{stage}_{n}") for n in ("stats", "std", "aggr"))

            def on_vector(dve):
                for b in range(B):
                    ins = dve.bn_aggr(MV[:, b, :], ST[:, b, :])
                ins.then_inc(aggregated, 1)
                dve.wait_ge(std_made, 1)
                dve.reciprocal(RS[:, :], SD[:, :]).then_inc(stats_made, 1)
                dve.wait_ge(stats_made, 1)

            def on_scalar(act):
                act.wait_ge(aggregated, 1)
                act.activation(SD[:, :], MV[:, :, 1], ACT.Sqrt, bias=EP[0:T, :]).then_inc(std_made, 1)
            return on_vector, on_scalar

        with ExitStack() as p1:
            PT = p1.enter_context(nc.sbuf_tensor("patches_T", [128, GB // 2, PK, 128], F32))
            TW = p1.enter_context(nc.sbuf_tensor("tok_w", [128, PK, C], F32))
            patches_loaded, tok_w_loaded = sem("patches_loaded"), sem("tok_w_loaded")
            tok_in_psum, tok_added = sem("tok_in_psum"), sem("tok_added")
            with nc.Block() as block:
                @block.sync
                def _(sp):
                    sp.dma_start(TW[:], tok_w).then_inc(tok_w_loaded, 16)
                    sp.dma_start(H[:], h_base).then_inc(h_loaded, 16)
                    sp.dma_start(ID[:], ident).then_inc(consts_loaded, 16)
                    sp.dma_start(PT[:], patches[0]).then_inc(patches_loaded, 16)
                    with sp.Fori(1, G) as g:
                        sp.wait_ge(tok_in_psum, g * 2)
                        sp.dma_start(PT[:], patches[bass.ds(g, 1)].rearrange("a p q k m -> (a p) q k m")).then_inc(patches_loaded, 16)

                @block.tensor
                def _(pe):
                    pe.wait_ge(tok_w_loaded, 16)
                    with pe.Fori(0, G) as g:
                        pe.wait_ge(patches_loaded, g * 16 + 16)
                        for q in range(2):
                            pe.wait_ge(tok_added, g * GB + 2 * q + 1)
                            for k in range(PK):
                                mm = pe.matmul(bank[q][:, 0:C], PT[:, q, k, :], TW[:, k, :], start=k == 0, stop=k == PK - 1)
                            mm.then_inc(tok_in_psum, 1)

                @block.vector
                def _(dve):
                    dve.memset(EP[:], EPS)
                    dve.memset(ONE[:], 1.0).then_inc(tok_added, 3)
                    dve.wait_ge(h_loaded, 16)
                    with dve.Fori(0, G) as g:
                        for q in range(2):
                            dve.wait_ge(tok_in_psum, g * 2 + q + 1)
                            for j in range(2):
                                b = g * GB + 2 * q + j
                                rows = H[0:NP + 1, bass.ds(b, 1), :].rearrange("p a c -> p (a c)")
                                dve.tensor_tensor(rows, bank[q][64 * j:64 * j + NP + 1, 0:C], rows, ALU.add).then_inc(tok_added, 1)
                        dve.wait_ge(tok_added, g * GB + GB + 3)
                        for j in range(GB):
                            b = g * GB + j
                            dve.bn_stats(ST[:, bass.ds(b, 1), :].rearrange("p a c -> p (a c)"),
                                         H[:, bass.ds(b, 1), :].rearrange("p a c -> p (a c)")).then_inc(const_set, 1)
                    dve.wait_ge(const_set, B)

        def after(eng, signal, value):
            eng.wait_ge(signal, value)
            eng.sem_inc(waited, 1)

        def normalise(dve, g, xn_ready):
            for j in range(GB):
                b = g * GB + j
                dve.tensor_scalar(XN[:, j, :], H[:, bass.ds(b, 1), :].rearrange("p a c -> p (a c)"),
                                  MV[:, bass.ds(b, 1), 0], RS[:, bass.ds(b, 1)],
                                  ALU.subtract, ALU.mult).then_inc(xn_ready, 1)

        def row(t, b):
            return t[:, bass.ds(b, 1), :].rearrange("p a c -> p (a c)")

        with ExitStack() as p2:
            def psb(name, shape, dt=F32):
                return p2.enter_context(nc.sbuf_tensor(name, shape, dt))
            WKV = psb("wkv", [128, KT, NH * 32])
            WQ = psb("wq", [128, KT, NH * 32])
            BKV = psb("bkv", [128, NH])
            BQ = psb("bq", [128, NH])
            WP = psb("wproj", [128, KT, C])
            BP = psb("bproj", [T, C])
            MF = psb("mask4_f", [T, GT])
            MK = psb("mask4", [T, GT], BF16)
            IB = psb("identity_bf", [128, 128], BF16)
            KV = psb("kv_T", [128, T * NH])
            Q = psb("q_T", [128, T * NH])
            KVA = psb("kv_T_all", [128, G, T * NH])
            QA = psb("q_T_all", [128, G, T * NH])
            VS = psb("v_rows", [T, NH, GB, 32])
            attn_w_loaded = sem("attn_w_loaded")
            v_frame_set, mask_made = sem("v_frame_set"), sem("mask_made")
            xn_ready, xnT_in_psum, xnT_ready = sem("a_xn"), sem("a_xnT_psum"), sem("a_xnT")
            kv_in_psum, q_in_psum, kv_made, q_made = sem("kv_psum"), sem("q_psum"), sem("kv_made"), sem("q_made")
            bias_added = sem("bproj_added")
            q_copied, kv_copied = sem("q_copied"), sem("kv_copied")
            on_vector, on_scalar = finish_norm("ln1")
            n_loads = 7

            with ExitStack() as p2a:
                XN2 = p2a.enter_context(nc.sbuf_tensor("attn_x", [T, 2, GB, C], F32))
                XTA = p2a.enter_context(nc.sbuf_tensor("attn_x_T", [128, KT, GB, G, T], F32))
                with nc.Block() as block:
                    @block.sync
                    def _(sp):
                        for dst, src in ((WKV, wkv), (WQ, wq), (BKV, bkv), (BQ, bq), (WP, wproj), (BP, bproj), (MF, mask4)):
                            sp.dma_start(dst[:], src).then_inc(attn_w_loaded, 16)

                    @block.gpsimd
                    def _(pool):
                        pool.memset(VS[:, :, :, HD:32], 0.0).then_inc(v_frame_set, 1)
                        pool.wait_ge(v_frame_set, 1)
                        pool.memset(VS[:, :, :, HD:HD + 1], 1.0).then_inc(v_frame_set, 1)
                        pool.wait_ge(attn_w_loaded, 16 * n_loads)
                        for g in range(G):
                            pool.wait_ge(xn_ready, g * GB + GB)
                            hs = H[:, g * GB:g * GB + GB, :]
                            pool.tensor_tensor(hs, hs, BP[:].rearrange("p (a c) -> p a c", a=1).to_broadcast([T, GB, C]), ALU.add).then_inc(bias_added, 1)
                        pool.wait_ge(bias_added, G)
                        pool.wait_ge(v_frame_set, 2)

                    @block.scalar
                    def _(act):
                        on_scalar(act)
                        for g in range(G):
                            for k in range(KT):
                                act.wait_ge(xnT_in_psum, g * KT + k + 1)
                                act.activation(XTA[:, k, :, g, :], bank[4 + 2 * (g % 2) + k][:, 0:GT].rearrange("p (b t) -> p b t", t=T), ACT.Copy).then_inc(xnT_ready, 1)
                        act.wait_ge(attn_w_loaded, 16 * n_loads)
                        for c in range(NH):
                            act.wait_ge(kv_in_psum, c + 1)
                            act.activation(KVA[:].rearrange("p g (t c) -> p g t c", c=NH)[:, :, :, c], bank[c % 2][:, 0:GT].rearrange("p (g t) -> p g t", t=T),
                                           ACT.Identity, bias=BKV[:, c:c + 1]).then_inc(kv_made, 1)
                        act.wait_ge(kv_made, NH)
                        act.activation(KV[:], KVA[:, 0, :], ACT.Copy).then_inc(kv_copied, 1)
                        act.wait_ge(kv_copied, 1)

                    @block.vector
                    def _(dve):
                        on_vector(dve)
                        for g in range(G):
                            if g >= 2:
                                dve.wait_ge(xnT_in_psum, (g - 1) * KT)
                            for j in range(GB):
                                b = g * GB + j
                                dve.tensor_scalar(XN2[:, g % 2, j, :], H[:, b, :], MV[:, b, 0:1], RS[:, b:b + 1], ALU.subtract, ALU.mult).then_inc(xn_ready, 1)
                        dve.wait_ge(attn_w_loaded, 16 * n_loads)
                        dve.wait_ge(consts_loaded, 16)
                        dve.tensor_copy(IB[:], ID[:])
                        dve.tensor_copy(MK[:], MF[:]).then_inc(mask_made, 1)
                        for c in range(NH):
                            dve.wait_ge(q_in_psum, c + 1)
                            dve.tensor_scalar(QA[:].rearrange("p g (t c) -> p g t c", c=NH)[:, :, :, c], bank[2 + c % 2][:, 0:GT].rearrange("p (g t) -> p g t", t=T),
                                              BQ[:, c:c + 1], None, ALU.add).then_inc(q_made, 1)
                        dve.wait_ge(q_made, NH)
                        dve.tensor_copy(Q[:], QA[:, 0, :]).then_inc(q_copied, 1)
                        dve.wait_ge(q_copied, 1)
                        dve.wait_ge(mask_made, 1)

                    @block.tensor
                    def _(pe):
                        pe.wait_ge(consts_loaded, 16)
                        for g in range(G):
                            pe.wait_ge(xn_ready, g * GB + GB)
                            if g >= 2:
                                pe.wait_ge(xnT_ready, (g - 1) * KT)
                            for k in range(KT):
                                for b in range(GB):
                                    mm = pe.transpose(bank[4 + 2 * (g % 2) + k][:, b * T:b * T + T], XN2[:, g % 2, b, k * 128:k * 128 + 128], ID[0:T, 0:T])
                                mm.then_inc(xnT_in_psum, 1)
                        pe.wait_ge(attn_w_loaded, 16 * n_loads)
                        pe.wait_ge(xnT_ready, G * KT)
                        for c in range(NH):
                            for w, first, in_psum, emptied in ((WKV, 0, kv_in_psum, kv_made), (WQ, 2, q_in_psum, q_made)):
                                if c >= 2:
                                    pe.wait_ge(emptied, c - 1)
                                for k in range(KT):
                                    for j in range(GB):
                                        mm = pe.matmul(bank[first + c % 2][32 * j:32 * j + 32, 0:GT], w[:, k, c * 32:c * 32 + 32],
                                                       XTA[:, k, j].rearrange("p g t -> p (g t)"), start=k == 0, stop=k == KT - 1)
                                mm.then_inc(in_psum, 1)

            PR = psb("probs", [T, 2, GB, GT])
            PTR = psb("probs_T", [T, 2, GB, GT])
            MX = psb("row_max", [T, GB, HQ])
            YT = psb("y_T", [128, 2, GT])
            RD = psb("row_sum_recip", [T, HQ, GB])
            YN = psb("y_normed", [T, GB, C])
            YNT = psb("y_normed_T", [128, KT, GT])
            vT_in_psum, v_ready = sem("vT_psum"), sem("v_ready")
            s_in_psum, s_shifted, max_made, p_ready = sem("s_psum"), sem("s_shifted"), sem("max_made"), sem("p_ready")
            pT_in_psum, pT_ready = sem("pT_psum"), sem("pT")
            y_in_psum, yT_ready, yrow_in_psum, y_normed, rd_made = (sem(n) for n in ("y_psum", "yT", "yrow_psum", "y_normed", "rd_made"))
            ynT_in_psum, ynT_ready, proj_in_psum, h_added, st_made = (sem(n) for n in ("ynT_psum", "ynT", "proj_psum", "h_added", "a_stats_made"))

            def groups(eng, body):
                body(0, False)
                with eng.Fori(1, G) as g:
                    body(g, True)

            with nc.Block() as block:
                @block.gpsimd
                def _(pool):
                    with pool.Fori(1, G) as g:
                        after(pool, s_in_psum, g * 16)
                        pool.tensor_copy(Q[:], QA[:, bass.ds(g, 1), :].rearrange("p a n -> p (a n)")).then_inc(q_copied, 1)
                        pool.tensor_copy(KV[:], KVA[:, bass.ds(g, 1), :].rearrange("p a n -> p (a n)")).then_inc(kv_copied, 1)

                @block.scalar
                def _(act):
                    def exp_scores(g, q, b):
                        act.wait_ge(s_shifted, g * 16 + 4 * q + b + 1)
                        act.activation(PR[:, q % 2, b, :], PR[:, q % 2, b, :], ACT.Exp, scale=HD ** -0.5).then_inc(p_ready, 1)

                    def move_probs(g, q, b):
                        n = 4 * q + b
                        act.wait_ge(pT_in_psum, g * 16 + n + 1)
                        act.activation(PTR[:, q % 2, b, :], bank[4 + n % 2][0:T, 0:GT], ACT.Copy).then_inc(pT_ready, 1)

                    def move_y(g, q):
                        act.wait_ge(y_in_psum, g * NQ + q + 1)
                        act.activation(YT[:, q % 2, :], bank[6][:, 0:GT], ACT.Copy).then_inc(yT_ready, 1)

                    def move_normed(g):
                        for k in range(KT):
                            act.wait_ge(ynT_in_psum, g * KT + k + 1)
                            act.activation(YNT[:, k, :], bank[6 + k][:, 0:GT], ACT.Copy).then_inc(ynT_ready, 1)

                    def body(g, late):
                        for q in range(NQ):
                            exp_scores(g, 0, q)
                            act.wait_ge(vT_in_psum, g * NQ + q + 1)
                            act.activation(VS[:, HQ * q:HQ * q + HQ, :, 0:HD],
                                           bank[4 + q % 2][0:T, :].rearrange("p (h b d) -> p h b d", h=HQ, b=GB)[:, :, :, HD:2 * HD],
                                           ACT.Copy).then_inc(v_ready, 1)
                        if late:
                            move_normed(g - 1)
                        for q in range(NQ):
                            for b in range(GB):
                                move_probs(g, q, b)
                                if q + 1 < NQ:
                                    exp_scores(g, q + 1, b)
                            move_y(g, q)

                    groups(act, body)
                    move_normed(G - 1)

                @block.vector
                def _(dve):
                    def shift_scores(g, q, b):
                        n = g * 16 + 4 * q + b + 1
                        dve.wait_ge(s_in_psum, n)
                        s = bank[b][0:T, 0:GT].rearrange("p (h s) -> p h s", h=HQ)
                        dve.tensor_reduce(MX[:, b, :], s, AX.X, ALU.max).then_inc(max_made, 1)
                        if q >= 2:
                            dve.wait_ge(pT_in_psum, g * 16 + 4 * (q - 2) + b + 1)
                        dve.wait_ge(max_made, n)
                        dve.tensor_tensor(PR[:, q % 2, b, :].rearrange("p (h s) -> p h s", h=HQ), s,
                                          MX[:, b, :].rearrange("p (h a) -> p h a", a=1).to_broadcast([T, HQ, T]),
                                          ALU.subtract).then_inc(s_shifted, 1)

                    def norm_y(g, q):
                        dve.wait_ge(yrow_in_psum, g * NQ + q + 1)
                        y = bank[7][0:T, :].rearrange("p (h b d) -> p h b d", h=HQ, b=GB)
                        dve.reciprocal(RD[:], y[:, :, :, HD]).then_inc(rd_made, 1)
                        dve.wait_ge(rd_made, g * NQ + q + 1)
                        dve.tensor_tensor(YN[:].rearrange("p b (h d) -> p h b d", d=HD)[:, HQ * q:HQ * q + HQ],
                                          y[:, :, :, 0:HD],
                                          RD[:].rearrange("p h (b a) -> p h b a", a=1).to_broadcast([T, HQ, GB, HD]),
                                          ALU.mult).then_inc(y_normed, 1)

                    def add_to_h(g):
                        for j in range(GB):
                            b = g * GB + j
                            dve.wait_ge(proj_in_psum, g * 2 + j // 2 + 1)
                            dve.tensor_tensor(row(H, b), bank[6 + j // 2][0:T, (j % 2) * C:(j % 2) * C + C], row(H, b), ALU.add).then_inc(h_added, 1)
                            dve.wait_ge(h_added, g * GB + j + 1)
                            dve.bn_stats(row(ST, b), row(H, b)).then_inc(st_made, 1)

                    def body(g, late):
                        for q in range(NQ):
                            if q == 3:
                                norm_y(g, 0)
                            for b in range(GB):
                                shift_scores(g, q, b)
                            if late and q == 0:
                                norm_y(g - 1, NQ - 1)
                            if late and q == 1:
                                add_to_h(g - 1)
                        norm_y(g, 1)
                        norm_y(g, 2)

                    groups(dve, body)
                    norm_y(G - 1, NQ - 1)
                    add_to_h(G - 1)
                    dve.wait_ge(st_made, B)

                @block.tensor
                def _(pe):
                    def scores(g, q):
                        for b in range(GB):
                            if q or not isinstance(g, int):
                                pe.wait_ge(s_shifted, g * 16 + 4 * q - 3 + b)
                            pe.matmul(bank[b][0:T, 0:GT], IB[0:T, 0:T], MK[:, :], start=True, stop=False, skip_group_check=True)
                        for h in range(HQ):
                            r = (HQ * q + h) * T
                            for b in range(GB):
                                mm = pe.matmul(bank[b][0:T, h * T:h * T + T], Q[32 * b:32 * b + HD, r:r + T],
                                               KV[32 * b:32 * b + HD, r:r + T], start=False, stop=True, skip_group_check=True)
                                if h == HQ - 1:
                                    mm.then_inc(s_in_psum, 1)

                    def transpose_v(g, late):
                        for q in range(NQ):
                            if q >= 2:
                                pe.wait_ge(v_ready, g * NQ + q - 1)
                            elif late:
                                pe.wait_ge(pT_ready, g * 16)
                            for h in range(HQ):
                                r = (HQ * q + h) * T
                                mm = pe.transpose(bank[4 + q % 2][0:T, h * 128:h * 128 + 128], KV[:, r:r + T], ID[:, :])
                            mm.then_inc(vT_in_psum, 1)

                    def transpose_probs(g, q):
                        for b in range(GB):
                            n = 4 * q + b
                            if n >= 2:
                                pe.wait_ge(pT_ready, g * 16 + n - 1)
                            else:
                                pe.wait_ge(v_ready, g * NQ + NQ)
                            pe.wait_ge(p_ready, g * 16 + n + 1)
                            for h in range(HQ):
                                mm = pe.transpose(bank[4 + n % 2][0:T, h * T:h * T + T], PR[:, q % 2, b, h * T:h * T + T], ID[0:T, 0:T])
                            mm.then_inc(pT_in_psum, 1)

                    def apply_probs(g, q, late):
                        pe.wait_ge(pT_ready, g * 16 + 4 * q + 4)
                        if q:
                            pe.wait_ge(yT_ready, g * NQ + q)
                        elif late:
                            pe.wait_ge(h_added, g * GB)
                        for h in range(HQ):
                            for b in range(GB):
                                mm = pe.matmul(bank[6][32 * b:32 * b + 32, h * T:h * T + T], VS[:, HQ * q + h, b, :],
                                               PTR[:, q % 2, b, h * T:h * T + T], start=True, stop=True)
                        mm.then_inc(y_in_psum, 1)

                    def y_rows(g, q):
                        pe.wait_ge(yT_ready, g * NQ + q + 1)
                        if q:
                            pe.wait_ge(y_normed, g * NQ + q)
                        for h in range(HQ):
                            mm = pe.transpose(bank[7][0:T, h * 128:h * 128 + 128], YT[:, q % 2, h * T:h * T + T], ID[:, :])
                        mm.then_inc(yrow_in_psum, 1)

                    def transpose_y(g):
                        pe.wait_ge(y_normed, g * NQ + NQ)
                        for k in range(KT):
                            for b in range(GB):
                                mm = pe.transpose(bank[6 + k][:, b * T:b * T + T], YN[:, b, k * 128:k * 128 + 128], ID[0:T, 0:T])
                            mm.then_inc(ynT_in_psum, 1)

                    def project(g):
                        pe.wait_ge(ynT_ready, g * KT + KT)
                        for b in range(GB):
                            for k in range(KT):
                                mm = pe.matmul(bank[6 + b // 2][0:T, (b % 2) * C:(b % 2) * C + C], YNT[:, k, b * T:b * T + T], WP[:, k, :], start=k == 0, stop=k == KT - 1)
                            if b % 2:
                                mm.then_inc(proj_in_psum, 1)

                    def body(g, late):
                        pe.wait_ge(q_copied, g + 1)
                        pe.wait_ge(kv_copied, g + 1)
                        scores(g, 0)
                        transpose_v(g, late)
                        if late:
                            y_rows(g - 1, NQ - 1)
                        scores(g, 1)
                        if late:
                            transpose_y(g - 1)
                        transpose_probs(g, 0)
                        if late:
                            project(g - 1)
                        scores(g, 2)
                        apply_probs(g, 0, late)
                        transpose_probs(g, 1)
                        y_rows(g, 0)
                        apply_probs(g, 1, late)
                        scores(g, 3)
                        for q in range(2, NQ):
                            transpose_probs(g, q)
                            y_rows(g, q - 1)
                            apply_probs(g, q, late)

                    groups(pe, body)
                    y_rows(G - 1, NQ - 1)
                    transpose_y(G - 1)
                    project(G - 1)

        with ExitStack() as p3:
            def psb(name, shape, dt=F32):
                return p3.enter_context(nc.sbuf_tensor(name, shape, dt))
            XG = psb("moe_rows", [T, B, ROW])
            KEEPB = psb("kept_bf", [T, E, B], BF16)
            W1 = psb("w1", [128, 2, KT, HID])
            W2 = psb("w2", [128, 2, HT, C])
            B1 = psb("b1", [128, 2, HT])
            RC = psb("route_consts", [128, RCOLS])
            IDX = psb("token_of_slot", [128, E, NBLK], I32)
            TB = psb("expert_counts", [1, 3 * E], I32)
            iota1, thr, pidx, pad, negpad, bidx, reset, tri = (RC[:, a:b] for a, b in zip(RAT[:-1], RAT[1:]))
            B2 = psb("b2", [128, 2, C])
            ZR = psb("zero_rows", [128, ROW])
            wld = [sem(f"experts_loaded{i}") for i in range(2)]
            rows_stored = sem("rows_stored")

            EXPERT_LOADED = 4 * 16

            def load_expert(sp, e, s):
                for dst, src in ((W1[:, s], w1), (W2[:, s], w2), (B1[:, s], b1)):
                    src = src[bass.ds(e, 1)]
                    src = src.rearrange("a p k n -> (a p) k n") if len(src.shape) == 4 else src.rearrange("a p k -> (a p) k")
                    sp.dma_start(dst, src).then_inc(wld[s], 16)
                sp.dma_start(B2[:, s, :], b2[bass.ds(e, 1), :].to_broadcast([128, C])).then_inc(wld[s], 16)

            with ExitStack() as p3a:
                def psb(name, shape, dt=F32):
                    return p3a.enter_context(nc.sbuf_tensor(name, shape, dt))
                WR = psb("wr", [128, KT, E])
                BR = psb("br", [T, E])
                XT3 = psb("moe_x_T", [128, 2, KT, GT])
                LG = psb("logits", [T, B, E])
                M8 = psb("logits_sorted", [T, B, E])
                KEEP = psb("kept", [T, B, E])
                EX = psb("gate_exp", [T, B, E])
                SM = psb("gate_sum", [T, B])
                ld, consts_in = sem("router_loaded"), sem("route_consts_loaded")
                xn_ready, xnT_in_psum, xnT_ready = sem("m_xn"), sem("m_xnT_psum"), sem("m_xnT")
                l_in_psum, chain, shifted, gate_exp, gates_made = sem("l_psum"), sem("gate_chain"), sem("logits_shifted"), sem("gate_exp_made"), sem("gates_made")
                zeros_set = sem("zeros_set")
                on_vector, on_scalar = finish_norm("ln2")
                with nc.Block() as block:
                    @block.sync
                    def _(sp):
                        for dst, src in ((WR, wr), (BR, br)):
                            sp.dma_start(dst[:], src).then_inc(ld, 16)
                        sp.dma_start(RC[:], route_consts).then_inc(consts_in, 16)
                        sp.dma_start(h_rows[0:B * T, :].rearrange("(b t) c -> t b c", t=T), H[:]).then_inc(rows_stored, 16)
                        sp.wait_ge(zeros_set, 1)
                        sp.dma_start(x_rows[B * T:, :], ZR[:]).then_inc(rows_stored, 16)
                        sp.dma_start(h_rows[B * T:, :], ZR[:, 0:C]).then_inc(rows_stored, 16)
                        load_expert(sp, 0, 0)
                        sp.wait_ge(gates_made, 1)
                        sp.dma_start(x_rows[0:B * T, :].rearrange("(b t) c -> t b c", t=T), XG[:]).then_inc(rows_stored, 16)
                        load_expert(sp, 1, 1)
                        sp.wait_ge(consts_in, 16)

                    @block.gpsimd
                    def _(pool):
                        pool.memset(ZR[:], 0.0).then_inc(zeros_set, 1)

                    @block.scalar
                    def _(act):
                        on_scalar(act)
                        for g in range(G):
                            for k in range(KT):
                                act.wait_ge(xnT_in_psum, g * KT + k + 1)
                                act.activation(XT3[:, g % 2, k, :], bank[4 + 2 * (g % 2) + k][:, 0:GT], ACT.Copy).then_inc(xnT_ready, 1)
                        act.wait_ge(shifted, 1)
                        act.activation(EX[:], EX[:], ACT.Exp).then_inc(gate_exp, 1)

                    @block.vector
                    def _(dve):
                        n = [0]

                        def link(ins):
                            n[0] += 1
                            ins.then_inc(chain, 1)
                            dve.wait_ge(chain, n[0])

                        def over_experts(t):
                            return t.rearrange("p (b a) -> p b a", a=1).to_broadcast([T, B, E])

                        on_vector(dve)
                        for b in range(B):
                            dve.tensor_scalar(XG[:, b, 0:C], H[:, b, :], MV[:, b, 0:1], RS[:, b:b + 1], ALU.subtract, ALU.mult).then_inc(xn_ready, 1)
                        dve.wait_ge(l_in_psum, 1)
                        link(dve.tensor_tensor(LG[:], bank[0][0:T, 0:B * E].rearrange("p (b e) -> p b e", e=E),
                                               BR[:].rearrange("p (a e) -> p a e", a=1).to_broadcast([T, B, E]), ALU.add))
                        for b in range(B):
                            ins = dve.max(M8[:, b, :], LG[:, b, :])
                        link(ins)
                        second = M8[:, :, 1:2].to_broadcast([T, B, E])
                        dve.tensor_tensor(EX[:], LG[:], M8[:, :, 0:1].to_broadcast([T, B, E]), ALU.subtract).then_inc(shifted, 1)
                        dve.tensor_tensor(KEEPB[:].rearrange("p e b -> p b e"), LG[:], second, ALU.is_ge)
                        link(dve.tensor_tensor(KEEP[:], LG[:], second, ALU.is_ge))
                        dve.wait_ge(gate_exp, 1)
                        link(dve.tensor_tensor(EX[:], EX[:], KEEP[:], ALU.mult))
                        link(dve.tensor_reduce(SM[:], EX[:], AX.X, ALU.add))
                        link(dve.reciprocal(SM[:], SM[:]))
                        dve.tensor_tensor(XG[:, :, C:C + E], EX[:], over_experts(SM[:]), ALU.mult).then_inc(gates_made, 1)
                        dve.wait_ge(gates_made, 1)

                    @block.tensor
                    def _(pe):
                        def transpose_x(g):
                            pe.wait_ge(xn_ready, g * GB + GB)
                            if g >= 2:
                                pe.wait_ge(xnT_ready, (g - 1) * KT)
                            for k in range(KT):
                                for j in range(GB):
                                    mm = pe.transpose(bank[4 + 2 * (g % 2) + k][:, j * T:j * T + T], XG[:, g * GB + j, k * 128:k * 128 + 128], ID[0:T, 0:T])
                                mm.then_inc(xnT_in_psum, 1)

                        def route(g):
                            pe.wait_ge(xnT_ready, g * KT + KT)
                            for j in range(GB):
                                b = g * GB + j
                                for k in range(KT):
                                    mm = pe.matmul(bank[0][0:T, b * E:b * E + E], XT3[:, g % 2, k, j * T:j * T + T], WR[:, k, :], start=k == 0, stop=k == KT - 1)
                            if g == G - 1:
                                mm.then_inc(l_in_psum, 1)

                        pe.wait_ge(ld, 32)
                        transpose_x(0)
                        for g in range(G):
                            if g + 1 < G:
                                transpose_x(g + 1)
                            route(g)

            with ExitStack() as p3b:
                def psb(name, shape, dt=F32):
                    return p3b.enter_context(nc.sbuf_tensor(name, shape, dt))
                TRI = psb("before", [T, T], BF16)
                ONES = psb("ones_bf", [T, 128], BF16)
                CN = psb("count", [T, E * B])
                INC = psb("count_incl", [T, E * B])
                P1 = psb("place", [T, E * B])
                GE = psb("place_ge", [T, E * B, NBLK + 1], BF16)
                HI = psb("place_block", [T, E * B])
                LO = psb("place_lane", [T, E * B])
                OH = psb("block_onehot", [T, E * B, 3, NBLK], BF16)
                OL = psb("lane_onehot", [T, 2, B, 128], BF16)
                LS = psb("slot_sums", [128, E, 3, NBLK])
                IDF = psb("slot_token", [128, E, NBLK])
                PF = psb("slot_pad", [128, E, NBLK])
                NGE = psb("block_used", [1, E, NBLK])
                TF = psb("counts_f", [1, 3 * E])
                chain, count_in_psum, lane_made, list_in_psum = sem("list_chain"), sem("count_psum"), sem("lane_made"), sem("list_psum")
                with nc.Block() as block:
                    @block.tensor
                    def _(pe):
                        pe.wait_ge(chain, 2)
                        keep = KEEPB[:].rearrange("p e b -> p (e b)")
                        pe.matmul(bank[0][0:T, 0:E * B], TRI[:], keep, start=True, stop=True)
                        pe.matmul(bank[1][:, 0:E * B], ONES[:], keep, start=True, stop=True).then_inc(count_in_psum, 1)
                        for e in range(E):
                            pe.wait_ge(lane_made, e + 1)
                            for b in range(B):
                                mm = pe.matmul(bank[2][:, e * 3 * NBLK:(e + 1) * 3 * NBLK], OL[:, e % 2, b, :],
                                               OH[:, e * B + b].rearrange("p k j -> p (k j)"), start=b == 0, stop=b == B - 1)
                            mm.then_inc(list_in_psum, 1)

                    @block.vector
                    def _(dve):
                        n = [0]

                        def link(ins):
                            n[0] += 1
                            ins.then_inc(chain, 1)
                            dve.wait_ge(chain, n[0])

                        def last(t, k):
                            return t.rearrange("p (n a) -> p n a", a=1).to_broadcast([t.shape[0], t.shape[1], k])

                        def mid(t, k):
                            return t.rearrange("p (a n) -> p a n", a=1).to_broadcast([t.shape[0], k, t.shape[1]])

                        link(dve.tensor_copy(TRI[:], tri[0:T]))
                        link(dve.memset(ONES[:], 1.0))
                        dve.wait_ge(count_in_psum, 1)
                        link(dve.tensor_copy(CN[:], bank[1][0:T, 0:E * B]))
                        link(dve.tensor_tensor_scan(INC[:], reset[0:T], CN[:], 0.0, ALU.mult, ALU.add))
                        link(dve.tensor_tensor(P1[:], bank[0][0:T, 0:E * B], CN[:], ALU.subtract))
                        link(dve.tensor_tensor(P1[:], P1[:], INC[:], ALU.add))
                        link(dve.scalar_tensor_tensor(out=P1[:], in0=P1[:], scalar=1.0, in1=KEEPB[:].rearrange("p e b -> p (e b)"), op0=ALU.add, op1=ALU.mult))
                        link(dve.tensor_tensor(GE[:], last(P1[:], NBLK + 1), mid(thr[0:T], E * B), ALU.is_ge))
                        link(dve.tensor_reduce(HI[:], GE[:, :, 1:NBLK + 1], AX.X, ALU.add))
                        link(dve.scalar_tensor_tensor(out=LO[:], in0=HI[:], scalar=-128.0, in1=P1[:], op0=ALU.mult, op1=ALU.add))
                        link(dve.tensor_tensor(OH[:, :, 0, :], GE[:, :, 0:NBLK], GE[:, :, 1:NBLK + 1], ALU.subtract))
                        link(dve.tensor_scalar(OH[:, :, 1, :], OH[:, :, 0, :], pidx[0:T], None, ALU.mult))
                        link(dve.tensor_tensor(OH[:, :, 2, :], OH[:, :, 0, :], last(bidx[0:T], NBLK), ALU.mult))
                        for e in range(E):
                            if e >= 2:
                                dve.wait_ge(list_in_psum, e - 1)
                            dve.tensor_tensor(OL[:, e % 2], mid(iota1[0:T], B), last(LO[:, e * B:e * B + B], 128), ALU.is_equal).then_inc(lane_made, 1)
                        tokens, ahead, upto = TF[:, 0:E], TF[:, E:2 * E], TF[:, 2 * E:]
                        link(dve.tensor_copy(tokens, INC[0:1, B - 1::B]))
                        link(dve.tensor_tensor(NGE[:], last(tokens, NBLK), mid(thr[0:1, 0:NBLK], E), ALU.is_ge))
                        link(dve.tensor_reduce(ahead, NGE[:], AX.X, ALU.add))
                        link(dve.tensor_tensor_scan(upto, reset[0:1, 1:1 + E], ahead, 0.0, ALU.mult, ALU.add))
                        link(dve.tensor_tensor(ahead, upto, ahead, ALU.subtract))
                        link(dve.tensor_copy(TB[:], TF[:]))
                        dve.wait_ge(list_in_psum, E)
                        link(dve.tensor_copy(LS[:].rearrange("p e k j -> p (e k j)"), bank[2][:, 0:E * 3 * NBLK]))
                        link(dve.scalar_tensor_tensor(out=IDF[:], in0=LS[:, :, 2, :], scalar=float(T), in1=LS[:, :, 1, :], op0=ALU.mult, op1=ALU.add))
                        link(dve.tensor_scalar(PF[:], LS[:, :, 0, :], negpad, pad, ALU.mult, ALU.add))
                        link(dve.tensor_tensor(IDX[:], IDF[:], PF[:], ALU.add))

            with ExitStack() as p3c:
                def psb(name, shape, dt=F32):
                    return p3c.enter_context(nc.sbuf_tensor(name, shape, dt))
                IF = psb("token_by_block", [128, (E + 1) * NBLK + 1], I32)
                IG = psb("gather_tokens", [128, 1], I32)
                IS = psb("scatter_tokens", [128, 1], I32)
                GX = psb("gathered", [128, ROW])
                GXT = psb("gathered_T", [128, KT, 128])
                GN = psb("weights_next", [128, E])
                GC = psb("weights_now", [128, E])
                HB = psb("hidden", [128, HT, 128])
                YB = psb("expert_out", [128, C])
                YW = psb("weighted", [128, C])
                (table_made, idx_copied, gathered, weight_copied, weight_moved, xT_in_psum, xT_ready, hid_in_psum, hid_ready, y_in_psum, y_moved, y_scaled, scattered, st_made) = (
                    sem(f"moe_{n}") for n in ("table_made", "idx_copied", "gathered", "weight_copied", "weight_moved", "xT_psum", "xT", "hid_psum", "hid", "y_psum", "y_moved", "y_scaled", "scattered", "stats_made"))
                h_back = [sem(f"h_back{g}") for g in range(G)]

                def blocks(eng, body):
                    with eng.Fori(0, E // 2) as p:
                        for s in range(2):
                            e = p * 2 + s
                            tokens = eng.value_load(TB[0:1, bass.ds(e, 1)], min_val=0, max_val=B * T)
                            ahead = eng.value_load(TB[0:1, bass.ds(e + E, 1)], min_val=0, max_val=E * NBLK)
                            with eng.Fori(0, NBLK // RUN) as r:
                                with eng.If(tokens > r * (RUN * 128)):
                                    with eng.Fori(0, RUN) as i:
                                        with eng.If(tokens > r * (RUN * 128) + i * 128):
                                            body(ahead + r * RUN + i, e, s, p)

                with nc.Block() as block:
                    @block.sync
                    def _(sp):
                        with sp.Fori(1, E // 2) as p:
                            for s in range(2):
                                done = sp.value_load(TB[0:1, bass.ds(p * 2 + s + 2 * E - 2, 1)], min_val=0, max_val=E * NBLK)
                                after(sp, y_moved, done + 1)
                                sp.wait_ge(wld[s], p * EXPERT_LOADED)
                                load_expert(sp, p * 2 + s, s)
                        total = sp.value_load(TB[0:1, 3 * E - 1:3 * E], min_val=1, max_val=E * NBLK)
                        sp.wait_ge(scattered, total * 16 + 16)
                        for g in range(G):
                            sp.dma_start(H[:, g * GB:g * GB + GB, :], h_rows[g * GT:g * GT + GT, :].rearrange("(b t) c -> t b c", t=T)).then_inc(h_back[g], 16)

                    @block.gpsimd
                    def _(pool):
                        def gather(made):
                            after(pool, idx_copied, made)
                            pool.indirect_dma_start(GX[:], None, x_rows, bass.IndirectOffsetOnAxis(ap=IG[:], axis=0)).then_inc(gathered, 16)

                        def add_rows(n, made):
                            after(pool, idx_copied, made)
                            after(pool, y_scaled, n + 1)
                            pool.indirect_dma_start(h_rows, bass.IndirectOffsetOnAxis(ap=IS[:], axis=0), YW[:], None, compute_op=ALU.add).then_inc(scattered, 16)

                        pool.wait_ge(table_made, 1 + E)
                        pool.wait_ge(rows_stored, 4 * 16)
                        pool.tensor_copy(IS[:], RC[:, RAT[3]:RAT[3] + 1]).then_inc(idx_copied, 1)
                        add_rows(0, 1)
                        pool.tensor_copy(IG[:], IF[:, 0:1]).then_inc(idx_copied, 1)
                        gather(2)

                        def body(u, e, s, p):
                            pool.wait_ge(gathered, u * 16 + 16)
                            pool.wait_ge(xT_in_psum, u + 1)
                            after(pool, weight_copied, u + 1)
                            pool.tensor_copy(IG[:], IF[:, bass.ds(u + 1, 1)]).then_inc(idx_copied, 1)
                            gather(u * 2 + 3)
                            after(pool, scattered, u * 16 + 16)
                            pool.tensor_copy(IS[:], IF[:, bass.ds(u, 1)]).then_inc(idx_copied, 1)
                            add_rows(u + 1, u * 2 + 4)

                        blocks(pool, body)

                    @block.scalar
                    def _(act):
                        act.sem_inc(hid_ready, GB)

                        def move_xT(n):
                            act.wait_ge(xT_in_psum, n + 1)
                            act.activation(GXT[:].rearrange("p k t -> p (k t)"), bank[4][:, 0:KT * 128], ACT.Copy).then_inc(xT_ready, 1)

                        move_xT(0)

                        def body(u, e, s, p):
                            act.wait_ge(wld[s], (p + 1) * EXPERT_LOADED)
                            for i in range(HT):
                                act.wait_ge(hid_in_psum, u * HT + i + 1)
                                at = 128 * (i // 4)
                                act.activation(HB[:, i, :], bank[i % 4][:, at:at + 128], ACT.Gelu, bias=B1[:, s, i:i + 1]).then_inc(hid_ready, 1)
                            move_xT(u + 1)
                        blocks(act, body)

                    @block.vector
                    def _(dve):
                        dve.sem_inc(y_moved, 1)
                        dve.memset(YW[:], 0.0).then_inc(y_scaled, 1)
                        dve.tensor_scalar(IF[:], IDX[:, 0, 0:1].to_broadcast([128, (E + 1) * NBLK + 1]), 0.0, pad, ALU.mult, ALU.add).then_inc(table_made, 1)
                        for e in range(E):
                            ahead = dve.value_load(TB[0:1, E + e:E + e + 1], min_val=0, max_val=(E - 1) * NBLK)
                            dve.wait_ge(table_made, e + 1)
                            dve.tensor_copy(IF[:, bass.ds(ahead, NBLK)], IDX[:, e, :]).then_inc(table_made, 1)

                        def take_weights(n):
                            dve.wait_ge(gathered, n * 16 + 16)
                            dve.tensor_copy(GN[:], GX[:, C:C + E]).then_inc(weight_copied, 1)

                        take_weights(0)
                        dve.wait_ge(weight_copied, 1)
                        dve.tensor_copy(GC[:], GN[:]).then_inc(weight_moved, 1)

                        def body(u, e, s, p):
                            dve.wait_ge(weight_moved, u + 1)
                            take_weights(u + 1)
                            dve.wait_ge(scattered, u * 16 + 16)
                            dve.wait_ge(wld[s], (p + 1) * EXPERT_LOADED)
                            dve.wait_ge(y_in_psum, u + 2)
                            wge = GC[:, bass.ds(e, 1)]
                            dve.tensor_tensor(YB[:], bank[5][:, 0:C], B2[:, s, :], ALU.add).then_inc(y_moved, 1)
                            dve.wait_ge(y_moved, u + 2)
                            dve.tensor_scalar(YW[:], YB[:], wge, None, ALU.mult).then_inc(y_scaled, 1)
                            dve.wait_ge(weight_copied, u + 2)
                            dve.wait_ge(y_scaled, u + 2)
                            dve.tensor_copy(GC[:], GN[:]).then_inc(weight_moved, 1)
                        blocks(dve, body)
                        for g in range(G):
                            dve.wait_ge(h_back[g], 16)
                            for b in range(g * GB, g * GB + GB):
                                dve.bn_stats(ST[:, b, :], H[:, b, :]).then_inc(st_made, 1)
                        dve.wait_ge(st_made, B)

                    @block.tensor
                    def _(pe):
                        pe.sem_inc(y_in_psum, 1)

                        def transpose_rows(n):
                            pe.wait_ge(gathered, n * 16 + 16)
                            for k in range(KT):
                                mm = pe.transpose(bank[4][:, k * 128:k * 128 + 128], GX[:, k * 128:k * 128 + 128], ID[:, :])
                            mm.then_inc(xT_in_psum, 1)

                        transpose_rows(0)

                        def body(u, e, s, p):
                            pe.wait_ge(wld[s], (p + 1) * EXPERT_LOADED)
                            pe.wait_ge(xT_ready, u + 1)
                            for i in range(HT):
                                pe.wait_ge(hid_ready, u * HT + i + 1)
                                at = 128 * (i // 4)
                                for k in range(KT):
                                    mm = pe.matmul(bank[i % 4][:, at:at + 128], W1[:, s, k, i * 128:i * 128 + 128], GXT[:, k, :], start=k == 0, stop=k == KT - 1)
                                mm.then_inc(hid_in_psum, 1)
                            pe.wait_ge(y_scaled, u + 1)
                            for i in range(HT):
                                if i == HT // 2:
                                    transpose_rows(u + 1)
                                pe.wait_ge(hid_ready, u * HT + i + 1 + GB)
                                mm = pe.matmul(bank[5][:, 0:C], HB[:, i, :], W2[:, s, i, :], start=i == 0, stop=i == HT - 1)
                            mm.then_inc(y_in_psum, 1)
                        blocks(pe, body)

        with ExitStack() as p4:
            def psb(name, shape, dt=F32):
                return p4.enter_context(nc.sbuf_tensor(name, shape, dt))
            HB_ = B // 2
            AW = psb("tssa_w", [128, KT, C])
            OW = psb("out_w", [128, KT, C])
            OB = psb("out_b", [T, C])
            TM = psb("temp", [T, NH])
            HO = psb("head_of", [128, KT, NH])
            HTO = psb("head_to", [NH, KT, 128])
            XN4 = psb("tssa_x", [T, 2, GB, C])
            XT4 = psb("tssa_x_T", [128, 2, KT, GT])
            WT = psb("w_T", [128, KT, B, T])
            WSQ = psb("w_sq_T", [128, KT, B, T])
            NS = psb("norm_sq", [128, KT, B])
            RI = psb("head_of_scaled", [128, KT, B, NH])
            SC = psb("tssa_score", [T, B, NH])
            SX = psb("tssa_max", [T, B])
            PI = psb("pi", [T, B, NH])
            PIT = psb("pi_T", [NH, B, T])
            PIE = psb("pi_by_channel", [128, KT, B, T])
            PIW = psb("pi_w", [128, KT, B, T])
            PWW = psb("pi_w_sq", [128, 2, KT, GB, T])
            DOT = psb("dots", [128, KT, B])
            SPI = psb("pi_sum", [128, KT, B])
            OT = psb("tssa_out_T", [128, KT, B, T])
            ld = sem("tssa_loaded")
            xn_ready, xnT_in_psum, xnT_ready = sem("t_xn"), sem("t_xnT_psum"), sem("t_xnT")
            w_in_psum, w_ready, chain, norms_made = sem("w_psum"), sem("w_ready"), sem("tssa_chain"), sem("norms_made")
            s_in_psum, s_shifted, pi_exp, pi_made = sem("ts_psum"), sem("ts_shifted"), sem("pi_exp"), sem("pi_made")
            piT_in_psum, piT_ready, pie_in_psum, pie_ready, piw_made = sem("piT_psum"), sem("piT"), sem("pie_psum"), sem("pie"), sem("piw")
            oT_made, o_in_psum, h_added, bias_added, st_made = sem("oT"), sem("to_psum"), sem("t_h_added"), sem("t_bias"), sem("t_stats_made")
            on_vector, on_scalar = finish_norm("ln3")

            def four(t, g):
                return t[:, :, g * GB:g * GB + GB, :]

            with nc.Block() as block:
                @block.sync
                def _(sp):
                    for dst, src in ((AW, tssa_w), (OW, out_w), (OB, out_b), (TM, temp), (HO, head_of), (HTO, head_to)):
                        sp.dma_start(dst[:], src).then_inc(ld, 16)

                @block.gpsimd
                def _(pool):
                    pool.wait_ge(ld, 96)
                    for g in range(G):
                        pool.wait_ge(xn_ready, g * GB + GB)
                        hs = H[:, g * GB:g * GB + GB, :]
                        pool.tensor_tensor(hs, hs, OB[:].rearrange("p (a c) -> p a c", a=1).to_broadcast([T, GB, C]), ALU.add).then_inc(bias_added, 1)
                    for g in range(G):
                        pool.wait_ge(pie_ready, g + 1)
                        pool.tensor_tensor(four(PIW, g), four(PIE, g), four(WT, g), ALU.mult).then_inc(piw_made, 1)

                @block.scalar
                def _(act):
                    on_scalar(act)

                    def project(g):
                        for k in range(KT):
                            act.wait_ge(w_in_psum, g * KT + k + 1)
                            w = bank[2 * (g % 2) + k][:, 0:GT].rearrange("p (b t) -> p b t", t=T)
                            act.activation(four(WSQ, g)[:, k], w, ACT.Square)
                            ins = act.activation(four(WT, g)[:, k], w, ACT.Copy)
                        ins.then_inc(w_ready, 1)

                    def move_xT(g):
                        for k in range(KT):
                            act.wait_ge(xnT_in_psum, g * KT + k + 1)
                            act.activation(XT4[:, g % 2, k, :], bank[4 + k][:, 0:GT], ACT.Copy).then_inc(xnT_ready, 1)

                    def exp_half(h):
                        act.wait_ge(s_shifted, h + 1)
                        act.activation(PI[:, h * HB_:h * HB_ + HB_, :], SC[:, h * HB_:h * HB_ + HB_, :], ACT.Exp).then_inc(pi_exp, 1)

                    def move_piT(g):
                        act.wait_ge(piT_in_psum, g + 1)
                        act.activation(PIT[:, g * GB:g * GB + GB, :], bank[4 + g % 2][0:NH, 0:GT].rearrange("p (b t) -> p b t", t=T), ACT.Copy).then_inc(piT_ready, 1)

                    def spread(g):
                        act.wait_ge(pie_in_psum, g + 1)
                        for k in range(KT):
                            for j in range(GB):
                                b = g * GB + j
                                ins = act.activation(PIE[:, k, b, :], bank[2 * (g % 2) + k][:, j * T:j * T + T], ACT.Copy, accum_out=SPI[:, k, b:b + 1])
                        ins.then_inc(pie_ready, 1)

                    for g in range(G):
                        if g == G - 1:
                            move_xT(g)
                            exp_half(0)
                            project(g)
                        else:
                            move_xT(g)
                            project(g)
                    move_piT(0)
                    move_piT(1)
                    exp_half(1)
                    spread(0)
                    spread(1)
                    move_piT(2)
                    move_piT(3)
                    spread(2)
                    spread(3)

                @block.vector
                def _(dve):
                    on_vector(dve)
                    n = [0]

                    def link(ins):
                        n[0] += 1
                        ins.then_inc(chain, 1)
                        dve.wait_ge(chain, n[0])

                    def half(t, h):
                        return t[..., h * HB_:h * HB_ + HB_]

                    def norm_x(g):
                        if g >= 2:
                            dve.wait_ge(xnT_in_psum, (g - 1) * KT)
                        for j in range(GB):
                            b = g * GB + j
                            dve.tensor_scalar(XN4[:, g % 2, j, :], H[:, b, :], MV[:, b, 0:1], RS[:, b:b + 1],
                                              ALU.subtract, ALU.mult).then_inc(xn_ready, 1)

                    def sum_squares(g):
                        dve.wait_ge(w_ready, g + 1)
                        link(dve.tensor_reduce(NS[:, :, g * GB:g * GB + GB], four(WSQ, g), AX.X, ALU.add))

                    def scale_heads(h):
                        ns = half(NS[:], h)
                        link(dve.tensor_scalar(ns, ns, 1e-24, None, ALU.max))
                        link(dve.reciprocal(ns, ns))
                        for k in range(KT):
                            ins = dve.tensor_tensor(RI[:, k, h * HB_:h * HB_ + HB_, :], HO[:, k:k + 1, :].to_broadcast([128, HB_, NH]),
                                                    ns[:, k].rearrange("p (b a) -> p b a", a=1).to_broadcast([128, HB_, NH]), ALU.mult)
                        ins.then_inc(norms_made, 1)

                    def over_heads(h):
                        return SX[:, h * HB_:h * HB_ + HB_].rearrange("p (b a) -> p b a", a=1).to_broadcast([T, HB_, NH])

                    def shift_scores(h):
                        sc = SC[:, h * HB_:h * HB_ + HB_, :]
                        dve.wait_ge(s_in_psum, h + 1)
                        link(dve.tensor_tensor(sc, bank[6 + h][0:T, 0:HB_ * NH].rearrange("p (b h) -> p b h", b=HB_),
                                               TM[:].rearrange("p (a h) -> p a h", a=1).to_broadcast([T, HB_, NH]), ALU.mult))
                        link(dve.tensor_reduce(SX[:, h * HB_:h * HB_ + HB_], sc, AX.X, ALU.max))
                        dve.tensor_tensor(sc, sc, over_heads(h), ALU.subtract).then_inc(s_shifted, 1)

                    def finish_pi(h):
                        pi = PI[:, h * HB_:h * HB_ + HB_, :]
                        dve.wait_ge(pi_exp, h + 1)
                        link(dve.tensor_reduce(SX[:, h * HB_:h * HB_ + HB_], pi, AX.X, ALU.add))
                        link(dve.reciprocal(SX[:, h * HB_:h * HB_ + HB_], SX[:, h * HB_:h * HB_ + HB_]))
                        dve.tensor_tensor(pi, pi, over_heads(h), ALU.mult).then_inc(pi_made, 1)

                    def sum_dots(g):
                        dve.wait_ge(piw_made, g + 1)
                        link(dve.tensor_tensor(PWW[:, g % 2], four(PIW, g), four(WT, g), ALU.mult))
                        link(dve.tensor_reduce(DOT[:, :, g * GB:g * GB + GB], PWW[:, g % 2], AX.X, ALU.add))

                    def attend(g):
                        at = slice(g * GB, g * GB + GB)
                        sp_, dot = SPI[:, :, at], DOT[:, :, at]
                        link(dve.tensor_scalar(sp_, sp_, 1e-8, None, ALU.add))
                        link(dve.reciprocal(sp_, sp_))
                        link(dve.tensor_tensor(dot, dot, sp_, ALU.mult))
                        link(dve.tensor_scalar(dot, dot, 1.0, None, ALU.add))
                        link(dve.reciprocal(dot, dot))
                        for k in range(KT):
                            ins = dve.scalar_tensor_tensor(out=OT[:, k, at, :], in0=PIW[:, k, at, :], scalar=-1.0,
                                                           in1=DOT[:, k, at].rearrange("p (b a) -> p b a", a=1).to_broadcast([128, GB, T]),
                                                           op0=ALU.mult, op1=ALU.mult)
                        ins.then_inc(oT_made, 1)

                    def add_to_h(g):
                        dve.wait_ge(bias_added, g + 1)
                        for b in range(g * GB, g * GB + GB):
                            dve.wait_ge(o_in_psum, b + 1)
                            dve.tensor_tensor(H[:, b, :], bank[4 + b % 4][0:T, 0:C], H[:, b, :], ALU.add).then_inc(h_added, 1)
                        for b in range(g * GB, g * GB + GB):
                            dve.wait_ge(h_added, b + 1)
                            dve.bn_stats(ST[:, b, :], H[:, b, :]).then_inc(st_made, 1)

                    norm_x(0)
                    norm_x(1)
                    dve.wait_ge(ld, 96)
                    sum_squares(0)
                    norm_x(2)
                    sum_squares(1)
                    scale_heads(0)
                    norm_x(3)
                    shift_scores(0)
                    sum_squares(2)
                    finish_pi(0)
                    sum_squares(3)
                    scale_heads(1)
                    shift_scores(1)
                    finish_pi(1)
                    for g in range(G):
                        sum_dots(g)
                        attend(g)
                        if g:
                            add_to_h(g - 1)
                    add_to_h(G - 1)
                    dve.wait_ge(st_made, B)

                @block.tensor
                def _(pe):
                    pe.wait_ge(ld, 96)

                    def project(g):
                        if g:
                            pe.wait_ge(xnT_ready, g * KT)
                        pe.wait_ge(xn_ready, g * GB + GB)
                        for k in range(KT):
                            for b in range(GB):
                                mm = pe.transpose(bank[4 + k][:, b * T:b * T + T], XN4[:, g % 2, b, k * 128:k * 128 + 128], ID[0:T, 0:T])
                            mm.then_inc(xnT_in_psum, 1)
                        pe.wait_ge(xnT_ready, g * KT + KT)
                        if g >= 2:
                            pe.wait_ge(w_ready, g - 1)
                        for o in range(KT):
                            for k in range(KT):
                                mm = pe.matmul(bank[2 * (g % 2) + o][:, 0:GT], AW[:, k, o * 128:o * 128 + 128], XT4[:, g % 2, k, :], start=k == 0, stop=k == KT - 1)
                            mm.then_inc(w_in_psum, 1)

                    def scores(h):
                        pe.wait_ge(norms_made, h + 1)
                        for b in range(h * HB_, h * HB_ + HB_):
                            j = b - h * HB_
                            for k in range(KT):
                                mm = pe.matmul(bank[6 + h][0:T, j * NH:j * NH + NH], WSQ[:, k, b, :], RI[:, k, b, :], start=k == 0, stop=k == KT - 1)
                        mm.then_inc(s_in_psum, 1)

                    def transpose_pi(h):
                        pe.wait_ge(pi_made, h + 1)
                        for g in (2 * h, 2 * h + 1):
                            if h:
                                pe.wait_ge(piT_ready, g - 1)
                            for b in range(GB):
                                mm = pe.transpose(bank[4 + g % 2][0:NH, b * T:b * T + T], PI[:, g * GB + b, :], ID[0:T, 0:T])
                            mm.then_inc(piT_in_psum, 1)

                    def spread(g):
                        pe.wait_ge(piT_ready, g + 1)
                        if g >= 2:
                            pe.wait_ge(pie_ready, g - 1)
                        for k in range(KT):
                            mm = pe.matmul(bank[2 * (g % 2) + k][:, 0:GT], HTO[:, k, :], PIT[:, g * GB:g * GB + GB, :].rearrange("p b t -> p (b t)"), start=True, stop=True)
                        mm.then_inc(pie_in_psum, 1)

                    project(0)
                    project(1)
                    project(2)
                    scores(0)
                    project(3)
                    transpose_pi(0)
                    pe.wait_ge(w_ready, G)
                    spread(0)
                    spread(1)
                    scores(1)
                    transpose_pi(1)
                    spread(2)
                    spread(3)
                    for b in range(B):
                        pe.wait_ge(oT_made, b // GB + 1)
                        if b >= 4:
                            pe.wait_ge(h_added, b - 3)
                        else:
                            pe.wait_ge(piT_ready, G)
                            pe.wait_ge(s_shifted, 2)
                        for k in range(KT):
                            mm = pe.matmul(bank[4 + b % 4][0:T, 0:C], OT[:, k, b, :], OW[:, k, :], start=k == 0, stop=k == KT - 1)
                        mm.then_inc(o_in_psum, 1)

        with ExitStack() as p5:
            def psb(name, shape, dt=F32):
                return p5.enter_context(nc.sbuf_tensor(name, shape, dt))
            CC = psb("conv_col", [128, KT, 2])
            CM = psb("conv_mask", [128, KT, 64])
            CWT = psb("conv_w", [128, KT, 128])
            CB = psb("conv_b", [128, 1])
            GA = psb("gamma", [128, 1])
            BE = psb("beta", [128, 1])
            LW = psb("lin_w", [128, C])
            LB = psb("lin_b", [1, 2 * C])
            FW = psb("ffn_w", [128, KT, C])
            FB = psb("ffn_bias", [T, C])
            XC = psb("gate_pre", [128, B * T])
            XA = psb("gate_act", [128, B * T])
            FU = psb("full", [T, B, C])
            X4 = psb("x_kept", [T, B, C])
            CST = psb("bn_stats", [128, G, 6])
            CMV = psb("bn_mean_var", [128, 2])
            CS = psb("bn_scale_bias", [128, 4])
            ld = sem("ffn_loaded")
            xn_ready, xnT_in_psum, xnT_ready = sem("f_xn"), sem("f_xnT_psum"), sem("f_xnT")
            cw_made, xc_in_psum, xc_ready, full_in_psum, full_ready = (sem(n) for n in ("cw_made", "xc_psum", "xc", "full_psum", "full_ready"))
            x_kept = sem("x_kept")
            cst_made, bn_made, bn_sd, xa_ready = sem("cst_made"), sem("bn_made"), sem("bn_sd"), sem("xa_ready")
            on_vector, on_scalar = finish_norm("ln4")
            with nc.Block() as block:
                @block.sync
                def _(sp):
                    for dst, src in ((CC, conv_col), (CM, conv_mask), (CB, conv_b), (GA, gamma), (BE, beta), (LW, lin_w), (LB, lin_b), (FW, ffn_w), (FB, ffn_bias)):
                        sp.dma_start(dst[:], src).then_inc(ld, 16)

                @block.gpsimd
                def _(pool):
                    pool.wait_ge(ld, 144)
                    for k in range(KT):
                        for br_ in range(2):
                            pool.tensor_scalar(CWT[:, k, 64 * br_:64 * br_ + 64], CM[:, k, :], CC[:, k, br_:br_ + 1], None, ALU.mult).then_inc(cw_made, 1)
                    with pool.Fori(0, G) as g:
                        after(pool, xn_ready, g * GB + GB)
                        pool.tensor_copy(X4[:, bass.ds(g * GB, GB), :], XN[:]).then_inc(x_kept, 1)
                        hs = H[:, bass.ds(g * GB, GB), :]
                        pool.tensor_tensor(hs, hs, FB[:].rearrange("p (a c) -> p a c", a=1).to_broadcast([T, GB, C]), ALU.add).then_inc(x_kept, 1)
                    pool.wait_ge(x_kept, 2 * G)

                @block.scalar
                def _(act):
                    on_scalar(act)
                    act.wait_ge(ld, 144)
                    act.sem_inc(full_ready, 2)
                    with act.Fori(0, G) as g:
                        for k in range(KT):
                            act.wait_ge(xnT_in_psum, g * KT + k + 1)
                            act.activation(XT[:, k, :], bank[4 + k][:, 0:GT], ACT.Copy).then_inc(xnT_ready, 1)
                        act.wait_ge(xc_in_psum, g + 1)
                        act.activation(XC[:, bass.ds(g * GT, GT)], bank[0][:, 0:GT], ACT.Identity, bias=CB[:]).then_inc(xc_ready, 1)
                        for j in range(GB):
                            act.wait_ge(full_in_psum, g * GB + j + 1)
                            act.activation(row(FU, g * GB + j), bank[2 + j % 2][0:T, 0:C], ACT.Copy).then_inc(full_ready, 1)
                    act.wait_ge(bn_made, 1)
                    act.activation(CS[:, 0:1], CMV[:, 1:2], ACT.Sqrt, bias=EP[:]).then_inc(bn_sd, 1)
                    act.wait_ge(bn_made, 5)
                    act.activation(XA[:], XC[:], ACT.Gelu, bias=CS[:, 3:4], scale=CS[:, 2:3]).then_inc(xa_ready, 1)

                @block.vector
                def _(dve):
                    on_vector(dve)
                    with dve.Fori(0, G) as g:
                        normalise(dve, g, xn_ready)
                        dve.wait_ge(xc_ready, g + 1)
                        dve.bn_stats(CST[:, bass.ds(g, 1), :].rearrange("p a c -> p (a c)"), XC[:, bass.ds(g * GT, GT)]).then_inc(cst_made, 1)
                        dve.wait_ge(xnT_ready, g * KT + KT)
                        dve.wait_ge(x_kept, g * 2 + 2)
                    dve.wait_ge(cst_made, G)
                    dve.bn_aggr(CMV[:], CST[:]).then_inc(bn_made, 1)
                    dve.wait_ge(bn_sd, 1)
                    dve.reciprocal(CS[:, 1:2], CS[:, 0:1]).then_inc(bn_made, 1)
                    dve.wait_ge(bn_made, 2)
                    dve.tensor_tensor(CS[:, 2:3], CS[:, 1:2], GA[:], ALU.mult).then_inc(bn_made, 1)
                    dve.wait_ge(bn_made, 3)
                    dve.tensor_tensor(CS[:, 3:4], CS[:, 2:3], CMV[:, 0:1], ALU.mult).then_inc(bn_made, 1)
                    dve.wait_ge(bn_made, 4)
                    dve.tensor_tensor(CS[:, 3:4], BE[:], CS[:, 3:4], ALU.subtract).then_inc(bn_made, 1)

                @block.tensor
                def _(pe):
                    pe.wait_ge(ld, 144)
                    pe.wait_ge(cw_made, 4)
                    with pe.Fori(0, G) as g:
                        pe.wait_ge(xn_ready, g * GB + GB)
                        for k in range(KT):
                            for b in range(GB):
                                mm = pe.transpose(bank[4 + k][:, b * T:b * T + T], XN[:, b, k * 128:k * 128 + 128], ID[0:T, 0:T])
                            mm.then_inc(xnT_in_psum, 1)
                        pe.wait_ge(xnT_ready, g * KT + KT)
                        for k in range(KT):
                            mm = pe.matmul(bank[0][:, 0:GT], CWT[:, k, :], XT[:, k, :], start=k == 0, stop=k == KT - 1)
                        mm.then_inc(xc_in_psum, 1)
                        for b in range(GB):
                            pe.wait_ge(full_ready, g * GB + b + 1)
                            for k in range(KT):
                                mm = pe.matmul(bank[2 + b % 2][0:T, 0:C], XT[:, k, b * T:b * T + T], FW[:, k, :], start=k == 0, stop=k == KT - 1)
                            mm.then_inc(full_in_psum, 1)

            XAB = psb("gate_act_step", [128, 2, T])
            M8 = psb("top8", [T, 2, 2, 8])
            NM = psb("neg_max", [T, 2, 2])
            EE = psb("score_exp", [T, 2, 2, C])
            E8 = psb("top8_exp", [T, 2, 2, 8])
            REM = psb("score_rest", [T, 2, 2, C])
            TOP = psb("score_top", [T, 2, 2, C])
            SS = psb("score_sum", [T, 2, 2])
            RSS = psb("score_sum_recip", [T, 2, 2])
            XS = psb("x_sparse", [T, 2, C])
            OS = psb("out_sparse", [T, 2, C])
            XST = psb("x_sparse_T", [128, 2, KT, T])
            OO = psb("out_tile", [T, 2, C])
            xab, l_in_psum, m8, ee, top, picked, scaled, xs_ready, os_ready, xsT_in_psum, xsT, in_psum, oo = (
                sem(n) for n in ("xab", "ffn_l_psum", "m8", "ee", "topk", "picked", "scaled", "xs", "os", "xsT_psum", "xsT", "in_psum", "oo"))
            stored = [sem(f"stored{s}") for s in range(2)]
            NT = 4 * (TOPK // 8) - 1

            def made(b):
                return b + 3

            def freed(b):
                return b + 1

            def pipeline(eng, tasks):
                first = -min(offset for offset, _ in tasks)
                pairs = (B - max(offset for offset, _ in tasks) - first) // 2

                def step(k, parity):
                    for offset, task in tasks:
                        if not isinstance(k, int) or 0 <= k + offset < B:
                            task(k + offset, (parity + offset) % 2)

                for k in range(-2, first):
                    step(k, k % 2)
                with eng.Fori(0, pairs) as i:
                    for s in range(2):
                        step(i * 2 + s + first, (s + first) % 2)
                for k in range(first + 2 * pairs, B + 2):
                    step(k, k % 2)

            with nc.Block() as block:
                @block.gpsimd
                def _(pool):
                    def copy_gate(b, s):
                        if not (isinstance(b, int) and b < 2):
                            after(pool, l_in_psum, b - 1)
                        pool.tensor_copy(XAB[:, s, :], XA[:, bass.ds(b * T, T)]).then_inc(xab, 1)

                    def pick(b, s):
                        after(pool, top, b * NT + NT)
                        after(pool, os_ready, freed(b))
                        pool.tensor_tensor(TOP[:, s], EE[:, s], REM[:, s], ALU.subtract).then_inc(picked, 1)

                    def weigh(b, s):
                        after(pool, xsT_in_psum, freed(b))
                        after(pool, scaled, b + 1)
                        pool.tensor_tensor(XS[:, s, :], TOP[:, s, 1, :], row(X4, b), ALU.mult).then_inc(xs_ready, 1)
                        after(pool, in_psum, freed(b))
                        pool.tensor_tensor(OS[:, s, :], TOP[:, s, 0, :], row(FU, b), ALU.mult).then_inc(os_ready, 1)

                    pipeline(pool, ((2, copy_gate), (-1, pick), (-1, weigh)))

                @block.scalar
                def _(act):
                    def scale(b, s):
                        act.wait_ge(picked, b + 1)
                        for r in range(2):
                            ins = act.activation(TOP[:, s, r, :], TOP[:, s, r, :], ACT.Copy, scale=RSS[:, s, r:r + 1])
                        ins.then_inc(scaled, 1)

                    def exp_scores(b, s):
                        if not (isinstance(b, int) and b < 2):
                            act.wait_ge(picked, b - 1)
                        act.wait_ge(m8, b * 2 + 2)
                        for r in range(2):
                            act.activation(EE[:, s, r, :], bank[2 * s + r][0:T, 0:C], ACT.Exp, bias=NM[:, s, r:r + 1],
                                           accum_out=SS[:, s, r:r + 1])
                            ins = act.activation(E8[:, s, r, :], M8[:, s, r, :], ACT.Exp, bias=NM[:, s, r:r + 1])
                        ins.then_inc(ee, 1)

                    def move(b, s):
                        act.wait_ge(in_psum, freed(b))
                        act.wait_ge(xsT_in_psum, made(b))
                        act.activation(XST[:, s], bank[4 + s][:, 0:KT * T].rearrange("p (k t) -> p k t", k=KT), ACT.Copy).then_inc(xsT, 1)

                    def store(b, s):
                        act.wait_ge(stored[s], (b - s) * 8 + 16)
                        act.wait_ge(in_psum, made(b))
                        act.activation(OO[:, s, :], bank[6 + s][0:T, 0:C], ACT.Copy).then_inc(oo, 1)

                    pipeline(act, ((-1, scale), (1, exp_scores), (-2, store), (-1, move)))

                @block.vector
                def _(dve):
                    for two in (xsT_in_psum, xsT, in_psum, os_ready, oo):
                        dve.sem_inc(two, 2)

                    def row_max(b, s):
                        after(dve, l_in_psum, b + 1)
                        for r in range(2):
                            ins = dve.max(M8[:, s, r, :], bank[2 * s + r][0:T, 0:C])
                        ins.then_inc(m8, 1)
                        dve.wait_ge(m8, b * 2 + 1)
                        dve.tensor_scalar(NM[:, s, :], M8[:, s, :, 0], -1.0, None, ALU.mult).then_inc(m8, 1)

                    def search(b, s):
                        after(dve, ee, b + 1)
                        dve.reciprocal(RSS[:, s, :], SS[:, s, :]).then_inc(top, 1)
                        n = 1
                        for rnd in range(TOPK // 8):
                            if rnd:
                                for r in range(2):
                                    after(dve, top, b * NT + n - 1)
                                    dve.max(E8[:, s, r, :], REM[:, s, r, :]).then_inc(top, 1)
                                    n += 1
                            for r in range(2):
                                if rnd:
                                    after(dve, top, b * NT + n - 1)
                                src = EE if rnd == 0 else REM
                                dve.match_replace(REM[:, s, r, :], E8[:, s, r, :], src[:, s, r, :], 0.0).then_inc(top, 1)
                                n += 1
                        assert n == NT, n

                    pipeline(dve, ((1, row_max), (0, search)))

                @block.sync
                def _(sp):
                    for s in range(2):
                        sp.sem_inc(stored[s], 16)
                    with sp.Fori(0, B // 2) as i:
                        for s in range(2):
                            sp.wait_ge(oo, made(i * 2 + s))
                            sp.dma_start(out[bass.ds(i * 2 + s, 1)].rearrange("b t c -> t (b c)"), OO[:, s, :]).then_inc(stored[s], 16)
                    for s in range(2):
                        sp.wait_ge(stored[s], 16 * (B // 2) + 16)

                @block.tensor
                def _(pe):
                    def logits(b, s):
                        if not (isinstance(b, int) and b < 2):
                            pe.wait_ge(ee, b - 1)
                        pe.wait_ge(xab, b + 1)
                        for r in range(2):
                            pe.matmul(bank[2 * s + r][0:T, 0:C], ONE[:, 0:T], LB[:, r * C:r * C + C], start=True, stop=False)
                        for r in range(2):
                            mm = pe.matmul(bank[2 * s + r][0:T, 0:C], XAB[64 * r:64 * r + 64, s, :], LW[64 * r:64 * r + 64, :], start=False, stop=True)
                        mm.then_inc(l_in_psum, 1)

                    def in_branch(b, s):
                        pe.wait_ge(xsT, freed(b))
                        pe.wait_ge(xs_ready, b + 1)
                        for k in range(KT):
                            mm = pe.transpose(bank[4 + s][:, k * T:k * T + T], XS[:, s, k * 128:k * 128 + 128], ID[0:T, 0:T])
                        mm.then_inc(xsT_in_psum, 1)
                        pe.wait_ge(oo, freed(b))
                        pe.matmul(bank[6 + s][0:T, 0:C], ID[0:T, 0:T], row(H, b), start=True, stop=False)
                        pe.wait_ge(os_ready, made(b))
                        pe.matmul(bank[6 + s][0:T, 0:C], ID[0:T, 0:T], OS[:, s, :], start=False, stop=False)
                        pe.wait_ge(xsT, made(b))
                        for k in range(KT):
                            mm = pe.matmul(bank[6 + s][0:T, 0:C], XST[:, s, k, :], FW[:, k, :], start=False, stop=k == KT - 1)
                        mm.then_inc(in_psum, 1)

                    pipeline(pe, ((2, logits), (-1, in_branch)))


def _layout(i):
    import numpy as np
    f = np.float32
    a = {k: np.asarray(v) for k, v in i.items()}
    o = {}
    p = a["x"].reshape(B, 3, 6, 16, 6, 16).transpose(1, 3, 5, 0, 2, 4).reshape(768, B, NP)
    pt = np.zeros((768, B // 2, 2, 64), f)
    pt[:, :, :, 1:1 + NP] = p.reshape(768, B // 2, 2, NP)
    o["patches"] = pt.reshape(PK, 128, G, GB // 2, 128).transpose(2, 1, 3, 0, 4)
    hb = np.zeros((B, T, C), f)
    hb[:, 0] = a["L0_tok_cls_token"][0]
    hb[:, 1:1 + NP] = a["L0_tok_b"]
    hb[:, 1 + NP:] = a["txt"]
    o["h_base"] = hb.transpose(1, 0, 2)
    kt = lambda w: w.reshape(-1, 128, w.shape[-1]).transpose(1, 0, 2)
    o["tok_w"] = kt(a["L0_tok_W"])
    w = a["L0_attn_Wqkv"].reshape(C, 3, NH, HD)
    bb = a["L0_attn_bqkv"].reshape(3, NH, HD)
    z = np.zeros_like(w[:, 0])
    o["wkv"] = kt(np.concatenate([w[:, 1], w[:, 2]], -1).reshape(C, -1))
    o["wq"] = kt(np.concatenate([w[:, 0], z], -1).reshape(C, -1))
    o["bkv"] = np.tile(np.concatenate([bb[1], bb[2]], -1).T, (GB, 1))
    o["bq"] = np.tile(np.concatenate([bb[0], np.zeros_like(bb[0])], -1).T, (GB, 1))
    o["wproj"] = kt(a["L0_attn_Wproj"])
    rep = lambda v: np.tile(v.reshape(1, -1), (T, 1))
    o["br"] = rep(a["L0_ffn_br"])
    o["bproj"] = rep(a["L0_attn_bproj"])
    m = np.where(np.arange(T)[None, :] <= np.arange(T)[:, None], 0.0, NEG)
    o["mask4"] = np.tile(m, (1, HQ)).astype(f)
    o["ident"] = np.eye(128, dtype=f)
    o["w1"] = a["L0_ffn_W1"].reshape(E, KT, 128, HID).transpose(0, 2, 1, 3)
    o["b1"] = a["L0_ffn_b1"].reshape(E, HT, 128).transpose(0, 2, 1)
    o["w2"] = a["L0_ffn_W2"].reshape(E, HT, 128, C).transpose(0, 2, 1, 3)
    o["b2"] = a["L0_ffn_b2"]
    o["wr"] = kt(a["L0_ffn_Wr"])
    lane = np.arange(128.0)
    parts = [np.tile(lane + 1, (128, 1)), np.tile(128.0 * np.arange(NBLK + 1) + 1, (128, 1)), lane[:, None],
             B * T + lane[:, None], -B * T - lane[:, None], np.tile(np.arange(float(B)), (128, E)),
             np.tile(np.arange(B) > 0, (128, E)), lane[:, None] < np.arange(T)]
    o["route_consts"] = np.concatenate([v.astype(f) for v in parts], 1)
    o["tssa_w"] = kt(a["L1_attn_qkv_w"].T)
    o["temp"] = rep(a["L1_attn_temp"])
    ho = np.repeat(np.eye(NH, dtype=f), HD, axis=0)
    o["head_of"] = kt(ho)
    o["head_to"] = ho.T.reshape(NH, KT, 128)
    o["out_w"] = kt(a["L1_attn_out_w"].T)
    o["out_b"] = rep(a["L1_attn_out_b"])
    cc = np.stack([a["L1_ffn_so_conv_w"].reshape(-1), a["L1_ffn_si_conv_w"].reshape(-1)], -1)
    o["conv_col"] = kt(cc)
    o["conv_mask"] = kt(np.repeat(np.eye(64, dtype=f), 4, axis=0))
    both = lambda n: np.concatenate([a[f"L1_ffn_so_{n}"], a[f"L1_ffn_si_{n}"]]).reshape(-1, 1)
    o["conv_b"], o["gamma"], o["beta"] = both("conv_b"), both("gamma"), both("beta")
    o["lin_w"] = np.concatenate([a["L1_ffn_so_lin_w"].T, a["L1_ffn_si_lin_w"].T])
    o["lin_b"] = both("lin_b").reshape(1, -1)
    o["ffn_w"] = kt(a["L1_ffn_weight"])
    o["ffn_bias"] = rep(a["L1_ffn_bias"])
    return {k: np.ascontiguousarray(v) for k, v in o.items()}


def kernel(**inputs):
    import concourse.bacc as _bacc
    from concourse import mybir as _mybir
    from concourse.bass_utils import run_bass_kernel_spmd as _run

    nc = _bacc.Bacc("TRN2", target_bir_lowering=False, num_devices=1)
    arrays = _layout(inputs)
    args = {k: nc.dram_tensor(f"in_{k}", v.shape, _mybir.dt.from_np(v.dtype), kind="ExternalInput").ap() for k, v in arrays.items()}
    args["out"] = nc.dram_tensor("out", (B, T, C), F32, kind="ExternalOutput").ap()
    early_fusion(nc, **args)
    arrays = {f"in_{k}": v for k, v in arrays.items()}
    return _run(nc, [arrays], core_ids=[0]).results[0]["out"]
```

```python
from contextlib import ExitStack, nullcontext

import concourse.bass as bass
from concourse import mybir

F32 = mybir.dt.float32
BF16 = mybir.dt.bfloat16
ALU = mybir.AluOpType
ACT = mybir.ActivationFunctionType
AX = mybir.AxisListType

B = 16
T = 114
NP = 36
C = 256
KT = C // 128
PK = 768 // 128
GB = 4
G = B // GB
GT = GB * T
NH, HD = 16, 16
HQ = 4
NQ = NH // HQ
E = 8
HID = 1024
HT = HID // 128
EPS = 1e-5
TOPK = 32
NEG = -1.0e30
I32 = mybir.dt.int32
NBLK = -(-B * T // 128)
STRETCHES = ((0, 4), (4, 8), (8, NBLK))
ROW = C + E
RAT = [0]
for _w in (128, NBLK + 1, 1, 1, 1, E * B, E * B, T):
    RAT.append(RAT[-1] + _w)
RCOLS = RAT[-1]


def early_fusion(nc: bass.Bass, patches, h_base, tok_w, wkv, wq, bkv, bq, wproj, bproj, mask4, ident,
                 w1, b1, w2, b2, wr, br, route_consts, tssa_w, temp, head_of, head_to, out_w, out_b,
                 conv_col, conv_mask, conv_b, gamma, beta, lin_w, lin_b, ffn_w, ffn_bias, out):
    with ExitStack() as ctx:
        def sb(name, shape, dt=F32):
            return ctx.enter_context(nc.sbuf_tensor(name, shape, dt))

        def sem(name):
            return ctx.enter_context(nc.semaphore(name))

        bank = [ctx.enter_context(nc.psum_tensor(f"bank{i}", [128, 512], F32)) for i in range(8)]

        x_rows = nc.dram_tensor("x_rows", (B * T + 128, ROW), F32, kind="Internal").ap()
        h_rows = nc.dram_tensor("h_rows", (B * T + 128, C), F32, kind="Internal").ap()

        H = sb("h", [T, B, C])
        ID = sb("identity", [128, 128])
        EP = sb("eps", [128, 1])
        ONE = sb("ones_row", [1, 128])
        ST = sb("ln_stats", [T, B, 6])
        MV = sb("ln_mean_var", [T, B, 2])
        SD = sb("ln_std", [T, B])
        RS = sb("ln_rstd", [T, B])

        h_loaded = sem("h_loaded")
        consts_loaded = sem("consts_loaded")
        const_set = sem("const_set")
        waited = sem("waited")

        def finish_norm(stage):
            stats_made, std_made, aggregated = (sem(f"{stage}_{n}") for n in ("stats", "std", "aggr"))

            def on_vector(dve):
                for b in range(B):
                    ins = dve.bn_aggr(MV[:, b, :], ST[:, b, :])
                ins.then_inc(aggregated, 1)
                dve.wait_ge(std_made, 1)
                dve.reciprocal(RS[:, :], SD[:, :]).then_inc(stats_made, 1)
                dve.wait_ge(stats_made, 1)

            def on_scalar(act):
                act.wait_ge(aggregated, 1)
                act.activation(SD[:, :], MV[:, :, 1], ACT.Sqrt, bias=EP[0:T, :]).then_inc(std_made, 1)
            return on_vector, on_scalar

        with ExitStack() as p1:
            PT = p1.enter_context(nc.sbuf_tensor("patches_T", [128, G, GB // 2, PK, 128], F32))
            TW = p1.enter_context(nc.sbuf_tensor("tok_w", [128, PK, C], F32))
            patches_loaded, tok_w_loaded = [sem(f"patches_loaded{g}") for g in range(G)], [sem(f"tok_w_loaded{k}") for k in range(PK)]
            tok_in_psum, tok_added = sem("tok_in_psum"), sem("tok_added")
            with nc.Block() as block:
                @block.sync
                def _(sp):
                    for k in range(PK):
                        sp.dma_start(TW[:, k, :], tok_w[:, k, :]).then_inc(tok_w_loaded[k], 16)
                        sp.dma_start(PT[:, 0, :, k, :], patches[0][:, :, k, :]).then_inc(tok_w_loaded[k], 16)
                    for g in range(1, G):
                        sp.dma_start(PT[:, g], patches[g]).then_inc(patches_loaded[g], 16)
                        if g == 1:
                            sp.dma_start(H[:], h_base).then_inc(h_loaded, 16)
                    sp.dma_start(ID[:], ident).then_inc(consts_loaded, 16)

                @block.tensor
                def _(pe):
                    for g in range(G):
                        if g:
                            pe.wait_ge(patches_loaded[g], 16)
                        if g >= 2:
                            pe.wait_ge(tok_added, (g - 1) * GB)
                        for k in range(PK):
                            if g == 0:
                                pe.wait_ge(tok_w_loaded[k], 32)
                            for q in range(2):
                                mm = pe.matmul(bank[2 * (g % 2) + q][:, 0:C], PT[:, g, q, k, :], TW[:, k, :], start=k == 0, stop=k == PK - 1)
                        mm.then_inc(tok_in_psum, 1)

                @block.vector
                def _(dve):
                    dve.memset(EP[:], EPS).then_inc(const_set, 1)
                    dve.memset(ONE[:], 1.0).then_inc(const_set, 1)
                    dve.wait_ge(h_loaded, 16)
                    for g in range(G):
                        dve.wait_ge(tok_in_psum, g + 1)
                        for j in range(GB):
                            rows = H[0:NP + 1, g * GB + j, :]
                            at = 64 * (j % 2)
                            dve.tensor_tensor(rows, bank[2 * (g % 2) + j // 2][at:at + NP + 1, 0:C], rows, ALU.add).then_inc(tok_added, 1)
                        for b in range(g * GB, g * GB + GB):
                            dve.wait_ge(tok_added, b + 1)
                            dve.bn_stats(ST[:, b, :], H[:, b, :]).then_inc(const_set, 1)
                    dve.wait_ge(const_set, B + 2)

        def after(eng, signal, value):
            eng.wait_ge(signal, value)
            eng.sem_inc(waited, 1)

        def row(t, b):
            return t[:, bass.ds(b, 1), :].rearrange("p a c -> p (a c)")

        with ExitStack() as p2:
            def psb(name, shape, dt=F32):
                return p2.enter_context(nc.sbuf_tensor(name, shape, dt))
            WKV = psb("wkv", [128, KT, NH * 32])
            WQ = psb("wq", [128, KT, NH * 32])
            BKV = psb("bkv", [128, NH])
            BQ = psb("bq", [128, NH])
            WP = psb("wproj", [128, KT, C])
            BP = psb("bproj", [T, C])
            MF = psb("mask4_f", [T, GT])
            MK = psb("mask4", [T, GT], BF16)
            IB = psb("identity_bf", [128, 128], BF16)
            KV = psb("kv_T", [128, T * NH])
            Q = psb("q_T", [128, T * NH])
            KVA = psb("kv_T_all", [128, G, T * NH])
            QA = psb("q_T_all", [128, G, T * NH])
            VS = psb("v_rows", [T, NH, GB, 32])
            attn_w_loaded = sem("attn_w_loaded")
            v_frame_set, mask_made = sem("v_frame_set"), sem("mask_made")
            xn_ready, xnT_in_psum, xnT_ready = sem("a_xn"), sem("a_xnT_psum"), sem("a_xnT")
            kv_in_psum, q_in_psum, kv_made, q_made = sem("kv_psum"), sem("q_psum"), sem("kv_made"), sem("q_made")
            bias_added = sem("bproj_added")
            q_copied, kv_copied = sem("q_copied"), sem("kv_copied")
            on_vector, on_scalar = finish_norm("ln1")
            n_loads = 7

            with ExitStack() as p2a:
                XN2 = p2a.enter_context(nc.sbuf_tensor("attn_x", [T, 2, GB, C], F32))
                XTA = p2a.enter_context(nc.sbuf_tensor("attn_x_T", [128, KT, GB, G, T], F32))
                with nc.Block() as block:
                    @block.sync
                    def _(sp):
                        for dst, src in ((WKV, wkv), (WQ, wq), (BKV, bkv), (BQ, bq), (WP, wproj), (BP, bproj), (MF, mask4)):
                            sp.dma_start(dst[:], src).then_inc(attn_w_loaded, 16)

                    @block.gpsimd
                    def _(pool):
                        pool.memset(VS[:, :, :, HD:32], 0.0).then_inc(v_frame_set, 1)
                        pool.wait_ge(v_frame_set, 1)
                        pool.memset(VS[:, :, :, HD:HD + 1], 1.0).then_inc(v_frame_set, 1)
                        pool.wait_ge(attn_w_loaded, 16 * n_loads)
                        for g in range(G):
                            pool.wait_ge(xn_ready, g * GB + GB)
                            hs = H[:, g * GB:g * GB + GB, :]
                            pool.tensor_tensor(hs, hs, BP[:].rearrange("p (a c) -> p a c", a=1).to_broadcast([T, GB, C]), ALU.add).then_inc(bias_added, 1)
                        pool.wait_ge(bias_added, G)
                        pool.wait_ge(v_frame_set, 2)

                    @block.scalar
                    def _(act):
                        on_scalar(act)
                        for g in range(G):
                            for k in range(KT):
                                act.wait_ge(xnT_in_psum, g * KT + k + 1)
                                act.activation(XTA[:, k, :, g, :], bank[4 + 2 * (g % 2) + k][:, 0:GT].rearrange("p (b t) -> p b t", t=T), ACT.Copy).then_inc(xnT_ready, 1)
                        act.wait_ge(attn_w_loaded, 16 * n_loads)
                        for c in range(NH):
                            act.wait_ge(kv_in_psum, c + 1)
                            act.activation(KVA[:].rearrange("p g (t c) -> p g t c", c=NH)[:, :, :, c], bank[c % 2][:, 0:GT].rearrange("p (g t) -> p g t", t=T),
                                           ACT.Identity, bias=BKV[:, c:c + 1]).then_inc(kv_made, 1)
                        act.wait_ge(kv_made, NH)
                        act.activation(KV[:], KVA[:, 0, :], ACT.Copy).then_inc(kv_copied, 1)
                        act.wait_ge(kv_copied, 1)

                    @block.vector
                    def _(dve):
                        on_vector(dve)
                        for g in range(G):
                            if g >= 2:
                                dve.wait_ge(xnT_in_psum, (g - 1) * KT)
                            for j in range(GB):
                                b = g * GB + j
                                dve.tensor_scalar(XN2[:, g % 2, j, :], H[:, b, :], MV[:, b, 0:1], RS[:, b:b + 1], ALU.subtract, ALU.mult).then_inc(xn_ready, 1)
                        dve.wait_ge(attn_w_loaded, 16 * n_loads)
                        dve.wait_ge(consts_loaded, 16)
                        dve.tensor_copy(IB[:], ID[:])
                        dve.tensor_copy(MK[:], MF[:]).then_inc(mask_made, 1)
                        for c in range(NH):
                            dve.wait_ge(q_in_psum, c + 1)
                            dve.tensor_scalar(QA[:].rearrange("p g (t c) -> p g t c", c=NH)[:, :, :, c], bank[2 + c % 2][:, 0:GT].rearrange("p (g t) -> p g t", t=T),
                                              BQ[:, c:c + 1], None, ALU.add).then_inc(q_made, 1)
                        dve.wait_ge(q_made, NH)
                        dve.tensor_copy(Q[:], QA[:, 0, :]).then_inc(q_copied, 1)
                        dve.wait_ge(q_copied, 1)
                        dve.wait_ge(mask_made, 1)

                    @block.tensor
                    def _(pe):
                        pe.wait_ge(consts_loaded, 16)
                        for g in range(G):
                            pe.wait_ge(xn_ready, g * GB + GB)
                            if g >= 2:
                                pe.wait_ge(xnT_ready, (g - 1) * KT)
                            for k in range(KT):
                                for b in range(GB):
                                    mm = pe.transpose(bank[4 + 2 * (g % 2) + k][:, b * T:b * T + T], XN2[:, g % 2, b, k * 128:k * 128 + 128], ID[0:T, 0:T])
                                mm.then_inc(xnT_in_psum, 1)
                        pe.wait_ge(attn_w_loaded, 16 * n_loads)
                        pe.wait_ge(xnT_ready, G * KT)
                        for c in range(NH):
                            for w, first, in_psum, emptied in ((WKV, 0, kv_in_psum, kv_made), (WQ, 2, q_in_psum, q_made)):
                                if c >= 2:
                                    pe.wait_ge(emptied, c - 1)
                                for k in range(KT):
                                    for j in range(GB):
                                        mm = pe.matmul(bank[first + c % 2][32 * j:32 * j + 32, 0:GT], w[:, k, c * 32:c * 32 + 32],
                                                       XTA[:, k, j].rearrange("p g t -> p (g t)"), start=k == 0, stop=k == KT - 1)
                                mm.then_inc(in_psum, 1)

            PR = psb("probs", [T, 2, GB, GT])
            PTR = psb("probs_T", [T, 2, GB, GT])
            MX = psb("row_max", [T, GB, HQ])
            YT = psb("y_T", [128, 2, GT])
            RD = psb("row_sum_recip", [T, HQ, GB])
            YN = psb("y_normed", [T, GB, C])
            YNT = psb("y_normed_T", [128, KT, GT])
            vT_in_psum, v_ready = sem("vT_psum"), sem("v_ready")
            s_in_psum, s_shifted, max_made, p_ready = sem("s_psum"), sem("s_shifted"), sem("max_made"), sem("p_ready")
            pT_in_psum, pT_ready = sem("pT_psum"), sem("pT")
            y_in_psum, yT_ready, yrow_in_psum, y_normed, rd_made = (sem(n) for n in ("y_psum", "yT", "yrow_psum", "y_normed", "rd_made"))
            ynT_in_psum, ynT_ready, proj_in_psum, h_added, st_made = (sem(n) for n in ("ynT_psum", "ynT", "proj_psum", "h_added", "a_stats_made"))

            def groups(eng, body):
                body(0, False)
                with eng.Fori(1, G) as g:
                    body(g, True)

            with nc.Block() as block:
                @block.gpsimd
                def _(pool):
                    with pool.Fori(1, G) as g:
                        after(pool, s_in_psum, g * 16)
                        pool.tensor_copy(Q[:], QA[:, bass.ds(g, 1), :].rearrange("p a n -> p (a n)")).then_inc(q_copied, 1)
                        pool.tensor_copy(KV[:], KVA[:, bass.ds(g, 1), :].rearrange("p a n -> p (a n)")).then_inc(kv_copied, 1)

                @block.scalar
                def _(act):
                    def exp_scores(g, q, b):
                        act.wait_ge(s_shifted, g * 16 + 4 * q + b + 1)
                        act.activation(PR[:, q % 2, b, :], PR[:, q % 2, b, :], ACT.Exp, scale=HD ** -0.5).then_inc(p_ready, 1)

                    def move_probs(g, q, b):
                        n = 4 * q + b
                        act.wait_ge(pT_in_psum, g * 16 + n + 1)
                        act.activation(PTR[:, q % 2, b, :], bank[4 + n % 2][0:T, 0:GT], ACT.Copy).then_inc(pT_ready, 1)

                    def move_y(g, q):
                        act.wait_ge(y_in_psum, g * NQ + q + 1)
                        act.activation(YT[:, q % 2, :], bank[6][:, 0:GT], ACT.Copy).then_inc(yT_ready, 1)

                    def move_normed(g):
                        for k in range(KT):
                            act.wait_ge(ynT_in_psum, g * KT + k + 1)
                            act.activation(YNT[:, k, :], bank[6 + k][:, 0:GT], ACT.Copy).then_inc(ynT_ready, 1)

                    def body(g, late):
                        for q in range(NQ):
                            exp_scores(g, 0, q)
                            act.wait_ge(vT_in_psum, g * NQ + q + 1)
                            act.activation(VS[:, HQ * q:HQ * q + HQ, :, 0:HD],
                                           bank[4 + q % 2][0:T, :].rearrange("p (h b d) -> p h b d", h=HQ, b=GB)[:, :, :, HD:2 * HD],
                                           ACT.Copy).then_inc(v_ready, 1)
                        if late:
                            move_normed(g - 1)
                        for q in range(NQ):
                            for b in range(GB):
                                move_probs(g, q, b)
                                if q + 1 < NQ:
                                    exp_scores(g, q + 1, b)
                            move_y(g, q)

                    groups(act, body)
                    move_normed(G - 1)

                @block.vector
                def _(dve):
                    def shift_scores(g, q, b):
                        n = g * 16 + 4 * q + b + 1
                        dve.wait_ge(s_in_psum, n)
                        s = bank[b][0:T, 0:GT].rearrange("p (h s) -> p h s", h=HQ)
                        dve.tensor_reduce(MX[:, b, :], s, AX.X, ALU.max).then_inc(max_made, 1)
                        if q >= 2:
                            dve.wait_ge(pT_in_psum, g * 16 + 4 * (q - 2) + b + 1)
                        dve.wait_ge(max_made, n)
                        dve.tensor_tensor(PR[:, q % 2, b, :].rearrange("p (h s) -> p h s", h=HQ), s,
                                          MX[:, b, :].rearrange("p (h a) -> p h a", a=1).to_broadcast([T, HQ, T]),
                                          ALU.subtract).then_inc(s_shifted, 1)

                    def norm_y(g, q):
                        dve.wait_ge(yrow_in_psum, g * NQ + q + 1)
                        y = bank[7][0:T, :].rearrange("p (h b d) -> p h b d", h=HQ, b=GB)
                        dve.reciprocal(RD[:], y[:, :, :, HD]).then_inc(rd_made, 1)
                        dve.wait_ge(rd_made, g * NQ + q + 1)
                        dve.tensor_tensor(YN[:].rearrange("p b (h d) -> p h b d", d=HD)[:, HQ * q:HQ * q + HQ],
                                          y[:, :, :, 0:HD],
                                          RD[:].rearrange("p h (b a) -> p h b a", a=1).to_broadcast([T, HQ, GB, HD]),
                                          ALU.mult).then_inc(y_normed, 1)

                    def add_to_h(g):
                        for j in range(GB):
                            b = g * GB + j
                            dve.wait_ge(proj_in_psum, g * 2 + j // 2 + 1)
                            dve.tensor_tensor(row(H, b), bank[6 + j // 2][0:T, (j % 2) * C:(j % 2) * C + C], row(H, b), ALU.add).then_inc(h_added, 1)
                            dve.wait_ge(h_added, g * GB + j + 1)
                            dve.bn_stats(row(ST, b), row(H, b)).then_inc(st_made, 1)

                    def body(g, late):
                        for q in range(NQ):
                            if q == 3:
                                norm_y(g, 0)
                            for b in range(GB):
                                shift_scores(g, q, b)
                            if late and q == 0:
                                norm_y(g - 1, NQ - 1)
                            if late and q == 1:
                                add_to_h(g - 1)
                        norm_y(g, 1)
                        norm_y(g, 2)

                    groups(dve, body)
                    norm_y(G - 1, NQ - 1)
                    add_to_h(G - 1)
                    dve.wait_ge(st_made, B)

                @block.tensor
                def _(pe):
                    def scores(g, q):
                        for b in range(GB):
                            if q or not isinstance(g, int):
                                pe.wait_ge(s_shifted, g * 16 + 4 * q - 3 + b)
                            pe.matmul(bank[b][0:T, 0:GT], IB[0:T, 0:T], MK[:, :], start=True, stop=False, skip_group_check=True)
                        for h in range(HQ):
                            r = (HQ * q + h) * T
                            for b in range(GB):
                                mm = pe.matmul(bank[b][0:T, h * T:h * T + T], Q[32 * b:32 * b + HD, r:r + T],
                                               KV[32 * b:32 * b + HD, r:r + T], start=False, stop=True, skip_group_check=True)
                                if h == HQ - 1:
                                    mm.then_inc(s_in_psum, 1)

                    def transpose_v(g, late):
                        for q in range(NQ):
                            if q >= 2:
                                pe.wait_ge(v_ready, g * NQ + q - 1)
                            elif late:
                                pe.wait_ge(pT_ready, g * 16)
                            for h in range(HQ):
                                r = (HQ * q + h) * T
                                mm = pe.transpose(bank[4 + q % 2][0:T, h * 128:h * 128 + 128], KV[:, r:r + T], ID[:, :])
                            mm.then_inc(vT_in_psum, 1)

                    def transpose_probs(g, q):
                        for b in range(GB):
                            n = 4 * q + b
                            if n >= 2:
                                pe.wait_ge(pT_ready, g * 16 + n - 1)
                            else:
                                pe.wait_ge(v_ready, g * NQ + NQ)
                            pe.wait_ge(p_ready, g * 16 + n + 1)
                            for h in range(HQ):
                                mm = pe.transpose(bank[4 + n % 2][0:T, h * T:h * T + T], PR[:, q % 2, b, h * T:h * T + T], ID[0:T, 0:T])
                            mm.then_inc(pT_in_psum, 1)

                    def apply_probs(g, q, late):
                        pe.wait_ge(pT_ready, g * 16 + 4 * q + 4)
                        if q:
                            pe.wait_ge(yT_ready, g * NQ + q)
                        elif late:
                            pe.wait_ge(h_added, g * GB)
                        for h in range(HQ):
                            for b in range(GB):
                                mm = pe.matmul(bank[6][32 * b:32 * b + 32, h * T:h * T + T], VS[:, HQ * q + h, b, :],
                                               PTR[:, q % 2, b, h * T:h * T + T], start=True, stop=True)
                        mm.then_inc(y_in_psum, 1)

                    def y_rows(g, q):
                        pe.wait_ge(yT_ready, g * NQ + q + 1)
                        if q:
                            pe.wait_ge(y_normed, g * NQ + q)
                        for h in range(HQ):
                            mm = pe.transpose(bank[7][0:T, h * 128:h * 128 + 128], YT[:, q % 2, h * T:h * T + T], ID[:, :])
                        mm.then_inc(yrow_in_psum, 1)

                    def transpose_y(g):
                        pe.wait_ge(y_normed, g * NQ + NQ)
                        for k in range(KT):
                            for b in range(GB):
                                mm = pe.transpose(bank[6 + k][:, b * T:b * T + T], YN[:, b, k * 128:k * 128 + 128], ID[0:T, 0:T])
                            mm.then_inc(ynT_in_psum, 1)

                    def project(g):
                        pe.wait_ge(ynT_ready, g * KT + KT)
                        for b in range(GB):
                            for k in range(KT):
                                mm = pe.matmul(bank[6 + b // 2][0:T, (b % 2) * C:(b % 2) * C + C], YNT[:, k, b * T:b * T + T], WP[:, k, :], start=k == 0, stop=k == KT - 1)
                            if b % 2:
                                mm.then_inc(proj_in_psum, 1)

                    def body(g, late):
                        pe.wait_ge(q_copied, g + 1)
                        pe.wait_ge(kv_copied, g + 1)
                        scores(g, 0)
                        transpose_v(g, late)
                        if late:
                            y_rows(g - 1, NQ - 1)
                        scores(g, 1)
                        if late:
                            transpose_y(g - 1)
                        transpose_probs(g, 0)
                        if late:
                            project(g - 1)
                        scores(g, 2)
                        apply_probs(g, 0, late)
                        transpose_probs(g, 1)
                        y_rows(g, 0)
                        apply_probs(g, 1, late)
                        scores(g, 3)
                        for q in range(2, NQ):
                            transpose_probs(g, q)
                            y_rows(g, q - 1)
                            apply_probs(g, q, late)

                    groups(pe, body)
                    y_rows(G - 1, NQ - 1)
                    transpose_y(G - 1)
                    project(G - 1)

        with ExitStack() as p3:
            def psb(name, shape, dt=F32):
                return p3.enter_context(nc.sbuf_tensor(name, shape, dt))
            XG = psb("moe_rows", [T, B, ROW])
            KEEPB = psb("kept_bf", [T, E, B], BF16)
            W1 = psb("w1", [128, 2, KT, HID])
            W2 = psb("w2", [128, 2, HT, C])
            B1 = psb("b1", [128, 2, HT])
            RC = psb("route_consts", [128, RCOLS])
            IF = psb("token_by_block", [128, (E + 1) * NBLK + 1])
            TB = psb("expert_counts", [1, 3 * E], I32)
            iota1, thr, pidx, pad, negpad, bidx, reset, tri = (RC[:, a:b] for a, b in zip(RAT[:-1], RAT[1:]))
            B2 = psb("b2", [128, 2, C])
            ZR = psb("zero_rows", [128, ROW])
            wld = [sem(f"experts_loaded{i}") for i in range(2)]
            rows_stored = sem("rows_stored")
            h_back = [sem(f"h_back{g}") for g in range(G)]

            EXPERT_LOADED = 4 * 16

            def load_expert(sp, e, s):
                for dst, src in ((W1[:, s], w1), (W2[:, s], w2), (B1[:, s], b1)):
                    src = src[bass.ds(e, 1)]
                    src = src.rearrange("a p k n -> (a p) k n") if len(src.shape) == 4 else src.rearrange("a p k -> (a p) k")
                    sp.dma_start(dst, src).then_inc(wld[s], 16)
                sp.dma_start(B2[:, s, :], b2[bass.ds(e, 1), :].to_broadcast([128, C])).then_inc(wld[s], 16)

            with ExitStack() as p3a:
                def psb(name, shape, dt=F32):
                    return p3a.enter_context(nc.sbuf_tensor(name, shape, dt))
                WR = psb("wr", [128, KT, E])
                BR = psb("br", [T, E])
                XT3 = psb("moe_x_T", [128, 2, KT, GT])
                LG = psb("logits", [T, B, E])
                M8 = psb("logits_sorted", [T, B, E])
                KEEP = psb("kept", [T, B, E])
                EX = psb("gate_exp", [T, B, E])
                SM = psb("gate_sum", [T, B])
                ld, consts_in = sem("router_loaded"), sem("route_consts_loaded")
                xn_ready, xnT_in_psum, xnT_ready = sem("m_xn"), sem("m_xnT_psum"), sem("m_xnT")
                l_in_psum, chain, shifted, gate_exp, gates_made = sem("l_psum"), sem("gate_chain"), sem("logits_shifted"), sem("gate_exp_made"), sem("gates_made")
                zeros_set = sem("zeros_set")
                on_vector, on_scalar = finish_norm("ln2")
                with nc.Block() as block:
                    @block.sync
                    def _(sp):
                        for dst, src in ((WR, wr), (BR, br)):
                            sp.dma_start(dst[:], src).then_inc(ld, 16)
                        sp.dma_start(RC[:], route_consts).then_inc(consts_in, 16)
                        sp.dma_start(h_rows[0:B * T, :].rearrange("(b t) c -> t b c", t=T), H[:]).then_inc(rows_stored, 16)
                        sp.wait_ge(zeros_set, 1)
                        sp.dma_start(x_rows[B * T:, :], ZR[:]).then_inc(rows_stored, 16)
                        sp.dma_start(h_rows[B * T:, :], ZR[:, 0:C]).then_inc(rows_stored, 16)
                        load_expert(sp, 0, 0)
                        sp.wait_ge(consts_in, 16)

                    @block.gpsimd
                    def _(pool):
                        pool.memset(ZR[:], 0.0).then_inc(zeros_set, 1)

                    @block.scalar
                    def _(act):
                        on_scalar(act)
                        for g in range(G):
                            for k in range(KT):
                                act.wait_ge(xnT_in_psum, g * KT + k + 1)
                                act.activation(XT3[:, g % 2, k, :], bank[4 + 2 * (g % 2) + k][:, 0:GT], ACT.Copy).then_inc(xnT_ready, 1)
                        act.wait_ge(shifted, 1)
                        act.activation(EX[:], EX[:], ACT.Exp).then_inc(gate_exp, 1)

                    @block.vector
                    def _(dve):
                        n = [0]

                        def link(ins):
                            n[0] += 1
                            ins.then_inc(chain, 1)
                            dve.wait_ge(chain, n[0])

                        def over_experts(t):
                            return t.rearrange("p (b a) -> p b a", a=1).to_broadcast([T, B, E])

                        on_vector(dve)
                        for b in range(B):
                            dve.tensor_scalar(XG[:, b, 0:C], H[:, b, :], MV[:, b, 0:1], RS[:, b:b + 1], ALU.subtract, ALU.mult).then_inc(xn_ready, 1)
                        dve.wait_ge(l_in_psum, 1)
                        link(dve.tensor_tensor(LG[:], bank[0][0:T, 0:B * E].rearrange("p (b e) -> p b e", e=E),
                                               BR[:].rearrange("p (a e) -> p a e", a=1).to_broadcast([T, B, E]), ALU.add))
                        for b in range(B):
                            ins = dve.max(M8[:, b, :], LG[:, b, :])
                        link(ins)
                        second = M8[:, :, 1:2].to_broadcast([T, B, E])
                        dve.tensor_tensor(EX[:], LG[:], M8[:, :, 0:1].to_broadcast([T, B, E]), ALU.subtract).then_inc(shifted, 1)
                        dve.tensor_tensor(KEEPB[:].rearrange("p e b -> p b e"), LG[:], second, ALU.is_ge)
                        link(dve.tensor_tensor(KEEP[:], LG[:], second, ALU.is_ge))
                        dve.wait_ge(gate_exp, 1)
                        link(dve.tensor_tensor(EX[:], EX[:], KEEP[:], ALU.mult))
                        link(dve.tensor_reduce(SM[:], EX[:], AX.X, ALU.add))
                        link(dve.reciprocal(SM[:], SM[:]))
                        dve.tensor_tensor(XG[:, :, C:C + E], EX[:], over_experts(SM[:]), ALU.mult).then_inc(gates_made, 1)
                        dve.wait_ge(gates_made, 1)

                    @block.tensor
                    def _(pe):
                        def transpose_x(g):
                            pe.wait_ge(xn_ready, g * GB + GB)
                            if g >= 2:
                                pe.wait_ge(xnT_ready, (g - 1) * KT)
                            for k in range(KT):
                                for j in range(GB):
                                    mm = pe.transpose(bank[4 + 2 * (g % 2) + k][:, j * T:j * T + T], XG[:, g * GB + j, k * 128:k * 128 + 128], ID[0:T, 0:T])
                                mm.then_inc(xnT_in_psum, 1)

                        def route(g):
                            pe.wait_ge(xnT_ready, g * KT + KT)
                            for j in range(GB):
                                b = g * GB + j
                                for k in range(KT):
                                    mm = pe.matmul(bank[0][0:T, b * E:b * E + E], XT3[:, g % 2, k, j * T:j * T + T], WR[:, k, :], start=k == 0, stop=k == KT - 1)
                            if g == G - 1:
                                mm.then_inc(l_in_psum, 1)

                        pe.wait_ge(ld, 32)
                        transpose_x(0)
                        for g in range(G):
                            if g + 1 < G:
                                transpose_x(g + 1)
                            route(g)

            with ExitStack() as p3b:
                def psb(name, shape, dt=F32):
                    return p3b.enter_context(nc.sbuf_tensor(name, shape, dt))
                TRI = psb("before", [T, T], BF16)
                ONES = psb("ones_bf", [T, 128], BF16)
                CN = psb("count", [T, E * B])
                INC = psb("count_incl", [T, E * B])
                P1 = psb("place", [T, E * B])
                GE = psb("place_ge", [T, E * B, NBLK + 1], BF16)
                HI = psb("place_block", [T, E * B])
                LO = psb("place_lane", [T, E * B])
                OH = psb("block_onehot", [T, E * B, 3, NBLK], BF16)
                OL = psb("lane_onehot", [T, 3, B, 128], BF16)
                AL = psb("lane_distance", [T, B, 128], BF16)
                IDF = psb("slot_token", [128, E, NBLK])
                PF = psb("slot_pad", [128, E, NBLK])
                IDX = psb("token_of_slot", [128, E, NBLK])
                NGE = psb("block_used", [1, E, NBLK])
                TF = psb("counts_f", [1, 3 * E])
                chain, count_in_psum, lane_made, list_in_psum = sem("list_chain"), sem("count_psum"), sem("lane_made"), sem("list_psum")
                places_made, blocks_made, last_lanes, counts_made, idx_made, table_made = (
                    sem(f"list_{n}") for n in ("places", "block_onehots", "last_lanes", "counts", "idx", "table"))
                with nc.Block() as block:
                    @block.sync
                    def _(sp):
                        sp.dma_start(x_rows[0:B * T, :].rearrange("(b t) c -> t b c", t=T), XG[:]).then_inc(rows_stored, 16)
                        load_expert(sp, 1, 1)

                    @block.tensor
                    def _(pe):
                        pe.wait_ge(chain, 2)
                        keep = KEEPB[:].rearrange("p e b -> p (e b)")
                        pe.matmul(bank[0][0:T, 0:E * B], TRI[:], keep, start=True, stop=True)
                        pe.matmul(bank[1][:, 0:E * B], ONES[:], keep, start=True, stop=True).then_inc(count_in_psum, 1)
                        for e in range(E):
                            if e == 0:
                                pe.wait_ge(blocks_made, 2)
                            if e == E - 1:
                                pe.wait_ge(last_lanes, 2)
                            else:
                                pe.wait_ge(lane_made, e + 1)
                            for b in range(B):
                                mm = pe.matmul(bank[2][:, e * 3 * NBLK:(e + 1) * 3 * NBLK], OL[:, 2 if e == E - 1 else e % 2, b, :],
                                               OH[:, e * B + b].rearrange("p k j -> p (k j)"), start=b == 0, stop=b == B - 1)
                            mm.then_inc(list_in_psum, 1)

                    def last(t, k):
                        return t.rearrange("p (n a) -> p n a", a=1).to_broadcast([t.shape[0], t.shape[1], k])

                    def mid(t, k):
                        return t.rearrange("p (a n) -> p a n", a=1).to_broadcast([t.shape[0], k, t.shape[1]])

                    @block.gpsimd
                    def _(pool):
                        pool.wait_ge(places_made, 1)
                        pool.tensor_tensor(OH[:, :, 2, :], OH[:, :, 0, :], last(bidx[0:T], NBLK), ALU.mult).then_inc(blocks_made, 1)

                    @block.scalar
                    def _(act):
                        act.activation(IF[:], RC[:, 0:(E + 1) * NBLK + 1], ACT.Identity, bias=pad, scale=0.0).then_inc(table_made, 1)
                        act.wait_ge(places_made, 1)
                        act.activation(OH[:, :, 1, :], OH[:, :, 0, :], ACT.Copy, scale=pidx[0:T]).then_inc(blocks_made, 1)
                        for b in range(B):
                            ins = act.activation(AL[:, b, :], iota1[0:T], ACT.Abs, bias=LO[:, (E - 1) * B + b:(E - 1) * B + b + 1], scale=-1.0)
                        ins.then_inc(last_lanes, 1)
                        act.wait_ge(last_lanes, 1)
                        act.activation(OL[:, 2], AL[:], ACT.Relu, bias=1.0, scale=-1.0).then_inc(last_lanes, 1)
                        act.wait_ge(counts_made, 1)
                        ahead = [act.value_load(TB[0:1, E + e:E + e + 1], min_val=0, max_val=(E - 1) * NBLK) for e in range(E)]
                        act.wait_ge(idx_made, 1)
                        for e in range(E):
                            act.wait_ge(table_made, e + 1)
                            act.activation(IF[:, bass.ds(ahead[e], NBLK)], IDX[:, e, :], ACT.Copy).then_inc(table_made, 1)
                        act.wait_ge(table_made, 1 + E)

                    @block.vector
                    def _(dve):
                        n = [0]

                        def link(ins):
                            n[0] += 1
                            ins.then_inc(chain, 1)
                            dve.wait_ge(chain, n[0])

                        link(dve.tensor_copy(TRI[:], tri[0:T]))
                        link(dve.memset(ONES[:], 1.0))
                        dve.wait_ge(count_in_psum, 1)
                        link(dve.tensor_copy(CN[:], bank[1][0:T, 0:E * B]))
                        link(dve.tensor_tensor_scan(INC[:], reset[0:T], CN[:], 0.0, ALU.mult, ALU.add))
                        link(dve.tensor_tensor(P1[:], bank[0][0:T, 0:E * B], CN[:], ALU.subtract))
                        link(dve.tensor_tensor(P1[:], P1[:], INC[:], ALU.add))
                        link(dve.scalar_tensor_tensor(out=P1[:], in0=P1[:], scalar=1.0, in1=KEEPB[:].rearrange("p e b -> p (e b)"), op0=ALU.add, op1=ALU.mult))
                        link(dve.tensor_tensor(GE[:], last(P1[:], NBLK + 1), mid(thr[0:T], E * B), ALU.is_ge))
                        link(dve.tensor_reduce(HI[:], GE[:, :, 1:NBLK + 1], AX.X, ALU.add))
                        link(dve.scalar_tensor_tensor(out=LO[:], in0=HI[:], scalar=-128.0, in1=P1[:], op0=ALU.mult, op1=ALU.add))
                        dve.tensor_tensor(OH[:, :, 0, :], GE[:, :, 0:NBLK], GE[:, :, 1:NBLK + 1], ALU.subtract).then_inc(places_made, 1)
                        tokens, ahead, upto = TF[:, 0:E], TF[:, E:2 * E], TF[:, 2 * E:]
                        link(dve.tensor_copy(tokens, INC[0:1, B - 1::B]))
                        link(dve.tensor_tensor(NGE[:], last(tokens, NBLK), mid(thr[0:1, 0:NBLK], E), ALU.is_ge))
                        link(dve.tensor_reduce(ahead, NGE[:], AX.X, ALU.add))
                        link(dve.tensor_tensor_scan(upto, reset[0:1, 1:1 + E], ahead, 0.0, ALU.mult, ALU.add))
                        link(dve.tensor_tensor(ahead, upto, ahead, ALU.subtract))
                        dve.tensor_copy(TB[:], TF[:]).then_inc(counts_made, 1)
                        for e in range(E - 1):
                            if e >= 2:
                                dve.wait_ge(list_in_psum, e - 1)
                            dve.tensor_tensor(OL[:, e % 2], mid(iota1[0:T], B), last(LO[:, e * B:e * B + B], 128), ALU.is_equal).then_inc(lane_made, 1)
                        dve.wait_ge(list_in_psum, E)
                        sums = bank[2][:, 0:E * 3 * NBLK].rearrange("p (e k j) -> p e k j", k=3, j=NBLK)
                        dve.tensor_scalar(IDF[:], sums[:, :, 2, :], float(T), None, ALU.mult)
                        link(dve.tensor_scalar(PF[:], sums[:, :, 0, :], negpad, pad, ALU.mult, ALU.add))
                        link(dve.tensor_tensor(PF[:], PF[:], sums[:, :, 1, :], ALU.add))
                        dve.tensor_tensor(IDX[:], IDF[:], PF[:], ALU.add).then_inc(idx_made, 1)
                        dve.wait_ge(idx_made, 1)

            with ExitStack() as p3c:
                def psb(name, shape, dt=F32):
                    return p3c.enter_context(nc.sbuf_tensor(name, shape, dt))
                IG = psb("gather_tokens", [128, 1], I32)
                IS = psb("scatter_tokens", [128, 1], I32)
                GX = psb("gathered", [128, ROW])
                GXT = psb("gathered_T", [128, KT, 128])
                GN = psb("weights_next", [128, E])
                GC = psb("weights_now", [128, E])
                HB = psb("hidden", [128, HT, 128])
                YB = psb("expert_out", [128, C])
                YW = psb("weighted", [128, C])
                (idx_copied, gathered, weight_copied, weight_moved, xT_in_psum, xT_ready, hid_in_psum, hid_ready, y_in_psum, y_moved, y_scaled, scattered) = (
                    sem(f"moe_{n}") for n in ("idx_copied", "gathered", "weight_copied", "weight_moved", "xT_psum", "xT", "hid_psum", "hid", "y_psum", "y_moved", "y_scaled", "scattered"))

                def blocks(eng, body):
                    with eng.Fori(0, E // 2) as p:
                        for s in range(2):
                            e = p * 2 + s
                            tokens = eng.value_load(TB[0:1, bass.ds(e, 1)], min_val=0, max_val=B * T)
                            ahead = eng.value_load(TB[0:1, bass.ds(e + E, 1)], min_val=0, max_val=E * NBLK)
                            for first, end in STRETCHES:
                                with (eng.If(tokens > first * 128) if first else nullcontext()):
                                    with eng.Fori(first, end) as i:
                                        with eng.If(tokens > i * 128):
                                            body(ahead + i, e, s, p)

                with nc.Block() as block:
                    @block.sync
                    def _(sp):
                        with sp.Fori(1, E // 2) as p:
                            for s in range(2):
                                done = sp.value_load(TB[0:1, bass.ds(p * 2 + s + 2 * E - 2, 1)], min_val=0, max_val=E * NBLK)
                                after(sp, y_moved, done + 1)
                                sp.wait_ge(wld[s], p * EXPERT_LOADED)
                                load_expert(sp, p * 2 + s, s)
                        for s in range(2):
                            sp.wait_ge(wld[s], E // 2 * EXPERT_LOADED)
                        total = sp.value_load(TB[0:1, 3 * E - 1:3 * E], min_val=1, max_val=E * NBLK)
                        sp.wait_ge(scattered, total * 16 + 16)
                        for g in range(G):
                            sp.dma_start(H[:, g * GB:g * GB + GB, :], h_rows[g * GT:g * GT + GT, :].rearrange("(b t) c -> t b c", t=T)).then_inc(h_back[g], 16)

                    @block.gpsimd
                    def _(pool):
                        def gather(made):
                            after(pool, idx_copied, made)
                            pool.indirect_dma_start(GX[:], None, x_rows, bass.IndirectOffsetOnAxis(ap=IG[:], axis=0)).then_inc(gathered, 16)

                        def add_rows(n, made):
                            after(pool, idx_copied, made)
                            after(pool, y_scaled, n + 1)
                            pool.indirect_dma_start(h_rows, bass.IndirectOffsetOnAxis(ap=IS[:], axis=0), YW[:], None, compute_op=ALU.add).then_inc(scattered, 16)

                        pool.wait_ge(rows_stored, 4 * 16)
                        pool.tensor_copy(IG[:], IF[:, 0:1]).then_inc(idx_copied, 1)
                        gather(1)
                        pool.tensor_copy(IS[:], RC[:, RAT[3]:RAT[3] + 1]).then_inc(idx_copied, 1)
                        add_rows(0, 2)

                        def body(u, e, s, p):
                            pool.wait_ge(gathered, u * 16 + 16)
                            pool.wait_ge(xT_in_psum, u + 1)
                            after(pool, weight_copied, u + 1)
                            pool.tensor_copy(IG[:], IF[:, bass.ds(u + 1, 1)]).then_inc(idx_copied, 1)
                            gather(u * 2 + 3)
                            after(pool, scattered, u * 16 + 16)
                            pool.tensor_copy(IS[:], IF[:, bass.ds(u, 1)]).then_inc(idx_copied, 1)
                            add_rows(u + 1, u * 2 + 4)

                        blocks(pool, body)

                    @block.scalar
                    def _(act):
                        act.sem_inc(hid_ready, GB)

                        def move_xT(n):
                            act.wait_ge(xT_in_psum, n + 1)
                            act.activation(GXT[:].rearrange("p k t -> p (k t)"), bank[4][:, 0:KT * 128], ACT.Copy).then_inc(xT_ready, 1)

                        move_xT(0)

                        def body(u, e, s, p):
                            act.wait_ge(wld[s], (p + 1) * EXPERT_LOADED)
                            for i in range(HT):
                                act.wait_ge(hid_in_psum, u * HT + i + 1)
                                at = 128 * (i // 4)
                                act.activation(HB[:, i, :], bank[i % 4][:, at:at + 128], ACT.Gelu, bias=B1[:, s, i:i + 1]).then_inc(hid_ready, 1)
                            move_xT(u + 1)
                        blocks(act, body)

                    @block.vector
                    def _(dve):
                        dve.sem_inc(y_moved, 1)
                        dve.memset(YW[:], 0.0).then_inc(y_scaled, 1)

                        def take_weights(n):
                            dve.wait_ge(gathered, n * 16 + 16)
                            dve.tensor_copy(GN[:], GX[:, C:C + E]).then_inc(weight_copied, 1)

                        take_weights(0)
                        dve.wait_ge(weight_copied, 1)
                        dve.tensor_copy(GC[:], GN[:]).then_inc(weight_moved, 1)

                        def body(u, e, s, p):
                            dve.wait_ge(weight_moved, u + 1)
                            take_weights(u + 1)
                            dve.wait_ge(scattered, u * 16 + 16)
                            dve.wait_ge(wld[s], (p + 1) * EXPERT_LOADED)
                            dve.wait_ge(y_in_psum, u + 2)
                            wge = GC[:, bass.ds(e, 1)]
                            dve.tensor_tensor(YB[:], bank[5][:, 0:C], B2[:, s, :], ALU.add).then_inc(y_moved, 1)
                            dve.wait_ge(y_moved, u + 2)
                            dve.tensor_scalar(YW[:], YB[:], wge, None, ALU.mult).then_inc(y_scaled, 1)
                            dve.wait_ge(weight_copied, u + 2)
                            dve.wait_ge(y_scaled, u + 2)
                            dve.tensor_copy(GC[:], GN[:]).then_inc(weight_moved, 1)
                        blocks(dve, body)

                    @block.tensor
                    def _(pe):
                        pe.sem_inc(y_in_psum, 1)

                        def transpose_rows(n):
                            pe.wait_ge(gathered, n * 16 + 16)
                            for k in range(KT):
                                mm = pe.transpose(bank[4][:, k * 128:k * 128 + 128], GX[:, k * 128:k * 128 + 128], ID[:, :])
                            mm.then_inc(xT_in_psum, 1)

                        transpose_rows(0)

                        def body(u, e, s, p):
                            pe.wait_ge(wld[s], (p + 1) * EXPERT_LOADED)
                            pe.wait_ge(xT_ready, u + 1)
                            for i in range(HT):
                                pe.wait_ge(hid_ready, u * HT + i + 1)
                                at = 128 * (i // 4)
                                for k in range(KT):
                                    mm = pe.matmul(bank[i % 4][:, at:at + 128], W1[:, s, k, i * 128:i * 128 + 128], GXT[:, k, :], start=k == 0, stop=k == KT - 1)
                                mm.then_inc(hid_in_psum, 1)
                            pe.wait_ge(y_scaled, u + 1)
                            for i in range(HT):
                                if i == HT // 2:
                                    transpose_rows(u + 1)
                                pe.wait_ge(hid_ready, u * HT + i + 1 + GB)
                                mm = pe.matmul(bank[5][:, 0:C], HB[:, i, :], W2[:, s, i, :], start=i == 0, stop=i == HT - 1)
                            mm.then_inc(y_in_psum, 1)
                        blocks(pe, body)

        CC = sb("conv_col", [128, KT, 2])
        CM = sb("conv_mask", [128, KT, 64])
        CWT = sb("conv_w", [128, KT, 128])
        CB = sb("conv_b", [128, 1])
        GA = sb("gamma", [128, 1])
        BE = sb("beta", [128, 1])
        LW = sb("lin_w", [128, C])
        LB = sb("lin_b", [1, 2 * C])
        FW = sb("ffn_w", [128, KT, C])
        FB = sb("ffn_bias", [T, C])
        ffn_loaded, cw_made = sem("ffn_loaded"), sem("conv_w_made")
        n_ffn_loads = 9

        with ExitStack() as p4:
            def psb(name, shape, dt=F32):
                return p4.enter_context(nc.sbuf_tensor(name, shape, dt))
            HB_ = B // 2
            AW = psb("tssa_w", [128, KT, C])
            OW = psb("out_w", [128, KT, C])
            OB = psb("out_b", [T, C])
            TM = psb("temp", [T, NH])
            HO = psb("head_of", [128, KT, NH])
            HTO = psb("head_to", [NH, KT, 128])
            XN4 = psb("tssa_x", [T, 2, GB, C])
            XT4 = psb("tssa_x_T", [128, 2, KT, GT])
            WT = psb("w_T", [128, KT, B, T])
            WSQ = psb("w_sq_T", [128, KT, B, T])
            NS = psb("norm_sq", [128, KT, B])
            RI = psb("head_of_scaled", [128, KT, B, NH])
            SC = psb("tssa_score", [T, B, NH])
            SX = psb("tssa_max", [T, B])
            PI = psb("pi", [T, B, NH])
            PIT = psb("pi_T", [NH, B, T])
            PIE = psb("pi_by_channel", [128, KT, B, T])
            PIW = psb("pi_w", [128, KT, B, T])
            PWW = psb("pi_w_sq", [128, 2, KT, GB, T])
            DOT = psb("dots", [128, KT, B])
            SPI = psb("pi_sum", [128, KT, B])
            OT = psb("tssa_out_T", [128, KT, B, T])
            ld = sem("tssa_loaded")
            xn_ready, xnT_in_psum, xnT_ready = sem("t_xn"), sem("t_xnT_psum"), sem("t_xnT")
            w_in_psum, w_ready, chain, norms_made = sem("w_psum"), sem("w_ready"), sem("tssa_chain"), sem("norms_made")
            s_in_psum, s_shifted, pi_exp, pi_made = sem("ts_psum"), sem("ts_shifted"), sem("pi_exp"), sem("pi_made")
            piT_in_psum, piT_ready, pie_in_psum, pie_ready, piw_made = sem("piT_psum"), sem("piT"), sem("pie_psum"), sem("pie"), sem("piw")
            attn_made, pww_made, dots_summed = sem("attn_made"), sem("pww"), sem("dots_summed")
            oT_made, o_in_psum, h_added, bias_added, st_made = sem("oT"), sem("to_psum"), sem("t_h_added"), sem("t_bias"), sem("t_stats_made")
            aggregated, std_made, rstd_made = sem("ln3_aggr"), sem("ln3_std"), sem("ln3_rstd")

            def four(t, g):
                return t[:, :, g * GB:g * GB + GB, :]

            with nc.Block() as block:
                @block.sync
                def _(sp):
                    for dst, src in ((AW, tssa_w), (OW, out_w), (OB, out_b), (TM, temp), (HO, head_of), (HTO, head_to)):
                        sp.dma_start(dst[:], src).then_inc(ld, 16)
                    for dst, src in ((CC, conv_col), (CM, conv_mask), (CB, conv_b), (GA, gamma), (BE, beta), (LW, lin_w), (LB, lin_b), (FW, ffn_w), (FB, ffn_bias)):
                        sp.dma_start(dst[:], src).then_inc(ffn_loaded, 16)
                    sp.wait_ge(ffn_loaded, 16 * n_ffn_loads)

                @block.gpsimd
                def _(pool):
                    pool.wait_ge(ld, 96)
                    for g in range(G):
                        pool.wait_ge(xn_ready, g * GB + GB)
                        hs = H[:, g * GB:g * GB + GB, :]
                        pool.tensor_tensor(hs, hs, OB[:].rearrange("p (a c) -> p a c", a=1).to_broadcast([T, GB, C]), ALU.add).then_inc(bias_added, 1)
                    for g in range(G):
                        pool.wait_ge(pie_ready, g + 1)
                        pool.tensor_tensor(four(PIW, g), four(PIE, g), four(WT, g), ALU.mult).then_inc(piw_made, 1)
                        if g >= 2:
                            pool.wait_ge(dots_summed, g - 1)
                        pool.wait_ge(piw_made, g + 1)
                        pool.tensor_tensor(PWW[:, g % 2], four(PIW, g), four(WT, g), ALU.mult).then_inc(pww_made, 1)
                    pool.wait_ge(ffn_loaded, 16 * n_ffn_loads)
                    for k in range(KT):
                        for br_ in range(2):
                            pool.tensor_scalar(CWT[:, k, 64 * br_:64 * br_ + 64], CM[:, k, :], CC[:, k, br_:br_ + 1], None, ALU.mult).then_inc(cw_made, 1)
                    pool.wait_ge(cw_made, 2 * KT)

                @block.scalar
                def _(act):
                    def root(g):
                        act.wait_ge(aggregated, g + 1)
                        at = slice(g * GB, g * GB + GB)
                        act.activation(SD[:, at], MV[:, at, 1], ACT.Sqrt, bias=EP[0:T, :]).then_inc(std_made, 1)

                    def project(g):
                        for k in range(KT):
                            act.wait_ge(w_in_psum, g * KT + k + 1)
                            w = bank[2 * (g % 2) + k][:, 0:GT].rearrange("p (b t) -> p b t", t=T)
                            act.activation(four(WSQ, g)[:, k], w, ACT.Square)
                            ins = act.activation(four(WT, g)[:, k], w, ACT.Copy)
                        ins.then_inc(w_ready, 1)

                    def move_xT(g):
                        for k in range(KT):
                            act.wait_ge(xnT_in_psum, g * KT + k + 1)
                            act.activation(XT4[:, g % 2, k, :], bank[4 + k][:, 0:GT], ACT.Copy).then_inc(xnT_ready, 1)

                    def exp_half(h):
                        act.wait_ge(s_shifted, h + 1)
                        act.activation(PI[:, h * HB_:h * HB_ + HB_, :], SC[:, h * HB_:h * HB_ + HB_, :], ACT.Exp).then_inc(pi_exp, 1)

                    def move_piT(g):
                        act.wait_ge(piT_in_psum, g + 1)
                        act.activation(PIT[:, g * GB:g * GB + GB, :], bank[4 + g % 2][0:NH, 0:GT].rearrange("p (b t) -> p b t", t=T), ACT.Copy).then_inc(piT_ready, 1)

                    def spread(g):
                        act.wait_ge(pie_in_psum, g + 1)
                        for k in range(KT):
                            for j in range(GB):
                                b = g * GB + j
                                ins = act.activation(PIE[:, k, b, :], bank[2 * (g % 2) + k][:, j * T:j * T + T], ACT.Copy, accum_out=SPI[:, k, b:b + 1])
                        ins.then_inc(pie_ready, 1)

                    for g in range(G - 1):
                        root(g)
                    for g in range(G):
                        move_xT(g)
                        if g == 0:
                            root(G - 1)
                        if g == G - 1:
                            exp_half(0)
                        project(g)
                    move_piT(0)
                    move_piT(1)
                    exp_half(1)
                    spread(0)
                    spread(1)
                    move_piT(2)
                    move_piT(3)
                    spread(2)
                    spread(3)
                    for g in range(G):
                        act.wait_ge(attn_made, g + 1)
                        for b in range(g * GB, g * GB + GB):
                            for k in range(KT):
                                ins = act.activation(OT[:, k, b, :], PIW[:, k, b, :], ACT.Copy, scale=DOT[:, k, b:b + 1])
                            ins.then_inc(oT_made, 1)

                @block.vector
                def _(dve):
                    n = [0]

                    def link(ins):
                        n[0] += 1
                        ins.then_inc(chain, 1)
                        dve.wait_ge(chain, n[0])

                    def half(t, h):
                        return t[..., h * HB_:h * HB_ + HB_]

                    def h_stats(g):
                        dve.wait_ge(h_back[g], 16)
                        for b in range(g * GB, g * GB + GB):
                            ins = dve.bn_stats(ST[:, b, :], H[:, b, :])
                        link(ins)
                        for b in range(g * GB, g * GB + GB):
                            ins = dve.bn_aggr(MV[:, b, :], ST[:, b, :])
                        ins.then_inc(aggregated, 1)

                    def norm_x(g):
                        dve.wait_ge(std_made, g + 1)
                        dve.reciprocal(RS[:, g * GB:g * GB + GB], SD[:, g * GB:g * GB + GB]).then_inc(rstd_made, 1)
                        dve.wait_ge(rstd_made, g + 1)
                        if g >= 2:
                            dve.wait_ge(xnT_in_psum, (g - 1) * KT)
                        for j in range(GB):
                            b = g * GB + j
                            dve.tensor_scalar(XN4[:, g % 2, j, :], H[:, b, :], MV[:, b, 0:1], RS[:, b:b + 1],
                                              ALU.subtract, ALU.mult).then_inc(xn_ready, 1)

                    def sum_squares(g):
                        dve.wait_ge(w_ready, g + 1)
                        link(dve.tensor_reduce(NS[:, :, g * GB:g * GB + GB], four(WSQ, g), AX.X, ALU.add))

                    def scale_heads(h):
                        ns = half(NS[:], h)
                        link(dve.tensor_scalar(ns, ns, 1e-24, None, ALU.max))
                        link(dve.reciprocal(ns, ns))
                        for k in range(KT):
                            ins = dve.tensor_tensor(RI[:, k, h * HB_:h * HB_ + HB_, :], HO[:, k:k + 1, :].to_broadcast([128, HB_, NH]),
                                                    ns[:, k].rearrange("p (b a) -> p b a", a=1).to_broadcast([128, HB_, NH]), ALU.mult)
                        ins.then_inc(norms_made, 1)

                    def over_heads(h):
                        return SX[:, h * HB_:h * HB_ + HB_].rearrange("p (b a) -> p b a", a=1).to_broadcast([T, HB_, NH])

                    def shift_scores(h):
                        sc = SC[:, h * HB_:h * HB_ + HB_, :]
                        dve.wait_ge(s_in_psum, h + 1)
                        link(dve.tensor_tensor(sc, bank[6 + h][0:T, 0:HB_ * NH].rearrange("p (b h) -> p b h", b=HB_),
                                               TM[:].rearrange("p (a h) -> p a h", a=1).to_broadcast([T, HB_, NH]), ALU.mult))
                        link(dve.tensor_reduce(SX[:, h * HB_:h * HB_ + HB_], sc, AX.X, ALU.max))
                        dve.tensor_tensor(sc, sc, over_heads(h), ALU.subtract).then_inc(s_shifted, 1)

                    def finish_pi(h):
                        pi = PI[:, h * HB_:h * HB_ + HB_, :]
                        dve.wait_ge(pi_exp, h + 1)
                        link(dve.tensor_reduce(SX[:, h * HB_:h * HB_ + HB_], pi, AX.X, ALU.add))
                        link(dve.reciprocal(SX[:, h * HB_:h * HB_ + HB_], SX[:, h * HB_:h * HB_ + HB_]))
                        dve.tensor_tensor(pi, pi, over_heads(h), ALU.mult).then_inc(pi_made, 1)

                    def sum_dots(g):
                        dve.wait_ge(pww_made, g + 1)
                        dve.tensor_reduce(DOT[:, :, g * GB:g * GB + GB], PWW[:, g % 2], AX.X, ALU.add).then_inc(dots_summed, 1)
                        dve.wait_ge(dots_summed, g + 1)

                    def attend(g):
                        at = slice(g * GB, g * GB + GB)
                        sp_, dot = SPI[:, :, at], DOT[:, :, at]
                        link(dve.tensor_scalar(sp_, sp_, 1e-8, None, ALU.add))
                        link(dve.reciprocal(sp_, sp_))
                        link(dve.tensor_tensor(dot, dot, sp_, ALU.mult))
                        link(dve.tensor_scalar(dot, dot, -1.0, -1.0, ALU.mult, ALU.add))
                        dve.reciprocal(dot, dot).then_inc(attn_made, 1)

                    def add_to_h(g):
                        dve.wait_ge(bias_added, g + 1)
                        for b in range(g * GB, g * GB + GB):
                            dve.wait_ge(o_in_psum, b + 1)
                            dve.tensor_tensor(H[:, b, :], bank[4 + b % 4][0:T, 0:C], H[:, b, :], ALU.add).then_inc(h_added, 1)
                        for b in range(g * GB, g * GB + GB):
                            dve.wait_ge(h_added, b + 1)
                            dve.bn_stats(ST[:, b, :], H[:, b, :]).then_inc(st_made, 1)

                    h_stats(0)
                    h_stats(1)
                    norm_x(0)
                    h_stats(2)
                    norm_x(1)
                    h_stats(3)
                    norm_x(2)
                    dve.wait_ge(ld, 96)
                    sum_squares(0)
                    norm_x(3)
                    sum_squares(1)
                    scale_heads(0)
                    shift_scores(0)
                    sum_squares(2)
                    finish_pi(0)
                    sum_squares(3)
                    scale_heads(1)
                    shift_scores(1)
                    finish_pi(1)
                    for g in range(G):
                        sum_dots(g)
                        attend(g)
                        if g:
                            add_to_h(g - 1)
                    add_to_h(G - 1)
                    dve.wait_ge(st_made, B)

                @block.tensor
                def _(pe):
                    pe.wait_ge(ld, 96)

                    def project(g):
                        if g:
                            pe.wait_ge(xnT_ready, g * KT)
                        pe.wait_ge(xn_ready, g * GB + GB)
                        for k in range(KT):
                            for b in range(GB):
                                mm = pe.transpose(bank[4 + k][:, b * T:b * T + T], XN4[:, g % 2, b, k * 128:k * 128 + 128], ID[0:T, 0:T])
                            mm.then_inc(xnT_in_psum, 1)
                        pe.wait_ge(xnT_ready, g * KT + KT)
                        if g >= 2:
                            pe.wait_ge(w_ready, g - 1)
                        for o in range(KT):
                            for k in range(KT):
                                mm = pe.matmul(bank[2 * (g % 2) + o][:, 0:GT], AW[:, k, o * 128:o * 128 + 128], XT4[:, g % 2, k, :], start=k == 0, stop=k == KT - 1)
                            mm.then_inc(w_in_psum, 1)

                    def scores(h):
                        pe.wait_ge(norms_made, h + 1)
                        for b in range(h * HB_, h * HB_ + HB_):
                            j = b - h * HB_
                            for k in range(KT):
                                mm = pe.matmul(bank[6 + h][0:T, j * NH:j * NH + NH], WSQ[:, k, b, :], RI[:, k, b, :], start=k == 0, stop=k == KT - 1)
                        mm.then_inc(s_in_psum, 1)

                    def transpose_pi(h):
                        pe.wait_ge(pi_made, h + 1)
                        for g in (2 * h, 2 * h + 1):
                            if h:
                                pe.wait_ge(piT_ready, g - 1)
                            for b in range(GB):
                                mm = pe.transpose(bank[4 + g % 2][0:NH, b * T:b * T + T], PI[:, g * GB + b, :], ID[0:T, 0:T])
                            mm.then_inc(piT_in_psum, 1)

                    def spread(g):
                        pe.wait_ge(piT_ready, g + 1)
                        if g >= 2:
                            pe.wait_ge(pie_ready, g - 1)
                        for k in range(KT):
                            mm = pe.matmul(bank[2 * (g % 2) + k][:, 0:GT], HTO[:, k, :], PIT[:, g * GB:g * GB + GB, :].rearrange("p b t -> p (b t)"), start=True, stop=True)
                        mm.then_inc(pie_in_psum, 1)

                    project(0)
                    project(1)
                    project(2)
                    scores(0)
                    project(3)
                    transpose_pi(0)
                    pe.wait_ge(w_ready, G)
                    spread(0)
                    spread(1)
                    scores(1)
                    transpose_pi(1)
                    spread(2)
                    spread(3)
                    for b in range(B):
                        pe.wait_ge(oT_made, b + 1)
                        if b >= 4:
                            pe.wait_ge(h_added, b - 3)
                        else:
                            pe.wait_ge(piT_ready, G)
                            pe.wait_ge(s_shifted, 2)
                        for k in range(KT):
                            mm = pe.matmul(bank[4 + b % 4][0:T, 0:C], OT[:, k, b, :], OW[:, k, :], start=k == 0, stop=k == KT - 1)
                        mm.then_inc(o_in_psum, 1)

        with ExitStack() as p5:
            def psb(name, shape, dt=F32):
                return p5.enter_context(nc.sbuf_tensor(name, shape, dt))
            XC = psb("gate_pre", [128, B * T])
            XA = psb("gate_act", [128, B * T])
            FU = psb("full", [T, B, C])
            X4 = psb("x_kept", [T, B, C])
            XT5 = psb("ffn_x_T", [128, KT, B, T])
            CST = psb("bn_stats", [128, G, 6])
            CMV = psb("bn_mean_var", [128, 2])
            CS = psb("bn_scale_bias", [128, 4])
            xn_ready, xnT_in_psum, xnT_ready = sem("f_xn"), sem("f_xnT_psum"), sem("f_xnT")
            xc_in_psum, xc_ready, full_in_psum, full_by_vector, full_by_scalar = (sem(n) for n in ("xc_psum", "xc", "full_psum", "full_by_vector", "full_by_scalar"))
            cst_made, bn_made, bn_sd, xa_ready, bias_added = sem("cst_made"), sem("bn_made"), sem("bn_sd"), sem("xa_ready"), sem("ffn_bias_added")
            on_vector, on_scalar = finish_norm("ln4")

            FV = 4

            XAB = psb("gate_act_step", [128, 2, T])
            M8 = psb("top8", [T, 2, 2, 8])
            NM = psb("neg_max", [T, 2, 2])
            EE = psb("score_exp", [T, 2, 2, C])
            E8 = psb("top8_exp", [T, 2, 2, 8])
            REM = psb("score_rest", [T, 2, 2, C])
            TOP = psb("score_top", [T, 2, 2, C])
            SS = psb("score_sum", [T, 2, 2])
            RSS = psb("score_sum_recip", [T, 2, 2])
            XS = psb("x_sparse", [T, 2, C])
            OS = psb("out_sparse", [T, 2, C])
            XST = psb("x_sparse_T", [128, 2, KT, T])
            OO = psb("out_tile", [T, 2, C])
            xab, l_in_psum, m8, ee, top, picked, scaled, xs_ready, os_weighed, os_ready, xsT_in_psum, xsT, in_psum, oo = (
                sem(n) for n in ("xab", "ffn_l_psum", "m8", "ee", "topk", "picked", "scaled", "xs", "os_weighed", "os", "xsT_psum", "xsT", "in_psum", "oo"))
            stored = [sem(f"stored{s}") for s in range(2)]
            NT = 4 * (TOPK // 8) - 1

            def made(b):
                return b + 3

            def freed(b):
                return b + 1

            def pipeline(eng, tasks, between={}):
                first = -min(offset for offset, _ in tasks)
                pairs = (B - max(offset for offset, _ in tasks) - first) // 2

                def step(k, parity):
                    for offset, task in tasks:
                        if not isinstance(k, int) or 0 <= k + offset < B:
                            task(k + offset, (parity + offset) % 2)

                for k in range(-2, first):
                    step(k, k % 2)
                    if k in between:
                        between[k]()
                with eng.Fori(0, pairs) as i:
                    for s in range(2):
                        step(i * 2 + s + first, (s + first) % 2)
                for k in range(first + 2 * pairs, B + 2):
                    step(k, k % 2)

            with nc.Block() as block:
                @block.sync
                def _(sp):
                    for s in range(2):
                        sp.sem_inc(stored[s], 16)
                    with sp.Fori(0, B // 2) as i:
                        for s in range(2):
                            sp.wait_ge(oo, made(i * 2 + s))
                            sp.dma_start(out[bass.ds(i * 2 + s, 1)].rearrange("b t c -> t (b c)"), OO[:, s, :]).then_inc(stored[s], 16)
                    for s in range(2):
                        sp.wait_ge(stored[s], 16 * (B // 2) + 16)

                @block.gpsimd
                def _(pool):
                    for g in range(G):
                        pool.wait_ge(xn_ready, g * GB + GB)
                        hs = H[:, g * GB:g * GB + GB, :]
                        pool.tensor_tensor(hs, hs, FB[:].rearrange("p (a c) -> p a c", a=1).to_broadcast([T, GB, C]), ALU.add).then_inc(bias_added, 1)
                    pool.wait_ge(bias_added, G)
                    after(pool, xa_ready, 1)

                    def copy_gate(b, s):
                        if not (isinstance(b, int) and b < 2):
                            after(pool, l_in_psum, b - 1)
                        pool.tensor_copy(XAB[:, s, :], XA[:, bass.ds(b * T, T)]).then_inc(xab, 1)

                    def pick(b, s):
                        after(pool, top, b * NT + NT)
                        after(pool, os_ready, freed(b))
                        pool.tensor_tensor(TOP[:, s], EE[:, s], REM[:, s], ALU.subtract).then_inc(picked, 1)

                    def weigh(b, s):
                        after(pool, xsT_in_psum, freed(b))
                        after(pool, scaled, b + 1)
                        if isinstance(b, int) and b == 0:
                            after(pool, full_by_vector, FV)
                            after(pool, full_by_scalar, B - FV)
                        pool.tensor_tensor(XS[:, s, :], TOP[:, s, 1, :], row(X4, b), ALU.mult).then_inc(xs_ready, 1)
                        after(pool, in_psum, freed(b))
                        pool.tensor_tensor(OS[:, s, :], TOP[:, s, 0, :], row(FU, b), ALU.mult).then_inc(os_weighed, 1)
                        after(pool, os_weighed, b + 1)
                        pool.tensor_tensor(OS[:, s, :], OS[:, s, :], row(H, b), ALU.add).then_inc(os_ready, 1)

                    pipeline(pool, ((2, copy_gate), (-1, pick), (-1, weigh)))

                @block.scalar
                def _(act):
                    on_scalar(act)

                    def move_gate(g):
                        act.wait_ge(xc_in_psum, g + 1)
                        act.activation(XC[:, g * GT:g * GT + GT], bank[g % 2][:, 0:GT], ACT.Identity, bias=CB[:]).then_inc(xc_ready, 1)

                    for g in range(G):
                        for k in range(KT):
                            act.wait_ge(xnT_in_psum, g * KT + k + 1)
                            act.activation(XT5[:, k, g * GB:g * GB + GB, :], bank[4 + 2 * (g % 2) + k][:, 0:GT].rearrange("p (b t) -> p b t", t=T), ACT.Copy).then_inc(xnT_ready, 1)
                        if g:
                            move_gate(g - 1)
                    move_gate(G - 1)
                    act.wait_ge(bn_made, 1)
                    act.activation(CS[:, 0:1], CMV[:, 1:2], ACT.Sqrt, bias=EP[:]).then_inc(bn_sd, 1)
                    act.wait_ge(bn_made, 5)
                    act.activation(XA[:], XC[:], ACT.Gelu, bias=CS[:, 3:4], scale=CS[:, 2:3]).then_inc(xa_ready, 1)

                    def scale(b, s):
                        act.wait_ge(picked, b + 1)
                        for r in range(2):
                            ins = act.activation(TOP[:, s, r, :], TOP[:, s, r, :], ACT.Copy, scale=RSS[:, s, r:r + 1])
                        ins.then_inc(scaled, 1)

                    def exp_scores(b, s):
                        if not (isinstance(b, int) and b < 2):
                            act.wait_ge(picked, b - 1)
                        act.wait_ge(m8, b * 2 + 2)
                        for r in range(2):
                            act.activation(EE[:, s, r, :], bank[2 * s + r][0:T, 0:C], ACT.Exp, bias=NM[:, s, r:r + 1],
                                           accum_out=SS[:, s, r:r + 1])
                            ins = act.activation(E8[:, s, r, :], M8[:, s, r, :], ACT.Exp, bias=NM[:, s, r:r + 1])
                        ins.then_inc(ee, 1)

                    def move(b, s):
                        act.wait_ge(in_psum, freed(b))
                        act.wait_ge(xsT_in_psum, made(b))
                        act.activation(XST[:, s], bank[4 + s][:, 0:KT * T].rearrange("p (k t) -> p k t", k=KT), ACT.Copy).then_inc(xsT, 1)

                    def store(b, s):
                        act.wait_ge(stored[s], (b - s) * 8 + 16)
                        act.wait_ge(in_psum, made(b))
                        act.activation(OO[:, s, :], bank[6 + s][0:T, 0:C], ACT.Copy).then_inc(oo, 1)

                    def move_full():
                        for b in range(FV, B):
                            act.wait_ge(full_in_psum, b + 1)
                            act.activation(FU[:, b, :], bank[4 + b % 4][0:T, 0:C], ACT.Copy).then_inc(full_by_scalar, 1)

                    pipeline(act, ((-1, scale), (1, exp_scores), (-2, store), (-1, move)), {0: move_full})

                @block.vector
                def _(dve):
                    for two in (xsT_in_psum, xsT, in_psum, os_ready, oo):
                        dve.sem_inc(two, 2)
                    on_vector(dve)
                    for b in range(B):
                        dve.tensor_scalar(X4[:, b, :], H[:, b, :], MV[:, b, 0:1], RS[:, b:b + 1], ALU.subtract, ALU.mult).then_inc(xn_ready, 1)
                    for g in range(G):
                        dve.wait_ge(xc_ready, g + 1)
                        dve.bn_stats(CST[:, g, :], XC[:, g * GT:g * GT + GT]).then_inc(cst_made, 1)
                    dve.wait_ge(cst_made, G)
                    dve.bn_aggr(CMV[:], CST[:]).then_inc(bn_made, 1)
                    dve.wait_ge(bn_sd, 1)
                    dve.reciprocal(CS[:, 1:2], CS[:, 0:1]).then_inc(bn_made, 1)
                    dve.wait_ge(bn_made, 2)
                    dve.tensor_tensor(CS[:, 2:3], CS[:, 1:2], GA[:], ALU.mult).then_inc(bn_made, 1)
                    dve.wait_ge(bn_made, 3)
                    dve.tensor_tensor(CS[:, 3:4], CS[:, 2:3], CMV[:, 0:1], ALU.mult).then_inc(bn_made, 1)
                    dve.wait_ge(bn_made, 4)
                    dve.tensor_tensor(CS[:, 3:4], BE[:], CS[:, 3:4], ALU.subtract).then_inc(bn_made, 1)
                    for b in range(FV):
                        dve.wait_ge(full_in_psum, b + 1)
                        dve.tensor_copy(FU[:, b, :], bank[4 + b % 4][0:T, 0:C]).then_inc(full_by_vector, 1)

                    def row_max(b, s):
                        after(dve, l_in_psum, b + 1)
                        for r in range(2):
                            ins = dve.max(M8[:, s, r, :], bank[2 * s + r][0:T, 0:C])
                        ins.then_inc(m8, 1)
                        dve.wait_ge(m8, b * 2 + 1)
                        dve.tensor_scalar(NM[:, s, :], M8[:, s, :, 0], -1.0, None, ALU.mult).then_inc(m8, 1)

                    def search(b, s):
                        after(dve, ee, b + 1)
                        dve.reciprocal(RSS[:, s, :], SS[:, s, :]).then_inc(top, 1)
                        n = 1
                        for rnd in range(TOPK // 8):
                            if rnd:
                                for r in range(2):
                                    after(dve, top, b * NT + n - 1)
                                    dve.max(E8[:, s, r, :], REM[:, s, r, :]).then_inc(top, 1)
                                    n += 1
                            for r in range(2):
                                if rnd:
                                    after(dve, top, b * NT + n - 1)
                                src = EE if rnd == 0 else REM
                                dve.match_replace(REM[:, s, r, :], E8[:, s, r, :], src[:, s, r, :], 0.0).then_inc(top, 1)
                                n += 1
                        assert n == NT, n

                    pipeline(dve, ((1, row_max), (0, search)))

                @block.tensor
                def _(pe):
                    def transpose_x(g):
                        pe.wait_ge(xn_ready, g * GB + GB)
                        if g >= 2:
                            pe.wait_ge(xnT_ready, (g - 1) * KT)
                        for k in range(KT):
                            for j in range(GB):
                                mm = pe.transpose(bank[4 + 2 * (g % 2) + k][:, j * T:j * T + T], X4[:, g * GB + j, k * 128:k * 128 + 128], ID[0:T, 0:T])
                            mm.then_inc(xnT_in_psum, 1)

                    def gate(g):
                        pe.wait_ge(xnT_ready, g * KT + KT)
                        if g >= 2:
                            pe.wait_ge(xc_ready, g - 1)
                        for k in range(KT):
                            mm = pe.matmul(bank[g % 2][:, 0:GT], CWT[:, k, :], XT5[:, k, g * GB:g * GB + GB, :].rearrange("p b t -> p (b t)"), start=k == 0, stop=k == KT - 1)
                        mm.then_inc(xc_in_psum, 1)

                    transpose_x(0)
                    for g in range(G):
                        if g + 1 < G:
                            transpose_x(g + 1)
                        gate(g)

                    def full(first, last):
                        for b in range(first, last):
                            if b >= 4 + FV:
                                pe.wait_ge(full_by_scalar, b - 3 - FV)
                            elif b >= 4:
                                pe.wait_ge(full_by_vector, b - 3)
                            for k in range(KT):
                                mm = pe.matmul(bank[4 + b % 4][0:T, 0:C], XT5[:, k, b, :], FW[:, k, :], start=k == 0, stop=k == KT - 1)
                            mm.then_inc(full_in_psum, 1)

                    full(0, FV)
                    pe.wait_ge(xc_ready, G)

                    def logits(b, s):
                        if not (isinstance(b, int) and b < 2):
                            pe.wait_ge(ee, b - 1)
                        pe.wait_ge(xab, b + 1)
                        for r in range(2):
                            pe.matmul(bank[2 * s + r][0:T, 0:C], ONE[:, 0:T], LB[:, r * C:r * C + C], start=True, stop=False)
                        for r in range(2):
                            mm = pe.matmul(bank[2 * s + r][0:T, 0:C], XAB[64 * r:64 * r + 64, s, :], LW[64 * r:64 * r + 64, :], start=False, stop=True)
                        mm.then_inc(l_in_psum, 1)

                    def in_branch(b, s):
                        pe.wait_ge(xsT, freed(b))
                        pe.wait_ge(xs_ready, b + 1)
                        for k in range(KT):
                            mm = pe.transpose(bank[4 + s][:, k * T:k * T + T], XS[:, s, k * 128:k * 128 + 128], ID[0:T, 0:T])
                        mm.then_inc(xsT_in_psum, 1)
                        pe.wait_ge(oo, freed(b))
                        pe.wait_ge(os_ready, made(b))
                        pe.matmul(bank[6 + s][0:T, 0:C], ID[0:T, 0:T], OS[:, s, :], start=True, stop=False)
                        pe.wait_ge(xsT, made(b))
                        for k in range(KT):
                            mm = pe.matmul(bank[6 + s][0:T, 0:C], XST[:, s, k, :], FW[:, k, :], start=False, stop=k == KT - 1)
                        mm.then_inc(in_psum, 1)

                    def rest_of_full():
                        full((B + FV) // 2, B)
                        pe.wait_ge(full_by_scalar, B - FV)

                    pipeline(pe, ((2, logits), (-1, in_branch)), {-1: lambda: full(FV, (B + FV) // 2), 0: rest_of_full})


def _layout(i):
    import numpy as np
    f = np.float32
    a = {k: np.asarray(v) for k, v in i.items()}
    o = {}
    p = a["x"].reshape(B, 3, 6, 16, 6, 16).transpose(1, 3, 5, 0, 2, 4).reshape(768, B, NP)
    pt = np.zeros((768, B // 2, 2, 64), f)
    pt[:, :, :, 1:1 + NP] = p.reshape(768, B // 2, 2, NP)
    o["patches"] = pt.reshape(PK, 128, G, GB // 2, 128).transpose(2, 1, 3, 0, 4)
    hb = np.zeros((B, T, C), f)
    hb[:, 0] = a["L0_tok_cls_token"][0]
    hb[:, 1:1 + NP] = a["L0_tok_b"]
    hb[:, 1 + NP:] = a["txt"]
    o["h_base"] = hb.transpose(1, 0, 2)
    kt = lambda w: w.reshape(-1, 128, w.shape[-1]).transpose(1, 0, 2)
    o["tok_w"] = kt(a["L0_tok_W"])
    w = a["L0_attn_Wqkv"].reshape(C, 3, NH, HD)
    bb = a["L0_attn_bqkv"].reshape(3, NH, HD)
    z = np.zeros_like(w[:, 0])
    o["wkv"] = kt(np.concatenate([w[:, 1], w[:, 2]], -1).reshape(C, -1))
    o["wq"] = kt(np.concatenate([w[:, 0], z], -1).reshape(C, -1))
    o["bkv"] = np.tile(np.concatenate([bb[1], bb[2]], -1).T, (GB, 1))
    o["bq"] = np.tile(np.concatenate([bb[0], np.zeros_like(bb[0])], -1).T, (GB, 1))
    o["wproj"] = kt(a["L0_attn_Wproj"])
    rep = lambda v: np.tile(v.reshape(1, -1), (T, 1))
    o["br"] = rep(a["L0_ffn_br"])
    o["bproj"] = rep(a["L0_attn_bproj"])
    m = np.where(np.arange(T)[None, :] <= np.arange(T)[:, None], 0.0, NEG)
    o["mask4"] = np.tile(m, (1, HQ)).astype(f)
    o["ident"] = np.eye(128, dtype=f)
    o["w1"] = a["L0_ffn_W1"].reshape(E, KT, 128, HID).transpose(0, 2, 1, 3)
    o["b1"] = a["L0_ffn_b1"].reshape(E, HT, 128).transpose(0, 2, 1)
    o["w2"] = a["L0_ffn_W2"].reshape(E, HT, 128, C).transpose(0, 2, 1, 3)
    o["b2"] = a["L0_ffn_b2"]
    o["wr"] = kt(a["L0_ffn_Wr"])
    lane = np.arange(128.0)
    parts = [np.tile(lane + 1, (128, 1)), np.tile(128.0 * np.arange(NBLK + 1) + 1, (128, 1)), lane[:, None],
             B * T + lane[:, None], -B * T - lane[:, None], np.tile(np.arange(float(B)), (128, E)),
             np.tile(np.arange(B) > 0, (128, E)), lane[:, None] < np.arange(T)]
    o["route_consts"] = np.concatenate([v.astype(f) for v in parts], 1)
    o["tssa_w"] = kt(a["L1_attn_qkv_w"].T)
    o["temp"] = rep(a["L1_attn_temp"])
    ho = np.repeat(np.eye(NH, dtype=f), HD, axis=0)
    o["head_of"] = kt(ho)
    o["head_to"] = ho.T.reshape(NH, KT, 128)
    o["out_w"] = kt(a["L1_attn_out_w"].T)
    o["out_b"] = rep(a["L1_attn_out_b"])
    cc = np.stack([a["L1_ffn_so_conv_w"].reshape(-1), a["L1_ffn_si_conv_w"].reshape(-1)], -1)
    o["conv_col"] = kt(cc)
    o["conv_mask"] = kt(np.repeat(np.eye(64, dtype=f), 4, axis=0))
    both = lambda n: np.concatenate([a[f"L1_ffn_so_{n}"], a[f"L1_ffn_si_{n}"]]).reshape(-1, 1)
    o["conv_b"], o["gamma"], o["beta"] = both("conv_b"), both("gamma"), both("beta")
    o["lin_w"] = np.concatenate([a["L1_ffn_so_lin_w"].T, a["L1_ffn_si_lin_w"].T])
    o["lin_b"] = both("lin_b").reshape(1, -1)
    o["ffn_w"] = kt(a["L1_ffn_weight"])
    o["ffn_bias"] = rep(a["L1_ffn_bias"])
    return {k: np.ascontiguousarray(v) for k, v in o.items()}


def kernel(**inputs):
    import concourse.bacc as _bacc
    from concourse import mybir as _mybir
    from concourse.bass_utils import run_bass_kernel_spmd as _run

    nc = _bacc.Bacc("TRN2", target_bir_lowering=False, num_devices=1)
    arrays = _layout(inputs)
    args = {k: nc.dram_tensor(f"in_{k}", v.shape, _mybir.dt.from_np(v.dtype), kind="ExternalInput").ap() for k, v in arrays.items()}
    args["out"] = nc.dram_tensor("out", (B, T, C), F32, kind="ExternalOutput").ap()
    early_fusion(nc, **args)
    arrays = {f"in_{k}": v for k, v in arrays.items()}
    return _run(nc, [arrays], core_ids=[0]).results[0]["out"]
```
